# Optimizing a Trainium2 kernel written in Bass

```python
import numpy as np
import jax
import jax.numpy as jnp

def _softmax(x, axis=-1):
    return jax.nn.softmax(x, axis=axis)

def _gelu(x):
    return jax.nn.gelu(x, approximate=True)

def _silu(x):
    return jax.nn.silu(x)

def _sigmoid(x):
    return jax.nn.sigmoid(x)

def _layernorm(x, axis=-1, eps=1e-05):
    m = jnp.mean(x, axis=axis, keepdims=True)
    v = jnp.var(x, axis=axis, keepdims=True)
    return (x - m) / jnp.sqrt(v + eps)

def _scatter_add(tgt, idx, src, axis=0):
    return tgt.at[idx].add(src)

def _segment_sum(src, seg, n):
    return jax.ops.segment_sum(src, seg, n)
kernel_name = 'mk_gnn_resnorm_d4_gnn_r32_5a6ff2'

def setup_inputs(seed: int=0):
    np.random.seed(seed)
    _w = jnp.asarray

    def _rec_inputs():
        import jax
        import jax.numpy as jnp
        _gk = jax.random.key(seed)
        x = -0.0007083 + 1.001 * jax.random.normal(jax.random.fold_in(_gk, 1), (50000, 48), jnp.float32)
        src = jax.random.randint(jax.random.fold_in(_gk, 2), (50000,), 0, 50000, jnp.int32)
        dst = jnp.minimum((50000 * jax.random.uniform(jax.random.fold_in(_gk, 3), (50000,)) ** 2.0).astype(jnp.int32), 49999)
        _o = jnp.argsort(dst, stable=True)
        src = src[_o]
        dst = dst[_o]
        edge_attr_40 = jax.random.uniform(jax.random.fold_in(_gk, 13), (50000, 40), jnp.float32, 0.0, 1)
        edge_type_8 = jax.random.randint(jax.random.fold_in(_gk, 15), (50000,), 0, 8, jnp.int32)
        edge_weight = jax.random.uniform(jax.random.fold_in(_gk, 16), (50000,), jnp.float32, 0.0, 6.99999)
        edge_weight1 = jax.random.uniform(jax.random.fold_in(_gk, 17), (50000, 1), jnp.float32, 0.0, 1)
        node_type_119 = jax.random.randint(jax.random.fold_in(_gk, 18), (50000,), 0, 119, jnp.int32)
        node_vec = jax.random.uniform(jax.random.fold_in(_gk, 19), (50000,), jnp.float32, 0.0, 1.49999)
        return (x, src, dst, edge_attr_40, edge_type_8, edge_weight, edge_weight1, node_type_119, node_vec)
    x, src, dst, edge_attr_40, edge_type_8, edge_weight, edge_weight1, node_type_119, node_vec = _rec_inputs()

    def _L0_gnn_setup():
        import jax, jax.numpy as jnp
        import numpy as np
        N_NODES = 50000
        N_EDGES = 50000
        D_IN = 48
        D_OUT = 48
        key = jax.random.key(seed)
        k1, k2, k3, k4 = jax.random.split(key, 4)
        features = jax.random.normal(k1, (N_NODES, D_IN), dtype=jnp.float32)
        src = jax.random.randint(k2, (N_EDGES,), 0, N_NODES, dtype=jnp.int64)
        dst = jax.random.randint(k3, (N_EDGES,), 0, N_NODES, dtype=jnp.int64)
        std = np.sqrt(2.0 / (D_IN + D_OUT))
        W = jax.random.normal(k4, (D_OUT, D_IN), dtype=jnp.float32) * std
        b = jnp.zeros((D_OUT,), dtype=jnp.float32)
        return {'features': features, 'src': src, 'dst': dst, 'W': W, 'b': b}
    _L0_gnn_all = _L0_gnn_setup()
    _L0_gnn_in = {k: v for k, v in _L0_gnn_all.items() if k in ('W', 'b')}
    del _L0_gnn_all

    def _L1_gnn_setup():
        import jax, jax.numpy as jnp
        import numpy as np
        CUTOFF = 6.0
        LN_EPS = 1e-05
        key = jax.random.key(seed)
        ks = jax.random.split(key, 16)
        N, E, H, R, NEL, G = (50000, 25000, 48, 40, 119, 32)
        inp = {'h': jax.random.normal(ks[0], (N, H), jnp.float32), 'edge_index': jax.random.randint(ks[1], (2, E), 0, N, jnp.int64), 'edge_attr': jax.random.uniform(ks[2], (E, R), jnp.float32), 'distances': jax.random.uniform(ks[3], (E,), jnp.float32) * 7.0, 'atom_z': jax.random.randint(ks[4], (N,), 0, NEL, jnp.int64), 'node_mult': jax.random.uniform(ks[5], (N,), jnp.float32) + 0.5, 'batch': jnp.zeros((N,), jnp.int64), 'W1': jax.random.normal(ks[6], (H, R), jnp.float32) / np.sqrt(R), 'b1': jax.random.normal(ks[7], (H,), jnp.float32) * 0.01, 'W2': jax.random.normal(ks[8], (H, H), jnp.float32) / np.sqrt(H), 'b2': jax.random.normal(ks[9], (H,), jnp.float32) * 0.01, 'emb': jax.random.normal(ks[10], (NEL, G), jnp.float32) * 0.01, 'adaptW': jax.random.normal(ks[11], (G, G), jnp.float32) * 0.01, 'gamma': jnp.ones((H,), jnp.float32), 'beta': jnp.zeros((H,), jnp.float32)}
        return inp
    _L1_gnn_all = _L1_gnn_setup()
    _L1_gnn_in = {k: v for k, v in _L1_gnn_all.items() if k in ('W1', 'b1', 'W2', 'b2', 'emb', 'adaptW', 'gamma', 'beta')}
    del _L1_gnn_all

    def _L2_gnn_setup():
        import jax, jax.numpy as jnp
        import numpy as np
        N_NODES = 50000
        N_EDGES = 50000
        IN_FEAT = 48
        OUT_FEAT = 48
        NUM_RELS = 8
        key = jax.random.key(seed)
        ks = jax.random.split(key, 9)
        s1 = float(np.sqrt(2.0) * np.sqrt(6.0 / (IN_FEAT + IN_FEAT)))
        s2 = float(np.sqrt(2.0) * np.sqrt(6.0 / (IN_FEAT + OUT_FEAT)))
        return {'inputs': jax.random.normal(ks[0], (N_NODES, IN_FEAT), dtype=jnp.float32), 'norm': jax.random.uniform(ks[1], (N_EDGES, 1), dtype=jnp.float32), 'weight1': jax.random.uniform(ks[2], (NUM_RELS, IN_FEAT, IN_FEAT), jnp.float32, -s1, s1), 'weight2': jax.random.uniform(ks[3], (NUM_RELS, IN_FEAT, OUT_FEAT), jnp.float32, -s2, s2), 'bias1': jax.random.normal(ks[4], (IN_FEAT,), dtype=jnp.float32) * 0.1, 'bias2': jax.random.normal(ks[5], (OUT_FEAT,), dtype=jnp.float32) * 0.1, 'src': jax.random.randint(ks[6], (N_EDGES,), 0, N_NODES, dtype=jnp.int64) if jax.config.jax_enable_x64 else jax.random.randint(ks[6], (N_EDGES,), 0, N_NODES).astype(jnp.int32), 'dst': jax.random.randint(ks[7], (N_EDGES,), 0, N_NODES).astype(jnp.int32), 'rel_type': jax.random.randint(ks[8], (N_EDGES,), 0, NUM_RELS).astype(jnp.int32)}
    _L2_gnn_all = _L2_gnn_setup()
    _L2_gnn_in = {k: v for k, v in _L2_gnn_all.items() if k in ('weight1', 'weight2', 'bias1', 'bias2')}
    del _L2_gnn_all

    def _L3_gnn_setup():
        import jax, jax.numpy as jnp
        import numpy as np
        N_NODES = 3125
        N_EDGES = 50000
        IN_CH = 48
        OUT_CH = 48
        BN_EPS = 1e-05
        key = jax.random.key(seed)
        k1, k2, k3, k4 = jax.random.split(key, 4)
        x = jax.random.normal(k1, (N_NODES, IN_CH), dtype=jnp.float32)
        edge_index = jax.random.randint(k2, (2, N_EDGES), 0, N_NODES, dtype=jnp.int32)
        W = jax.random.normal(k3, (IN_CH, OUT_CH), dtype=jnp.float32) * (1.0 / np.sqrt(IN_CH))
        b = jnp.zeros((OUT_CH,), dtype=jnp.float32)
        gamma = jnp.ones((OUT_CH,), dtype=jnp.float32)
        beta = jnp.zeros((OUT_CH,), dtype=jnp.float32)
        return {'x': x, 'edge_index': edge_index, 'W': W, 'b': b, 'gamma': gamma, 'beta': beta}
    _L3_gnn_all = _L3_gnn_setup()
    _L3_gnn_in = {k: v for k, v in _L3_gnn_all.items() if k in ('W', 'b', 'gamma', 'beta')}
    del _L3_gnn_all
    return {'x': x, 'src': src, 'dst': dst, 'edge_attr_40': edge_attr_40, 'edge_type_8': edge_type_8, 'edge_weight': edge_weight, 'edge_weight1': edge_weight1, 'node_type_119': node_type_119, 'node_vec': node_vec, 'L0_gnn_W': _L0_gnn_in['W'], 'L0_gnn_b': _L0_gnn_in['b'], 'L1_gnn_W1': _L1_gnn_in['W1'], 'L1_gnn_b1': _L1_gnn_in['b1'], 'L1_gnn_W2': _L1_gnn_in['W2'], 'L1_gnn_b2': _L1_gnn_in['b2'], 'L1_gnn_emb': _L1_gnn_in['emb'], 'L1_gnn_adaptW': _L1_gnn_in['adaptW'], 'L1_gnn_gamma': _L1_gnn_in['gamma'], 'L1_gnn_beta': _L1_gnn_in['beta'], 'L2_gnn_weight1': _L2_gnn_in['weight1'], 'L2_gnn_weight2': _L2_gnn_in['weight2'], 'L2_gnn_bias1': _L2_gnn_in['bias1'], 'L2_gnn_bias2': _L2_gnn_in['bias2'], 'L3_gnn_W': _L3_gnn_in['W'], 'L3_gnn_b': _L3_gnn_in['b'], 'L3_gnn_gamma': _L3_gnn_in['gamma'], 'L3_gnn_beta': _L3_gnn_in['beta']}

def reference(x, src, dst, edge_attr_40, edge_type_8, edge_weight, edge_weight1, node_type_119, node_vec, L0_gnn_W, L0_gnn_b, L1_gnn_W1, L1_gnn_b1, L1_gnn_W2, L1_gnn_b2, L1_gnn_emb, L1_gnn_adaptW, L1_gnn_gamma, L1_gnn_beta, L2_gnn_weight1, L2_gnn_weight2, L2_gnn_bias1, L2_gnn_bias2, L3_gnn_W, L3_gnn_b, L3_gnn_gamma, L3_gnn_beta):
    import jax
    import jax.numpy as jnp

    def _L0_gnn_ref(features, src, dst, W, b):
        import jax, jax.numpy as jnp
        import numpy as np
        N_NODES = 50000
        N_EDGES = 50000
        D_IN = 48
        D_OUT = 48
        n = features.shape[0]
        ones = jnp.ones(src.shape[0], dtype=features.dtype)
        out_deg = jax.ops.segment_sum(ones, src, num_segments=n)
        in_deg = jax.ops.segment_sum(ones, dst, num_segments=n)
        ci = jax.lax.rsqrt(jnp.maximum(out_deg, 1.0))
        cj = jax.lax.rsqrt(jnp.maximum(in_deg, 1.0))
        msg = features[src] * ci[src][:, None]
        agg = jax.ops.segment_sum(msg, dst, num_segments=n) * cj[:, None]
        h = jnp.where(in_deg[:, None] > 0, agg, features)
        out = jax.nn.relu(h @ W.T + b)
        return out

    def _L1_gnn_ref(h, edge_index, edge_attr, distances, atom_z, node_mult, batch, W1, b1, W2, b2, emb, adaptW, gamma, beta):
        import jax, jax.numpy as jnp
        import numpy as np
        CUTOFF = 6.0
        LN_EPS = 1e-05
        src, dst = (edge_index[0], edge_index[1])
        N = h.shape[0]
        gate = jax.nn.silu(edge_attr @ W1.T + b1) @ W2.T + b2
        ei = emb[atom_z[src]]
        ej = emb[atom_z[dst]]
        adapt_logit = jnp.sum(ei * (ej @ adaptW.T), axis=-1, keepdims=True)
        gate = gate + adapt_logit
        cw = jnp.where(distances < CUTOFF, 0.5 * (jnp.cos(jnp.pi * distances / CUTOFF) + 1.0), 0.0)
        mj = node_mult[dst]
        msg = gate * h[dst] * (cw * mj)[:, None]
        agg = jax.ops.segment_sum(msg, src, num_segments=N)
        tot = jax.ops.segment_sum(mj, src, num_segments=N)
        agg = agg / jnp.clip(tot, 1e-08, None)[:, None]
        x = h + agg
        mu = jnp.mean(x, axis=-1, keepdims=True)
        var = jnp.mean(jnp.square(x - mu), axis=-1, keepdims=True)
        return (x - mu) / jnp.sqrt(var + LN_EPS) * gamma + beta

    def _L2_gnn_ref(inputs, norm, weight1, weight2, bias1, bias2, src, dst, rel_type):
        import jax, jax.numpy as jnp
        import numpy as np
        N_NODES = 50000
        N_EDGES = 50000
        IN_FEAT = 48
        OUT_FEAT = 48
        NUM_RELS = 8
        h1 = jax.nn.relu(jnp.einsum('ni,rij->nrj', inputs, weight1) + bias1)
        h2 = jnp.einsum('nrj,rjo->nro', h1, weight2)
        msg = h2[src, rel_type] * norm
        agg = jax.ops.segment_sum(msg, dst, num_segments=inputs.shape[0])
        return jax.nn.relu(agg + bias2)

    def _L3_gnn_ref(x, edge_index, W, b, gamma, beta):
        import jax, jax.numpy as jnp
        import numpy as np
        N_NODES = 3125
        N_EDGES = 50000
        IN_CH = 48
        OUT_CH = 48
        BN_EPS = 1e-05
        N = x.shape[0]
        loops = jnp.arange(N, dtype=edge_index.dtype)
        src = jnp.concatenate([edge_index[0], loops])
        dst = jnp.concatenate([edge_index[1], loops])
        deg = jax.ops.segment_sum(jnp.ones_like(dst, dtype=x.dtype), dst, num_segments=N)
        dinv = jax.lax.rsqrt(deg)
        norm = dinv[src] * dinv[dst]
        h = x @ W
        msg = h[src] * norm[:, None]
        agg = jax.ops.segment_sum(msg, dst, num_segments=N) + b
        mean = jnp.mean(agg, axis=0)
        var = jnp.mean(jnp.square(agg - mean), axis=0)
        y = (agg - mean) * jax.lax.rsqrt(var + BN_EPS) * gamma + beta
        return jax.nn.relu(y)
    edge_index = jnp.stack([src, dst])
    batch0 = jnp.zeros((50000,), jnp.int32)
    x = _layernorm(x + _L0_gnn_ref(x, src, dst, L0_gnn_W, L0_gnn_b), axis=-1)
    x = _layernorm(x + _L1_gnn_ref(x, edge_index, edge_attr_40, edge_weight, node_type_119, node_vec, batch0, L1_gnn_W1, L1_gnn_b1, L1_gnn_W2, L1_gnn_b2, L1_gnn_emb, L1_gnn_adaptW, L1_gnn_gamma, L1_gnn_beta), axis=-1)
    x = _layernorm(x + _L2_gnn_ref(x, edge_weight1, L2_gnn_weight1, L2_gnn_weight2, L2_gnn_bias1, L2_gnn_bias2, src, dst, edge_type_8), axis=-1)
    x = _layernorm(x + _L3_gnn_ref(x, edge_index, L3_gnn_W, L3_gnn_b, L3_gnn_gamma, L3_gnn_beta), axis=-1)
    return x

_drawn_inputs = setup_inputs


def setup_inputs(seed=0):
    import zlib

    import numpy as np

    out = dict(_drawn_inputs(seed))
    spreads = {'L0_gnn_b': (0.0, 0.1),
     'L1_gnn_gamma': (1.0, 0.2),
     'L1_gnn_beta': (0.0, 0.1),
     'L3_gnn_b': (0.0, 2.0),
     'L3_gnn_gamma': (1.0, 0.2),
     'L3_gnn_beta': (0.0, 0.1)}
    factors = {'node_vec': 10.015,
     'L1_gnn_b1': 40.854,
     'L1_gnn_b2': 25.384,
     'L1_gnn_emb': 64.0,
     'L1_gnn_adaptW': 64.0,
     'edge_attr_40': 3.014}
    for name, (base, spread) in spreads.items():
        noise = np.random.default_rng([zlib.crc32(name.encode()), seed]).standard_normal(out[name].shape)
        drawn = base * np.exp(spread * noise) if base else spread * noise
        out[name] = jnp.asarray(drawn.astype(out[name].dtype))
    for name, factor in factors.items():
        out[name] = (out[name] * factor).astype(out[name].dtype)
    return out
```

```python
from contextlib import ExitStack

import concourse.bass as bass
from concourse import mybir

P = 128
N = 50000
D = 48
G = 25
SUB = 5
UNITS = G // SUB
FULL = P * G
NG = -(-N // FULL)
TAIL0 = (NG - 1) * FULL
TAIL = (N - TAIL0) // G
PAIRS = NG // 2 - 1
SLOTS = SUB
LAG = 2
NR = 8
RBITS = 9
RLOW = 1 << RBITS
RHIGH = -(-N // RLOW)
NZ = 119
NE = 32
NA = 40
EPS = 1e-5
CUTOFF = 6.0
PI = 3.141592653589793
FAR = -1e30
assert TAIL * G == N - TAIL0 and NG % 2 == 0 and SUB * UNITS == G

F32 = mybir.dt.float32
F16 = mybir.dt.float16
BF16 = mybir.dt.bfloat16
I32 = mybir.dt.int32
ALU = mybir.AluOpType
ACT = mybir.ActivationFunctionType
AX = mybir.AxisListType.X


def over_groups(eng, body):
    body(0, 0, P)
    body(0, 1, P)
    with eng.Fori(1, PAIRS) as u:
        body(u, 0, P)
        body(u, 1, P)
    body(PAIRS, 0, P)
    body(PAIRS, 1, TAIL)


def wait(eng, sem, value):
    if not (isinstance(value, int) and value <= 0):
        eng.wait_ge(sem, value)


def hold(eng, sem, value, passed):
    if not (isinstance(value, int) and value <= 0):
        eng.wait_ge(sem, value)
        eng.sem_inc(passed, 1)


def group_rows(dram, g, rows, width=1):
    part = dram[bass.ds(g * FULL, FULL)] if rows == P else dram[TAIL0:N]
    if width == 1 and len(dram.shape) == 1:
        return part.rearrange("(p t) -> p t", t=G)
    return part.rearrange("(p t) c -> p (t c)", t=G)


def group_line(dram, g, rows):
    part = dram[bass.ds(g * FULL, FULL)] if rows == P else dram[TAIL0:N]
    return part.partition_broadcast(rows)


class Steps:

    def __init__(self, eng, sem, per, g):
        self.eng, self.sem, self.per, self.base, self.n = eng, sem, per, g * per, 0

    def did(self, ins):
        ins.then_inc(self.sem, 1)
        self.n += 1

    def wait(self):
        wait(self.eng, self.sem, self.base + self.n)

    def end(self):
        assert self.n == self.per, (self.n, self.per)


def spread(ap, n):
    return ap.unsqueeze(2).broadcast_to([ap.shape[0], ap.shape[1], n])


def along(ap, t):
    return ap.unsqueeze(1).broadcast_to([ap.shape[0], t, ap.shape[1]])


PSUM_OF = {}


class Scope:

    def __init__(self, nc, ctx, tag):
        self.nc, self.ctx, self.tag, self.bank, self.taken = nc, ctx, tag, 0, []
        ctx.callback(self.release)

    def sb(self, name, shape, dt=F32):
        return self.ctx.enter_context(self.nc.sbuf_tensor(f"{self.tag}_{name}", shape, dt))

    def ps(self, shape):
        n = shape[1] if len(shape) == 3 else 1
        part = PSUM_OF[self.nc][0:shape[0], self.bank:self.bank + n, 0:shape[-1]]
        self.bank += n
        assert self.bank <= 8
        return part if len(shape) == 3 else part.rearrange("p b c -> p (b c)")

    def sem(self, name):
        self.taken.append(self.nc.alloc_semaphore(f"{self.tag}_{name}"))
        return self.taken[-1]

    def release(self):
        if self.taken:
            self.nc.clear_and_free_semaphores(self.taken)
            self.nc.all_engine_barrier()

    def sems(self, name, n):
        return [self.sem(f"{name}{i}") for i in range(n)]



def load_constants(nc, keep, d):
    c = {}
    spec = dict(ident=[P, P], before=[P, P], ones=[P, P], spare=[P, 1], w0=[D, D], b0=[1, D], f1=[NA, D],
                f1b=[D, 1], f2=[D, D], f2b=[1, D], embT=[NE, NZ], adT=[NE, NE], ejT=[NE, NZ], pairs=[NZ, NZ],
                gamma1=[P, D], beta1=[P, D], r1=[D + NR + 1, NR * D], r2=[2 * D, NR // 2, D], rb2=[P, D],
                w3=[D, D], b3=[P, D], gamma3=[P, D], beta3=[P, D], farm=[NR, NR * D], zline=[P, NZ],
                rline=[P, NR], mean=[P, D], scale3=[P, D])
    for name, shape in spec.items():
        c[name] = keep.sb(name, shape)
    c["lows"] = keep.sb("lows", [P, RLOW], F16)
    c["highs"] = keep.sb("highs", [P, RHIGH], F16)
    c["zeros"] = keep.sb("zeros", [P, 49 * 49])
    with ExitStack() as ctx:
        s = Scope(nc, ctx, "const")
        landed, shaped, made, multiplied, copied = (s.sem(x) for x in
                                                    ("landed", "shaped", "made", "multiplied", "copied"))
        placed = s.sem("placed")
        pt = s.ps([P, 512])
        block = ctx.enter_context(nc.Block())
        loads = [("w0", d["w0"]), ("b0", d["b0"].unsqueeze(0)), ("f1", d["f1"]),
                 ("f1b", d["f1b"].unsqueeze(1)), ("f2", d["f2"]), ("f2b", d["f2b"].unsqueeze(0)),
                 ("embT", d["embT"]), ("adT", d["adT"]),
                 ("gamma1", d["gamma1"].partition_broadcast(P)), ("beta1", d["beta1"].partition_broadcast(P)),
                 ("rb2", d["rb2"].partition_broadcast(P)), ("w3", d["w3"]),
                 ("b3", d["b3"].partition_broadcast(P)), ("gamma3", d["gamma3"].partition_broadcast(P)),
                 ("beta3", d["beta3"].partition_broadcast(P))]

        @block.sync
        def _(sp):
            for name, src in loads:
                sp.dma_start(c[name][:, :], src).then_inc(landed, 16)
            sp.dma_start(c["r2"][:, :, :], d["r2"].rearrange("(q a) j o -> (a j) q o", a=2)).then_inc(landed, 16)
            for r in range(NR):
                sp.dma_start(c["r1"][0:D, r * D:(r + 1) * D], d["r1"][r]).then_inc(landed, 16)
                sp.dma_start(c["r1"][D + NR:D + NR + 1, r * D:(r + 1) * D],
                             d["rb1"].unsqueeze(0)).then_inc(landed, 16)
            sp.wait_ge(shaped, 7)
            sp.dma_start(c["r1"][D:D + NR, :], c["farm"][:, :]).then_inc(placed, 16)
            sp.wait_ge(placed, 16)

        @block.gpsimd
        def _(pool):
            g = nc.gpsimd
            g.memset(c["ones"][:, :], 1.0).then_inc(made, 1)
            g.memset(c["zeros"][:, :], 0.0).then_inc(made, 1)
            g.memset(c["farm"][:, :], 0.0).then_inc(made, 1)
            g.iota(c["spare"][:, :], [[1, 1]], base=N, channel_multiplier=1,
                   allow_small_or_imprecise_dtypes=True).then_inc(shaped, 1)
            g.iota(c["lows"][:, :], [[1, RLOW]], base=0, channel_multiplier=0,
                   allow_small_or_imprecise_dtypes=True).then_inc(shaped, 1)
            g.iota(c["highs"][:, :], [[1, RHIGH]], base=0, channel_multiplier=0,
                   allow_small_or_imprecise_dtypes=True).then_inc(shaped, 1)
            g.iota(c["zline"][:, :], [[1, NZ]], base=0, channel_multiplier=0,
                   allow_small_or_imprecise_dtypes=True).then_inc(shaped, 1)
            g.iota(c["rline"][:, :], [[1, NR]], base=0, channel_multiplier=0,
                   allow_small_or_imprecise_dtypes=True).then_inc(shaped, 1)
            pool.wait_ge(made, 3)
            g.affine_select(out=c["ident"][:, :], in_=c["zeros"][:, 0:P], compare_op=ALU.not_equal, fill=1.0,
                            base=0, pattern=[[-1, P]], channel_multiplier=1).then_inc(shaped, 1)
            g.affine_select(out=c["farm"][:, :].rearrange("p (r j) -> p r j", r=NR),
                            in_=c["farm"][:, :].rearrange("p (r j) -> p r j", r=NR),
                            compare_op=ALU.not_equal, fill=FAR, base=0, pattern=[[-1, NR], [0, D]],
                            channel_multiplier=1).then_inc(shaped, 1)
            g.affine_select(out=c["before"][:, :], in_=c["ones"][:, :], compare_op=ALU.is_gt, fill=0.0,
                            base=0, pattern=[[-1, P]], channel_multiplier=1).then_inc(shaped, 1)
            pool.wait_ge(shaped, 8)

        @block.tensor
        def _(pe):
            pe.wait_ge(landed, 16 * (len(loads) + 1 + 2 * NR))
            nc.tensor.matmul(pt[0:NE, 0:NZ], c["adT"][:, :], c["embT"][:, :], start=True,
                             stop=True).then_inc(multiplied, 1)
            pe.wait_ge(copied, 1)
            nc.tensor.matmul(pt[0:NZ, 128:128 + NZ], c["ejT"][:, :], c["embT"][:, :], start=True,
                             stop=True).then_inc(multiplied, 1)

        @block.scalar
        def _(act):
            act.wait_ge(multiplied, 1)
            nc.scalar.activation(c["ejT"][:, :], pt[0:NE, 0:NZ], ACT.Copy).then_inc(copied, 1)
            act.wait_ge(multiplied, 2)
            nc.scalar.activation(c["pairs"][:, :], pt[0:NZ, 128:128 + NZ], ACT.Copy).then_inc(copied, 1)
            act.wait_ge(copied, 2)
    return c



def clear_sums(nc, eng, sums, width, cleared):
    n = 0
    for copy in sums:
        rows = copy.rearrange("(k p q) c -> k p (q c)", p=P, q=49)
        for k in range(rows.shape[0]):
            eng.dma_start(rows[k], ZEROS[nc][:, 0:49 * width]).then_inc(cleared, 16)
            n += 16
    return n


ZEROS = {}


def out_degree(nc, c, d, sums0):
    with ExitStack() as ctx:
        s = Scope(nc, ctx, "deg")
        key = [s.sb(f"key{b}", [P, G], I32) for b in range(2)]
        part = s.sb("part", [P, 2, G], I32)
        partf = [s.sb(f"partf{b}", [P, 2, G]) for b in range(2)]
        low = [s.sb(f"low{k}", [P, SUB, RLOW], BF16) for k in range(2)]
        high = [s.sb(f"high{k}", [P, SUB, RHIGH], BF16) for k in range(2)]
        count = s.sb("count", [RHIGH, RLOW])
        ps = s.ps([RHIGH, RLOW])
        loaded = s.sems("loaded", 2)
        stepped, hot, used, counted, copied, stored, cleared = (
            s.sem(x) for x in ("stepped", "hot", "used", "counted", "copied", "stored", "cleared"))
        block = ctx.enter_context(nc.Block())

        @block.sync
        def _(sp):
            def body(u, b, rows):
                g = 2 * u + b
                wait(sp, stepped, 4 * (g - 1))
                sp.dma_start(key[b][0:rows, :], group_rows(d["src"], g, rows)).then_inc(loaded[b], 16)
            over_groups(sp, body)
            sp.wait_ge(copied, 1)
            sp.dma_start(d["outdeg"].rearrange("(h l) -> h l", l=RLOW), count[:, :]).then_inc(stored, 16)
            sp.wait_ge(stored, 16)

        @block.scalar
        def _(act):
            n = clear_sums(nc, act, sums0, 49, cleared)
            act.wait_ge(cleared, n)

        @block.vector
        def _(dve):
            v = nc.vector

            def body(u, b, rows):
                g = 2 * u + b
                st = Steps(dve, stepped, 4, g)
                wait(dve, loaded[b], 16 * (u + 1))
                st.did(v.tensor_scalar(part[0:rows, 0, :], key[b][0:rows, :], RBITS, None,
                                       ALU.logical_shift_right))
                st.did(v.tensor_scalar(part[0:rows, 1, :], key[b][0:rows, :], RLOW - 1, None, ALU.bitwise_and))
                st.wait()
                wait(dve, used, 5 * (g - 1))
                st.did(v.tensor_copy(partf[b][0:rows, 0, :], part[0:rows, 0, :]))
                st.did(v.tensor_copy(partf[b][0:rows, 1, :], part[0:rows, 1, :]))
                st.wait()
                for k in range(UNITS):
                    r = (b + k) % 2
                    wait(dve, used, 5 * g + k - 1)
                    for t in range(SUB):
                        col = SUB * k + t
                        v.tensor_scalar(high[r][0:rows, t, :], c["highs"][0:rows, :],
                                        partf[b][0:rows, 0, col:col + 1], None, ALU.is_equal)
                        last = v.tensor_scalar(low[r][0:rows, t, :], c["lows"][0:rows, :],
                                               partf[b][0:rows, 1, col:col + 1], None, ALU.is_equal)
                    last.then_inc(hot, 1)
                st.end()
            over_groups(dve, body)
            dve.wait_ge(counted, 1)
            v.tensor_copy(count[:, :], ps[:, :]).then_inc(copied, 1)

        @block.tensor
        def _(pe):
            def body(u, b, rows):
                g = 2 * u + b
                for k in range(UNITS):
                    r = (b + k) % 2
                    wait(pe, hot, 5 * g + k + 1)
                    for t in range(SUB):
                        first = isinstance(u, int) and u == 0 and b == 0 and k == 0 and t == 0
                        end = rows == TAIL and k == UNITS - 1 and t == SUB - 1
                        last = nc.tensor.matmul(ps[:, :], high[r][0:rows, t, :], low[r][0:rows, t, :],
                                                start=first, stop=end)
                    last.then_inc(used, 1)
            over_groups(pe, body)
            pe.wait_ge(used, UNITS * NG)
            pe.sem_inc(counted, 1)


def first_table(nc, c, d):
    with ExitStack() as ctx:
        s = Scope(nc, ctx, "t0")
        x = [s.sb(f"x{b}", [P, G * D]) for b in range(2)]
        deg = [s.sb(f"deg{b}", [P, G]) for b in range(2)]
        z = [s.sb(f"z{b}", [P, G], I32) for b in range(2)]
        row = [s.sb(f"row{b}", [P, G, D + 2]) for b in range(2)]
        dm = s.sb("dm", [P, G])
        root = s.sb("root", [P, G])
        ci = s.sb("ci", [P, G])
        loaded, stored = s.sems("loaded", 2), s.sems("stored", 2)
        stepped, rooted, built = s.sem("stepped"), s.sem("rooted"), s.sem("built")
        block = ctx.enter_context(nc.Block())

        @block.sync
        def _(sp):
            def body(u, b, rows):
                g = 2 * u + b
                wait(sp, built, g - 1)
                sp.dma_start(x[b][0:rows, :], group_rows(d["x"], g, rows, D)).then_inc(loaded[b], 16)
                sp.dma_start(deg[b][0:rows, :], group_rows(d["outdeg"], g, rows)).then_inc(loaded[b], 16)
                sp.dma_start(z[b][0:rows, :], group_rows(d["z"], g, rows)).then_inc(loaded[b], 16)
            over_groups(sp, body)

        @block.vector
        def _(dve):
            v = nc.vector

            def body(u, b, rows):
                g = 2 * u + b
                st = Steps(dve, stepped, 4, g)
                R = slice(0, rows)
                wait(dve, loaded[b], 48 * (u + 1))
                st.did(v.tensor_scalar_max(dm[R, :], deg[b][R, :], 1.0))
                wait(dve, stored[b], 16 * u)
                st.did(v.tensor_copy(row[b][R, :, D + 1], z[b][R, :]))
                st.did(v.tensor_copy(row[b][R, :, D], c["ones"][R, 0:G]))
                wait(dve, rooted, g + 1)
                st.did(v.reciprocal(ci[R, :], root[R, :]))
                st.wait()
                v.tensor_tensor(row[b][R, :, 0:D], x[b][R, :].rearrange("p (t c) -> p t c", c=D),
                                spread(ci[R, :], D), ALU.mult).then_inc(built, 1)
                st.end()
            over_groups(dve, body)

        @block.scalar
        def _(act):
            def body(u, b, rows):
                g = 2 * u + b
                R = slice(0, rows)
                wait(act, stepped, 4 * g + 1)
                nc.scalar.activation(root[R, :], dm[R, :], ACT.Sqrt).then_inc(rooted, 1)
                wait(act, built, g + 1)
                act.dma_start(group_rows(d["table0"], g, rows, D + 2),
                              row[b][R, :, :].rearrange("p t c -> p (t c)")).then_inc(stored[b], 16)
            over_groups(act, body)
            act.wait_ge(stored[0], 16 * (PAIRS + 1))
            act.wait_ge(stored[1], 16 * (PAIRS + 1))


class EdgeStage:

    def __init__(self, nc, ctx, c, d, tag, *, table, width, source, target, sums, out_width, clear):
        self.nc, self.c, self.d = nc, c, d
        self.table, self.width, self.sums, self.out_width = d[table], width, [d[x] for x in sums], out_width
        self.source, self.target, self.clear = source, target, clear
        s = self.s = Scope(nc, ctx, tag)
        self.take = [s.sb(f"take{b}", [P, G], I32) for b in range(2)]
        self.key = [s.sb(f"key{b}", [P, G], I32) for b in range(2)]
        self.line = [s.sb(f"line{b}", [P, FULL], I32) for b in range(2)]
        self.keyf = [s.sb(f"keyf{b}", [P, G]) for b in range(2)]
        self.keyd = [s.sb(f"keyd{b}", [P, G]) for b in range(2)]
        self.put = [s.sb(f"put{b}", [P, G], I32) for b in range(2)]
        self.same = [s.sb(f"same{k}", [P, SUB * P]) for k in range(SLOTS)]
        self.earlier = s.sb("earlier", [P, SUB, P])
        self.nearlier = s.sb("nearlier", [P, SUB])
        self.putd = s.sb("putd", [P, SUB])
        self.total = [s.sb(f"total{k}", [P, SUB, out_width]) for k in range(SLOTS)]
        self.psum = s.ps([P, 512])
        self.take_loaded = s.sems("take_loaded", 2)
        self.keys_loaded = s.sems("keys_loaded", 2)
        self.gathered = s.sems("gathered", SLOTS)
        self.added = s.sems("added", 2)
        self.put_ready = s.sem("put_ready")
        self.same_ready = s.sem("same_ready")
        self.summed = s.sem("summed")
        self.total_ready = s.sem("total_ready")
        self.keyed = s.sem("keyed")
        self.passed = s.sem("passed")
        self.cleared = s.sem("cleared")

    def load_indices(self, sp, u, b, rows):
        g = 2 * u + b
        wait(sp, self.gathered[SLOTS - 1], 16 * SUB * (g - 1))
        sp.dma_start(self.take[b][0:rows, :], group_rows(self.d[self.source], g, rows)).then_inc(
            self.take_loaded[b], 16)
        wait(sp, self.put_ready, UNITS * (g - 1))
        sp.dma_start(self.key[b][0:rows, :], group_rows(self.d[self.target], g, rows)).then_inc(
            self.keys_loaded[b], 16)
        sp.dma_start(self.line[b][0:rows, 0:rows * G], group_line(self.d[self.target + "_line"], g, rows)).then_inc(
            self.keys_loaded[b], 16)

    def gather(self, pool, u, b, rows, k, into, freed):
        g = 2 * u + b
        if k == 0:
            hold(pool, self.take_loaded[b], 16 * (u + 1), self.passed)
        hold(pool, freed, UNITS * g + k - (SLOTS - 1), self.passed)
        for t in range(SUB):
            col = SUB * k + t
            self.nc.gpsimd.indirect_dma_start(
                out=into[k][0:rows, t, 0:self.width], out_offset=None, in_=self.table,
                in_offset=bass.IndirectOffsetOnAxis(ap=self.take[b][0:rows, col:col + 1], axis=0),
            ).then_inc(self.gathered[k], 16)

    def scatter(self, pool, u, b, rows, k):
        g = 2 * u + b
        hold(pool, self.put_ready, UNITS * g + k + 1, self.passed)
        hold(pool, self.total_ready, UNITS * g + k + 1, self.passed)
        for t in range(SUB):
            col = SUB * k + t
            copy = (b + col) % 2
            hold(pool, self.added[copy], 16 * (G * u + (G * b + col) // 2), self.passed)
            self.nc.gpsimd.indirect_dma_start(
                out=self.sums[copy], in_=self.total[k][0:rows, t, :], in_offset=None,
                out_offset=bass.IndirectOffsetOnAxis(ap=self.put[b][0:rows, col:col + 1], axis=0),
                compute_op=ALU.add).then_inc(self.added[copy], 16)

    def pool_program(self, pool, into, freed):
        def body(u, b, rows):
            first = isinstance(u, int) and u == 0 and b == 0
            for k in range(UNITS):
                self.gather(pool, u, b, rows, k, into, freed)
                if k >= LAG:
                    self.scatter(pool, u, b, rows, k - LAG)
                elif not first:
                    self.scatter(pool, u if b else u - 1, 1 - b, P, k - LAG + UNITS)
        over_groups(pool, body)
        for k in range(UNITS - LAG, UNITS):
            self.scatter(pool, PAIRS, 1, TAIL, k)
        for copy in range(2):
            pool.wait_ge(self.added[copy], 16 * G * NG // 2)

    KEY_STEPS = 2 + 4 * UNITS

    def key_group(self, dve, st, u, b, rows):
        g = 2 * u + b
        v, R = self.nc.vector, slice(0, rows)
        wait(dve, self.keys_loaded[b], 32 * (u + 1))
        st.did(v.tensor_copy(self.keyf[b][R, :], self.key[b][R, :]))
        st.wait()
        st.did(v.tensor_scalar(self.keyd[b][R, :], self.keyf[b][R, :], self.c["spare"][R, 0:1], None, ALU.subtract))
        st.wait()
        for copy in range(2):
            wait(dve, self.added[copy], 16 * (G * u + (G * (b - 1) + 1 - copy) // 2))

    def same_unit(self, dve, st, u, b, rows, k):
        g = 2 * u + b
        v, R = self.nc.vector, slice(0, rows)
        wait(dve, self.summed, UNITS * g + k - (SLOTS - 1))
        for t in range(SUB):
            col = SUB * k + t
            last = v.tensor_scalar(self.same[k][R, t * rows:(t + 1) * rows],
                                   self.line[b][R, col * rows:(col + 1) * rows],
                                   self.keyf[b][R, col:col + 1], None, ALU.is_equal)
        last.then_inc(self.same_ready, 1)
        wait(dve, self.same_ready, UNITS * g + k + 1)
        cols = slice(SUB * k, SUB * (k + 1))
        st.did(v.tensor_tensor(self.earlier[R, :, R], self.same[k][R, 0:SUB * rows].rearrange("p (t e) -> p t e", t=SUB),
                               along(self.c["before"][R, R], SUB), ALU.mult))
        st.wait()
        st.did(v.tensor_reduce(self.nearlier[R, :], self.earlier[R, :, R], AX, ALU.add))
        st.wait()
        st.did(v.tensor_scalar(self.nearlier[R, :], self.nearlier[R, :], 0.0, None, ALU.is_equal))
        st.wait()
        st.did(v.tensor_tensor(self.putd[R, :], self.nearlier[R, :], self.keyd[b][R, cols], ALU.mult))
        st.wait()
        v.tensor_scalar(self.put[b][R, cols], self.putd[R, :], self.c["spare"][R, 0:1], None,
                        ALU.add).then_inc(self.put_ready, 1)

    def sum_unit(self, pe, u, b, rows, k, messages):
        g = 2 * u + b
        W, R = self.out_width, slice(0, rows)
        wait(pe, self.same_ready, UNITS * g + k + 1)
        wait(pe, self.total_ready, UNITS * g + k)
        for t in range(SUB):
            last = self.nc.tensor.matmul(self.psum[R, t * W:(t + 1) * W], self.same[k][R, t * rows:(t + 1) * rows],
                                         messages[R, t, 0:W], start=True, stop=True)
        last.then_inc(self.summed, 1)

    def copy_unit(self, act, u, b, rows, k):
        g = 2 * u + b
        R = slice(0, rows)
        wait(act, self.summed, UNITS * g + k + 1)
        J = G * b + SUB * k + SUB - G
        for copy in range(2):
            wait(act, self.added[copy], 16 * (G * u + (J + 1 - copy) // 2))
        self.nc.scalar.activation(self.total[k][R, :, :].rearrange("p t c -> p (t c)"),
                                  self.psum[R, 0:SUB * self.out_width], ACT.Copy).then_inc(self.total_ready, 1)

    def clear_next(self, act):
        if self.clear is None:
            return 0
        names, width = self.clear
        return clear_sums(self.nc, act, [self.d[x] for x in names], width, self.cleared)


def plain_edges(nc, c, d, tag, table, width, sums, out_width, clear, types):
    with ExitStack() as ctx:
        e = EdgeStage(nc, ctx, c, d, tag, table=table, width=width, source="src", target="dst", sums=sums,
                      out_width=out_width, clear=clear)
        rows_of = [e.s.sb(f"rows{k}", [P, SUB, width]) for k in range(SLOTS)]
        kind = [e.s.sb(f"kind{b}", [P, G]) for b in range(2)]
        kind_taken = e.s.sem("kind_taken")
        kind_stored = e.s.sems("kind_stored", 2)
        block = ctx.enter_context(nc.Block())

        @block.sync
        def _(sp):
            over_groups(sp, lambda u, b, rows: e.load_indices(sp, u, b, rows))

        @block.gpsimd
        def _(pool):
            e.pool_program(pool, rows_of, e.total_ready)

        @block.vector
        def _(dve):
            def body(u, b, rows):
                st = Steps(dve, e.keyed, e.KEY_STEPS, 2 * u + b)
                e.key_group(dve, st, u, b, rows)
                for k in range(UNITS):
                    e.same_unit(dve, st, u, b, rows, k)
                st.end()
            over_groups(dve, body)

        @block.tensor
        def _(pe):
            def body(u, b, rows):
                for k in range(UNITS):
                    wait(pe, e.gathered[k], 16 * SUB * (2 * u + b + 1))
                    e.sum_unit(pe, u, b, rows, k, rows_of[k])
            over_groups(pe, body)

        @block.scalar
        def _(act):
            n = e.clear_next(act)

            def body(u, b, rows):
                g = 2 * u + b
                if types:
                    wait(act, kind_stored[b], 16 * u)
                for k in range(UNITS):
                    if types:
                        wait(act, e.gathered[k], 16 * SUB * (g + 1))
                        nc.scalar.activation(kind[b][0:rows, SUB * k:SUB * (k + 1)],
                                             rows_of[k][0:rows, :, width - 1], ACT.Copy).then_inc(kind_taken, 1)
                    e.copy_unit(act, u, b, rows, k)
                if types:
                    wait(act, kind_taken, UNITS * (g + 1))
                    act.dma_start(group_rows(d["srctype"], g, rows), kind[b][0:rows, :]).then_inc(kind_stored[b], 16)
            over_groups(act, body)
            if types:
                for b in range(2):
                    act.wait_ge(kind_stored[b], 16 * (PAIRS + 1))
            wait(act, e.cleared, n)


def filter_edges(nc, c, d):
    W1 = D + 2
    A, B = 3, SUB - 3
    with ExitStack() as ctx:
        e = EdgeStage(nc, ctx, c, d, "flt", table="table1", width=W1, source="dst", target="src",
                      sums=("sum1a", "sum1b"), out_width=D + 1, clear=(("sum2a", "sum2b"), D))
        s = e.s
        rows_of = [s.sb(f"rows{k}", [P, SUB, W1]) for k in range(SLOTS)]
        attr = [s.sb(f"attr{b}", [NA, FULL]) for b in range(2)]
        dist = [s.sb(f"dist{b}", [P, G]) for b in range(2)]
        kind = [s.sb(f"kind{b}", [P, G]) for b in range(2)]
        near = s.sb("near", [P, G])
        sine = s.sb("sine", [P, G])
        inside = s.sb("inside", [P, G])
        cut = [s.sb(f"cut{b}", [P, G]) for b in range(2)]
        hot_d = s.sb("hot_d", [P, SUB, NZ])
        hot_s = s.sb("hot_s", [P, SUB, NZ])
        hot_dT = s.sb("hot_dT", [NZ, SUB * P])
        hidden = s.sb("hidden", [D, SUB * P])
        picked = s.sb("picked", [P, SUB, NZ])
        logit = s.sb("logit", [P, SUB])
        weight = s.sb("weight", [P, SUB])
        hw = s.sb("hw", [P, SUB, D])
        gated = s.sb("gated", [P, SUB, D])
        message = [s.sb(f"message{k}", [P, SUB, D + 1]) for k in range(2)]
        p_hidden = s.ps([P, 2, 512])
        p_hot = s.ps([P, 2, 512])
        p_pair = s.ps([P, 2, 512])
        p_gate = s.ps([P, 512])
        linear_loaded = s.sems("linear_loaded", 2)
        pe_passed = s.sem("pe_passed")
        near_ready, sine_ready, hot_ready, hidden_mult, hidden_ready = (
            s.sem(x) for x in ("near_ready", "sine_ready", "hot_ready", "hidden_mult", "hidden_ready"))
        turned, turned_copied, pair_ready, gate_ready, message_ready = (
            s.sem(x) for x in ("turned", "turned_copied", "pair_ready", "gate_ready", "message_ready"))
        block = ctx.enter_context(nc.Block())

        @block.sync
        def _(sp):
            def body(u, b, rows):
                g = 2 * u + b
                e.load_indices(sp, u, b, rows)
                wait(sp, message_ready, UNITS * (g - 1))
                if rows == P:
                    sp.dma_start(attr[b][:, :], d["attr"][bass.ds(g * NA, NA), :]).then_inc(linear_loaded[b], 16)
                else:
                    sp.dma_start(attr[b][:, 0:rows * G], d["attr_tail"]).then_inc(linear_loaded[b], 16)
                sp.dma_start(dist[b][0:rows, :], group_rows(d["dist"], g, rows)).then_inc(linear_loaded[b], 16)
                sp.dma_start(kind[b][0:rows, :], group_rows(d["srctype"], g, rows)).then_inc(linear_loaded[b], 16)
            over_groups(sp, body)

        @block.gpsimd
        def _(pool):
            e.pool_program(pool, rows_of, message_ready)

        @block.vector
        def _(dve):
            v = nc.vector

            def body(u, b, rows):
                g = 2 * u + b
                R = slice(0, rows)
                st = Steps(dve, e.keyed, e.KEY_STEPS + 4 + 8 * UNITS, g)
                e.key_group(dve, st, u, b, rows)
                wait(dve, linear_loaded[b], 48 * (u + 1))
                v.tensor_scalar(near[R, :], dist[b][R, :], CUTOFF, PI / (2 * CUTOFF), ALU.min,
                                ALU.mult).then_inc(near_ready, 1)
                st.did(v.tensor_scalar(inside[R, :], dist[b][R, :], CUTOFF, None, ALU.is_lt))
                wait(dve, sine_ready, g + 1)
                st.did(v.tensor_tensor(cut[b][R, :], sine[R, :], sine[R, :], ALU.mult))
                st.wait()
                st.did(v.tensor_scalar(cut[b][R, :], cut[b][R, :], -1.0, 1.0, ALU.mult, ALU.add))
                st.wait()
                st.did(v.tensor_tensor(cut[b][R, :], cut[b][R, :], inside[R, :], ALU.mult))
                for k in range(UNITS):
                    q = UNITS * g + k
                    wait(dve, e.gathered[k], 16 * SUB * (g + 1))
                    got = rows_of[k]
                    wait(dve, turned, q)
                    v.tensor_tensor(hot_d[R, :, :], spread(got[R, :, W1 - 1], NZ), along(c["zline"][R, :], SUB),
                                    ALU.is_equal).then_inc(hot_ready, 1)
                    cols = slice(SUB * k, SUB * (k + 1))
                    st.wait()
                    st.did(v.tensor_tensor(hot_s[R, :, :], spread(kind[b][R, cols], NZ),
                                           along(c["zline"][R, :], SUB), ALU.is_equal))
                    e.same_unit(dve, st, u, b, rows, k)
                    st.did(v.tensor_tensor(weight[R, :], cut[b][R, cols], got[R, :, D], ALU.mult))
                    st.wait()
                    st.did(v.tensor_tensor(hw[R, :, :], got[R, :, 0:D], spread(weight[R, :], D), ALU.mult))
                    wait(dve, pair_ready, q + 1)
                    st.did(v.tensor_tensor(picked[R, 0:A, :], p_pair[R, 0, 0:A * NZ].rearrange("p (t z) -> p t z", t=A),
                                           hot_s[R, 0:A, :], ALU.mult))
                    st.did(v.tensor_tensor(picked[R, A:SUB, :], p_pair[R, 1, 0:B * NZ].rearrange("p (t z) -> p t z", t=B),
                                           hot_s[R, A:SUB, :], ALU.mult))
                    st.wait()
                    st.did(v.tensor_reduce(logit[R, :], picked[R, :, :], AX, ALU.add))
                    st.wait()
                    wait(dve, gate_ready, q + 1)
                    st.did(v.tensor_tensor(gated[R, :, :], p_gate[R, 0:SUB * D].rearrange("p (t c) -> p t c", t=SUB),
                                           spread(logit[R, :], D), ALU.add))
                    st.wait()
                    m = message[(b + k) % 2]
                    wait(dve, e.summed, q - 1)
                    st.did(v.tensor_copy(m[R, :, D], got[R, :, D]))
                    v.tensor_tensor(m[R, :, 0:D], gated[R, :, :], hw[R, :, :], ALU.mult).then_inc(message_ready, 1)
                st.end()
            over_groups(dve, body)

        @block.tensor
        def _(pe):
            def body(u, b, rows):
                g = 2 * u + b
                R = slice(0, rows)
                hold(pe, linear_loaded[b], 48 * (u + 1), pe_passed)
                for k in range(UNITS):
                    q = UNITS * g + k
                    hold(pe, hidden_ready, q, pe_passed)
                    for bank, t0, n in ((0, 0, A), (1, A, B)):
                        at = (SUB * k + t0) * rows
                        last = nc.tensor.matmul(p_hidden[0:D, bank, 0:n * rows], c["f1"][:, :],
                                                attr[b][:, at:at + n * rows], start=True, stop=True)
                    last.then_inc(hidden_mult, 1)
                    wait(pe, hot_ready, q + 1)
                    wait(pe, turned_copied, q)
                    for t in range(SUB):
                        bank, o = (0, t) if t < A else (1, t - A)
                        last = nc.tensor.transpose(p_hot[0:NZ, bank, o * rows:(o + 1) * rows], hot_d[R, t, :],
                                                   c["ident"][R, R])
                    last.then_inc(turned, 1)
                    wait(pe, turned_copied, q + 1)
                    wait(pe, message_ready, q)
                    for t in range(SUB):
                        bank, o = (0, t) if t < A else (1, t - A)
                        last = nc.tensor.matmul(p_pair[R, bank, o * NZ:(o + 1) * NZ],
                                                hot_dT[:, t * rows:(t + 1) * rows], c["pairs"][:, :],
                                                start=True, stop=True)
                    last.then_inc(pair_ready, 1)
                    wait(pe, hidden_ready, q + 1)
                    for t in range(SUB):
                        nc.tensor.matmul(p_gate[R, t * D:(t + 1) * D], hidden[:, t * rows:(t + 1) * rows],
                                         c["f2"][:, :], start=True, stop=False)
                        last = nc.tensor.matmul(p_gate[R, t * D:(t + 1) * D], c["ones"][0:1, R], c["f2b"][:, :],
                                                start=False, stop=True)
                    last.then_inc(gate_ready, 1)
                    wait(pe, message_ready, q + 1)
                    e.sum_unit(pe, u, b, rows, k, message[(b + k) % 2])
            over_groups(pe, body)

        @block.scalar
        def _(act):
            n = e.clear_next(act)

            def body(u, b, rows):
                g = 2 * u + b
                R = slice(0, rows)
                wait(act, near_ready, g + 1)
                nc.scalar.activation(sine[R, :], near[R, :], ACT.Sin).then_inc(sine_ready, 1)
                for k in range(UNITS):
                    q = UNITS * g + k
                    wait(act, hidden_mult, q + 1)
                    wait(act, gate_ready, q)
                    nc.scalar.activation(hidden[:, 0:A * rows], p_hidden[0:D, 0, 0:A * rows], ACT.Silu,
                                         bias=c["f1b"][:, 0:1])
                    nc.scalar.activation(hidden[:, A * rows:SUB * rows], p_hidden[0:D, 1, 0:B * rows], ACT.Silu,
                                         bias=c["f1b"][:, 0:1]).then_inc(hidden_ready, 1)
                    wait(act, turned, q + 1)
                    wait(act, pair_ready, q)
                    nc.scalar.activation(hot_dT[:, 0:A * rows], p_hot[0:NZ, 0, 0:A * rows], ACT.Copy)
                    nc.scalar.activation(hot_dT[:, A * rows:SUB * rows], p_hot[0:NZ, 1, 0:B * rows],
                                         ACT.Copy).then_inc(turned_copied, 1)
                    e.copy_unit(act, u, b, rows, k)
            over_groups(act, body)
            wait(act, e.cleared, n)


def relation_edges(nc, c, d):
    K = D + NR + 1
    A, B = 3, SUB - 3
    CH = NR // 2
    with ExitStack() as ctx:
        e = EdgeStage(nc, ctx, c, d, "rel", table="table2", width=D, source="src", target="dst",
                      sums=("sum2a", "sum2b"), out_width=D, clear=(("sum3a", "sum3b"), D))
        s = e.s
        rows_of = [s.sb(f"rows{k}", [P, SUB, K]) for k in range(SLOTS)]
        norm = [s.sb(f"norm{b}", [P, G]) for b in range(2)]
        rel = [s.sb(f"rel{b}", [P, G], I32) for b in range(2)]
        relf = s.sb("relf", [P, G])
        xT = s.sb("xT", [K, SUB * P])
        h1 = [s.sb(f"h1_{q}", [2 * D, SUB * P]) for q in range(CH)]
        message = [s.sb(f"message{k}", [P, SUB, D]) for k in range(2)]
        p_x = s.ps([P, 2, 512])
        p_h1 = [s.ps([P, 2, 512]) for q in range(2)]
        p_h2 = s.ps([P, 512])
        linear_loaded = s.sems("linear_loaded", 2)
        pe_passed = s.sem("pe_passed")
        ones_ready, off_ready, turned, turned_copied, h2_ready, message_ready = (
            s.sem(x) for x in ("ones_ready", "off_ready", "turned", "turned_copied", "h2_ready", "message_ready"))
        h1_mult = s.sems("h1_mult", 2)
        h1_ready = s.sems("h1_ready", 2)
        block = ctx.enter_context(nc.Block())

        @block.sync
        def _(sp):
            def body(u, b, rows):
                g = 2 * u + b
                e.load_indices(sp, u, b, rows)
                wait(sp, message_ready, UNITS * (g - 1))
                sp.dma_start(norm[b][0:rows, :], group_rows(d["norm"], g, rows)).then_inc(linear_loaded[b], 16)
                sp.dma_start(rel[b][0:rows, :], group_rows(d["rel"], g, rows)).then_inc(linear_loaded[b], 16)
            over_groups(sp, body)

        @block.gpsimd
        def _(pool):
            e.pool_program(pool, rows_of, turned)

        @block.vector
        def _(dve):
            v = nc.vector
            for k in range(SLOTS):
                v.tensor_copy(rows_of[k][:, :, K - 1], c["ones"][:, 0:SUB]).then_inc(ones_ready, 1)

            def relu(rows, q):
                ps = p_h1[q % 2]
                v.tensor_scalar_max(h1[q][:, 0:A * rows], ps[0:2 * D, 0, 0:A * rows], 0.0)
                v.tensor_scalar_max(h1[q][:, A * rows:SUB * rows], ps[0:2 * D, 1, 0:B * rows],
                                    0.0).then_inc(h1_ready[1], 1)

            def body(u, b, rows):
                g = 2 * u + b
                R = slice(0, rows)
                st = Steps(dve, e.keyed, e.KEY_STEPS + 1, g)
                e.key_group(dve, st, u, b, rows)
                wait(dve, linear_loaded[b], 32 * (u + 1))
                st.did(v.tensor_copy(relf[R, :], rel[b][R, :]))
                st.wait()
                for k in range(UNITS):
                    q = UNITS * g + k
                    cols = slice(SUB * k, SUB * (k + 1))
                    wait(dve, turned, q - (SLOTS - 1))
                    v.tensor_tensor(rows_of[k][R, :, D:D + NR], spread(relf[R, cols], NR),
                                    along(c["rline"][R, :], SUB), ALU.not_equal).then_inc(off_ready, 1)
                    e.same_unit(dve, st, u, b, rows, k)
                    for i in range(2):
                        wait(dve, h1_mult[1], 2 * q + i + 1)
                        wait(dve, h2_ready, q)
                        relu(rows, 2 * i + 1)
                    wait(dve, h2_ready, q + 1)
                    wait(dve, e.summed, q - 1)
                    v.tensor_tensor(message[(b + k) % 2][R, :, :],
                                    p_h2[R, 0:SUB * D].rearrange("p (t c) -> p t c", t=SUB),
                                    spread(norm[b][R, cols], D), ALU.mult).then_inc(message_ready, 1)
                st.end()
            over_groups(dve, body)

        @block.tensor
        def _(pe):
            pe.wait_ge(ones_ready, SLOTS)

            def body(u, b, rows):
                g = 2 * u + b
                R = slice(0, rows)
                for k in range(UNITS):
                    q = UNITS * g + k
                    hold(pe, e.gathered[k], 16 * SUB * (g + 1), pe_passed)
                    hold(pe, off_ready, q + 1, pe_passed)
                    hold(pe, turned_copied, q, pe_passed)
                    for t in range(SUB):
                        bank, o = (0, t) if t < A else (1, t - A)
                        last = nc.tensor.transpose(p_x[0:K, bank, o * rows:(o + 1) * rows], rows_of[k][R, t, :],
                                                   c["ident"][R, R])
                    last.then_inc(turned, 1)
                    wait(pe, turned_copied, q + 1)
                    for ch in range(CH):
                        wait(pe, h1_ready[ch % 2], 2 * q + ch // 2)
                        for bank, t0, n in ((0, 0, A), (1, A, B)):
                            last = nc.tensor.matmul(p_h1[ch % 2][0:2 * D, bank, 0:n * rows],
                                                    c["r1"][:, ch * 2 * D:(ch + 1) * 2 * D],
                                                    xT[:, t0 * rows:(t0 + n) * rows], start=True, stop=True)
                        last.then_inc(h1_mult[ch % 2], 1)
                    wait(pe, message_ready, q)
                    wait(pe, h1_ready[0], 2 * q + 2)
                    wait(pe, h1_ready[1], 2 * q + 2)
                    for t in range(SUB):
                        for ch in range(CH):
                            last = nc.tensor.matmul(p_h2[R, t * D:(t + 1) * D], h1[ch][:, t * rows:(t + 1) * rows],
                                                    c["r2"][:, ch, :], start=(ch == 0), stop=(ch == CH - 1))
                    last.then_inc(h2_ready, 1)
                    wait(pe, message_ready, q + 1)
                    e.sum_unit(pe, u, b, rows, k, message[(b + k) % 2])
            over_groups(pe, body)

        @block.scalar
        def _(act):
            n = e.clear_next(act)

            def body(u, b, rows):
                g = 2 * u + b
                for k in range(UNITS):
                    q = UNITS * g + k
                    wait(act, turned, q + 1)
                    wait(act, h1_mult[1], 2 * q)
                    nc.scalar.activation(xT[:, 0:A * rows], p_x[0:K, 0, 0:A * rows], ACT.Copy)
                    nc.scalar.activation(xT[:, A * rows:SUB * rows], p_x[0:K, 1, 0:B * rows],
                                         ACT.Copy).then_inc(turned_copied, 1)
                    for i in range(2):
                        wait(act, h1_mult[0], 2 * q + i + 1)
                        wait(act, h2_ready, q)
                        ps = p_h1[0]
                        nc.scalar.activation(h1[2 * i][:, 0:A * rows], ps[0:2 * D, 0, 0:A * rows], ACT.Relu)
                        nc.scalar.activation(h1[2 * i][:, A * rows:SUB * rows], ps[0:2 * D, 1, 0:B * rows],
                                             ACT.Relu).then_inc(h1_ready[0], 1)
                    e.copy_unit(act, u, b, rows, k)
            over_groups(act, body)
            wait(act, e.cleared, n)


class Norm:

    STEPS = 6

    def __init__(self, s, nc, tag):
        self.nc = nc
        self.total = s.sb(tag + "_total", [P, G])
        self.mean = s.sb(tag + "_mean", [P, G])
        self.centred = s.sb(tag + "_centred", [P, G, D])
        self.square = s.sb(tag + "_square", [P, G, D])
        self.spread = s.sb(tag + "_spread", [P, G])
        self.var = s.sb(tag + "_var", [P, G])
        self.root = s.sb(tag + "_root", [P, G])
        self.inv = s.sb(tag + "_inv", [P, G])
        self.centred_ready = s.sem(tag + "_centred_ready")
        self.squared = s.sem(tag + "_squared")
        self.var_ready = s.sem(tag + "_var_ready")
        self.rooted = s.sem(tag + "_rooted")

    def vector(self, dve, st, g, rows, x, out):
        v, R = self.nc.vector, slice(0, rows)
        st.did(v.tensor_reduce(self.total[R, :], x, AX, ALU.add))
        st.wait()
        st.did(v.tensor_scalar(self.mean[R, :], self.total[R, :], 1.0 / D, None, ALU.mult))
        st.wait()
        v.tensor_tensor(self.centred[R, :, :], x, spread(self.mean[R, :], D), ALU.subtract).then_inc(
            self.centred_ready, 1)
        wait(dve, self.squared, g + 1)
        st.did(v.tensor_reduce(self.spread[R, :], self.square[R, :, :], AX, ALU.add))
        st.wait()
        v.tensor_scalar(self.var[R, :], self.spread[R, :], 1.0 / D, EPS, ALU.mult, ALU.add).then_inc(
            self.var_ready, 1)
        wait(dve, self.rooted, g + 1)
        st.did(v.reciprocal(self.inv[R, :], self.root[R, :]))
        st.wait()
        last = v.tensor_tensor(out, self.centred[R, :, :], spread(self.inv[R, :], D), ALU.mult)
        self.n = 4
        return last

    def scalar(self, act, g, rows):
        R = slice(0, rows)
        wait(act, self.centred_ready, g + 1)
        self.nc.scalar.activation(self.square[R, :, :], self.centred[R, :, :], ACT.Square).then_inc(self.squared, 1)
        wait(act, self.var_ready, g + 1)
        self.nc.scalar.activation(self.root[R, :], self.var[R, :], ACT.Sqrt).then_inc(self.rooted, 1)


NORM_STEPS = 4


def turn_and_multiply(nc, c, pe, s_, g, rows, x, x_ready, weight, bias, units_done):
    R = slice(0, rows)
    A = 3
    for k in range(UNITS):
        q = UNITS * g + k
        if k == 0:
            hold(pe, x_ready, g + 1, s_["pe_passed"])
        hold(pe, s_["turned_copied"], q, s_["pe_passed"])
        for t in range(SUB):
            bank, o = (0, t) if t < A else (1, t - A)
            last = nc.tensor.transpose(s_["p_x"][0:D, bank, o * rows:(o + 1) * rows], x[R, SUB * k + t, 0:D],
                                       c["ident"][R, R])
        last.then_inc(s_["turned"], 1)
        wait(pe, s_["turned_copied"], q + 1)
        wait(pe, units_done, q - 1)
        p_y = s_["p_y"][(s_["b"] + k) % 2]
        for t in range(SUB):
            last = nc.tensor.matmul(p_y[R, t * D:(t + 1) * D], s_["xT"][k % 2][:, t * rows:(t + 1) * rows],
                                    weight[:, :], start=True, stop=(bias is None))
            if bias is not None:
                last = nc.tensor.matmul(p_y[R, t * D:(t + 1) * D], c["ones"][0:1, R], bias[:, :], start=False,
                                        stop=True)
        last.then_inc(s_["multiplied"], 1)


def turn_copies(nc, act, s_, g, rows):
    A, B = 3, SUB - 3
    for k in range(UNITS):
        q = UNITS * g + k
        wait(act, s_["turned"], q + 1)
        wait(act, s_["multiplied"], q - 1)
        xT = s_["xT"][k % 2]
        nc.scalar.activation(xT[:, 0:A * rows], s_["p_x"][0:D, 0, 0:A * rows], ACT.Copy)
        nc.scalar.activation(xT[:, A * rows:SUB * rows], s_["p_x"][0:D, 1, 0:B * rows],
                             ACT.Copy).then_inc(s_["turned_copied"], 1)


def turn_memory(s):
    s_ = dict(p_x=s.ps([P, 2, 512]), p_y=[s.ps([P, 512]) for i in range(2)],
              xT=[s.sb(f"xT{i}", [D, SUB * P]) for i in range(2)])
    for x in ("turned", "turned_copied", "multiplied", "pe_passed"):
        s_[x] = s.sem(x)
    return s_


def nodes0(nc, c, d):
    W = D + 1
    with ExitStack() as ctx:
        s = Scope(nc, ctx, "n0")
        sa = [s.sb(f"sa{b}", [P, G * W]) for b in range(2)]
        sb_ = [s.sb(f"sb{b}", [P, G * W]) for b in range(2)]
        x = [s.sb(f"x{b}", [P, G, D]) for b in range(2)]
        z = [s.sb(f"z{b}", [P, G], I32) for b in range(2)]
        mult = [s.sb(f"mult{b}", [P, G]) for b in range(2)]
        total = s.sb("total", [P, G, W])
        deg = [s.sb(f"deg{b}", [P, G]) for b in range(2)]
        dm, root, cj, alone = (s.sb(n, [P, G]) for n in ("dm", "root", "cj", "alone"))
        own = s.sb("own", [P, G, D])
        h = [s.sb(f"h{b}", [P, G, D]) for b in range(2)]
        y = s.sb("y", [P, G, D])
        row = [s.sb(f"row{b}", [P, G, D + 2]) for b in range(2)]
        norm = Norm(s, nc, "norm")
        s_ = turn_memory(s)
        loaded, stored = s.sems("loaded", 2), s.sems("stored", 2)
        stepped, dm_ready, rooted, h_ready, y_ready, built = (
            s.sem(n) for n in ("stepped", "dm_ready", "rooted", "h_ready", "y_ready", "built"))
        block = ctx.enter_context(nc.Block())

        @block.sync
        def _(sp):
            def body(u, b, rows):
                g = 2 * u + b
                R = slice(0, rows)
                wait(sp, built, g - 1)
                for dst, src, w in ((sa[b][R, :], d["sum0a"], W), (sb_[b][R, :], d["sum0b"], W),
                                    (x[b][R, :, :].rearrange("p t c -> p (t c)"), d["x"], D), (z[b][R, :], d["z"], 1),
                                    (mult[b][R, :], d["mult"], 1)):
                    sp.dma_start(dst, group_rows(src, g, rows, w)).then_inc(loaded[b], 16)
            over_groups(sp, body)

        @block.vector
        def _(dve):
            v = nc.vector

            def body(u, b, rows):
                g = 2 * u + b
                R = slice(0, rows)
                st = Steps(dve, stepped, 8 + NORM_STEPS, g)
                wait(dve, loaded[b], 80 * (u + 1))
                st.did(v.tensor_tensor(total[R, :, :].rearrange("p t c -> p (t c)"), sa[b][R, :], sb_[b][R, :], ALU.add))
                st.wait()
                v.tensor_scalar_max(dm[R, :], total[R, :, D], 1.0).then_inc(dm_ready, 1)
                wait(dve, stored[b], 32 * u)
                st.did(v.tensor_copy(deg[b][R, :], total[R, :, D]))
                st.did(v.tensor_scalar(alone[R, :], total[R, :, D], 0.0, None, ALU.is_equal))
                st.did(v.tensor_copy(row[b][R, :, D + 1], z[b][R, :]))
                st.did(v.tensor_copy(row[b][R, :, D], mult[b][R, :]))
                st.wait()
                st.did(v.tensor_tensor(own[R, :, :], x[b][R, :, :], spread(alone[R, :], D), ALU.mult))
                wait(dve, rooted, g + 1)
                st.did(v.reciprocal(cj[R, :], root[R, :]))
                st.wait()
                st.did(v.tensor_tensor(h[b][R, :, :], total[R, :, 0:D], spread(cj[R, :], D), ALU.mult))
                st.wait()
                v.tensor_tensor(h[b][R, :, :], h[b][R, :, :], own[R, :, :], ALU.add).then_inc(h_ready, 1)
                for k in range(UNITS):
                    q = UNITS * g + k
                    cols = slice(SUB * k, SUB * (k + 1))
                    wait(dve, s_["multiplied"], q + 1)
                    v.scalar_tensor_tensor(y[R, cols, :], s_["p_y"][(b + k) % 2][R, 0:SUB * D].rearrange(
                        "p (t c) -> p t c", t=SUB), 0.0, x[b][R, cols, :], ALU.max, ALU.add).then_inc(y_ready, 1)
                wait(dve, y_ready, UNITS * (g + 1))
                norm.vector(dve, st, g, rows, y[R, :, :], row[b][R, :, 0:D]).then_inc(built, 1)
                st.end()
            over_groups(dve, body)

        @block.tensor
        def _(pe):
            def body(u, b, rows):
                g = 2 * u + b
                s_["b"] = b
                turn_and_multiply(nc, c, pe, s_, g, rows, h[b], h_ready, c["w0"], c["b0"], y_ready)
            over_groups(pe, body)

        @block.scalar
        def _(act):
            def body(u, b, rows):
                g = 2 * u + b
                R = slice(0, rows)
                wait(act, dm_ready, g + 1)
                nc.scalar.activation(root[R, :], dm[R, :], ACT.Sqrt).then_inc(rooted, 1)
                turn_copies(nc, act, s_, g, rows)
                norm.scalar(act, g, rows)
                wait(act, built, g + 1)
                act.dma_start(group_rows(d["table1"], g, rows, D + 2),
                              row[b][R, :, :].rearrange("p t c -> p (t c)")).then_inc(stored[b], 16)
                act.dma_start(group_rows(d["indeg"], g, rows), deg[b][R, :]).then_inc(stored[b], 16)
            over_groups(act, body)
            for b in range(2):
                act.wait_ge(stored[b], 32 * (PAIRS + 1))


def nodes1(nc, c, d):
    W = D + 1
    with ExitStack() as ctx:
        s = Scope(nc, ctx, "n1")
        sa = [s.sb(f"sa{b}", [P, G * W]) for b in range(2)]
        sb_ = [s.sb(f"sb{b}", [P, G * W]) for b in range(2)]
        x = [s.sb(f"x{b}", [P, G, D + 2]) for b in range(2)]
        total = s.sb("total", [P, G, W])
        share = s.sb("share", [P, G])
        y = s.sb("y", [P, G, D])
        y2 = s.sb("y2", [P, G, D])
        out = [s.sb(f"out{b}", [P, G, D]) for b in range(2)]
        norm, norm2 = Norm(s, nc, "norm"), Norm(s, nc, "norm2")
        loaded, stored = s.sems("loaded", 2), s.sems("stored", 2)
        stepped, built = s.sem("stepped"), s.sem("built")
        block = ctx.enter_context(nc.Block())

        @block.sync
        def _(sp):
            def body(u, b, rows):
                g = 2 * u + b
                R = slice(0, rows)
                wait(sp, built, g - 1)
                for dst, src, w in ((sa[b][R, :], d["sum1a"], W), (sb_[b][R, :], d["sum1b"], W),
                                    (x[b][R, :, :].rearrange("p t c -> p (t c)"), d["table1"], D + 2)):
                    sp.dma_start(dst, group_rows(src, g, rows, w)).then_inc(loaded[b], 16)
            over_groups(sp, body)

        @block.vector
        def _(dve):
            v = nc.vector

            def body(u, b, rows):
                g = 2 * u + b
                R = slice(0, rows)
                st = Steps(dve, stepped, 9 + 2 * NORM_STEPS, g)
                wait(dve, loaded[b], 48 * (u + 1))
                st.did(v.tensor_tensor(total[R, :, :].rearrange("p t c -> p (t c)"), sa[b][R, :], sb_[b][R, :], ALU.add))
                st.wait()
                st.did(v.tensor_scalar_max(share[R, :], total[R, :, D], 1e-8))
                st.wait()
                st.did(v.reciprocal(share[R, :], share[R, :]))
                st.wait()
                st.did(v.tensor_tensor(y[R, :, :], total[R, :, 0:D], spread(share[R, :], D), ALU.mult))
                st.wait()
                st.did(v.tensor_tensor(y[R, :, :], y[R, :, :], x[b][R, :, 0:D], ALU.add))
                st.wait()
                st.did(norm.vector(dve, st, g, rows, y[R, :, :], y2[R, :, :]))
                st.wait()
                st.did(v.tensor_tensor(y[R, :, :], y2[R, :, :], along(c["gamma1"][R, :], G), ALU.mult))
                st.wait()
                st.did(v.tensor_tensor(y2[R, :, :], x[b][R, :, 0:D], along(c["beta1"][R, :], G), ALU.add))
                st.wait()
                st.did(v.tensor_tensor(y[R, :, :], y[R, :, :], y2[R, :, :], ALU.add))
                st.wait()
                wait(dve, stored[b], 16 * u)
                norm2.vector(dve, st, g, rows, y[R, :, :], out[b][R, :, :]).then_inc(built, 1)
                st.end()
            over_groups(dve, body)

        @block.scalar
        def _(act):
            def body(u, b, rows):
                g = 2 * u + b
                norm.scalar(act, g, rows)
                norm2.scalar(act, g, rows)
                wait(act, built, g + 1)
                act.dma_start(group_rows(d["table2"], g, rows, D),
                              out[b][0:rows, :, :].rearrange("p t c -> p (t c)")).then_inc(stored[b], 16)
            over_groups(act, body)
            for b in range(2):
                act.wait_ge(stored[b], 16 * (PAIRS + 1))


def nodes2(nc, c, d):
    with ExitStack() as ctx:
        s = Scope(nc, ctx, "n2")
        sa = [s.sb(f"sa{b}", [P, G, D]) for b in range(2)]
        sb_ = [s.sb(f"sb{b}", [P, G, D]) for b in range(2)]
        x = [s.sb(f"x{b}", [P, G, D]) for b in range(2)]
        deg = [s.sb(f"deg{b}", [P, G]) for b in range(2)]
        y = s.sb("y", [P, G, D])
        dm, root, dinv = (s.sb(n, [P, G]) for n in ("dm", "root", "dinv"))
        out = [s.sb(f"out{b}", [P, G, D]) for b in range(2)]
        row = [s.sb(f"row{b}", [P, G, D]) for b in range(2)]
        norm = Norm(s, nc, "norm")
        loaded, stored = s.sems("loaded", 2), s.sems("stored", 2)
        stepped, dm_ready, rooted, built = (s.sem(n) for n in ("stepped", "dm_ready", "rooted", "built"))
        block = ctx.enter_context(nc.Block())

        @block.sync
        def _(sp):
            def body(u, b, rows):
                g = 2 * u + b
                R = slice(0, rows)
                wait(sp, built, g - 1)
                for dst, src in ((sa[b], d["sum2a"]), (sb_[b], d["sum2b"]), (x[b], d["table2"])):
                    sp.dma_start(dst[R, :, :].rearrange("p t c -> p (t c)"), group_rows(src, g, rows, D)).then_inc(
                        loaded[b], 16)
                sp.dma_start(deg[b][R, :], group_rows(d["indeg"], g, rows)).then_inc(loaded[b], 16)
            over_groups(sp, body)

        @block.vector
        def _(dve):
            v = nc.vector

            def body(u, b, rows):
                g = 2 * u + b
                R = slice(0, rows)
                st = Steps(dve, stepped, 5 + NORM_STEPS, g)
                wait(dve, loaded[b], 64 * (u + 1))
                v.tensor_scalar_add(dm[R, :], deg[b][R, :], 1.0).then_inc(dm_ready, 1)
                st.did(v.tensor_tensor(y[R, :, :], sa[b][R, :, :], sb_[b][R, :, :], ALU.add))
                st.wait()
                st.did(v.tensor_tensor(y[R, :, :], y[R, :, :], along(c["rb2"][R, :], G), ALU.add))
                st.wait()
                st.did(v.scalar_tensor_tensor(y[R, :, :], y[R, :, :], 0.0, x[b][R, :, :], ALU.max, ALU.add))
                st.wait()
                wait(dve, stored[b], 32 * u)
                st.did(norm.vector(dve, st, g, rows, y[R, :, :], out[b][R, :, :]))
                wait(dve, rooted, g + 1)
                st.did(v.reciprocal(dinv[R, :], root[R, :]))
                st.wait()
                v.tensor_tensor(row[b][R, :, :], out[b][R, :, :], spread(dinv[R, :], D), ALU.mult).then_inc(built, 1)
                st.end()
            over_groups(dve, body)

        @block.scalar
        def _(act):
            def body(u, b, rows):
                g = 2 * u + b
                R = slice(0, rows)
                wait(act, dm_ready, g + 1)
                nc.scalar.activation(root[R, :], dm[R, :], ACT.Sqrt).then_inc(rooted, 1)
                norm.scalar(act, g, rows)
                wait(act, built, g + 1)
                for dst, src in ((d["x3"], out[b]), (d["table3"], row[b])):
                    act.dma_start(group_rows(dst, g, rows, D),
                                  src[R, :, :].rearrange("p t c -> p (t c)")).then_inc(stored[b], 16)
            over_groups(act, body)
            for b in range(2):
                act.wait_ge(stored[b], 32 * (PAIRS + 1))


def nodes3(nc, c, d, ally):
    with ExitStack() as ctx:
        s = Scope(nc, ctx, "n3")
        sa = [s.sb(f"sa{b}", [P, G, D]) for b in range(2)]
        sb_ = [s.sb(f"sb{b}", [P, G, D]) for b in range(2)]
        x = [s.sb(f"x{b}", [P, G, D]) for b in range(2)]
        deg = [s.sb(f"deg{b}", [P, G]) for b in range(2)]
        h = [s.sb(f"h{b}", [P, G, D]) for b in range(2)]
        dm, root, dinv = (s.sb(n, [P, G]) for n in ("dm", "root", "dinv"))
        s_ = turn_memory(s)
        loaded = s.sems("loaded", 2)
        stepped, dm_ready, rooted, h_ready, y_ready = (
            s.sem(n) for n in ("stepped", "dm_ready", "rooted", "h_ready", "y_ready"))
        block = ctx.enter_context(nc.Block())

        @block.sync
        def _(sp):
            def body(u, b, rows):
                g = 2 * u + b
                R = slice(0, rows)
                wait(sp, h_ready, g - 1)
                for dst, src in ((sa[b], d["sum3a"]), (sb_[b], d["sum3b"]), (x[b], d["table3"])):
                    sp.dma_start(dst[R, :, :].rearrange("p t c -> p (t c)"), group_rows(src, g, rows, D)).then_inc(
                        loaded[b], 16)
                sp.dma_start(deg[b][R, :], group_rows(d["indeg"], g, rows)).then_inc(loaded[b], 16)
            over_groups(sp, body)

        @block.vector
        def _(dve):
            v = nc.vector

            def body(u, b, rows):
                g = 2 * u + b
                R = slice(0, rows)
                st = Steps(dve, stepped, 3, g)
                wait(dve, loaded[b], 64 * (u + 1))
                v.tensor_scalar_add(dm[R, :], deg[b][R, :], 1.0).then_inc(dm_ready, 1)
                wait(dve, s_["multiplied"], UNITS * (g - 1))
                st.did(v.tensor_tensor(h[b][R, :, :], sa[b][R, :, :], sb_[b][R, :, :], ALU.add))
                st.wait()
                st.did(v.tensor_tensor(h[b][R, :, :], h[b][R, :, :], x[b][R, :, :], ALU.add))
                wait(dve, rooted, g + 1)
                st.did(v.reciprocal(dinv[R, :], root[R, :]))
                st.wait()
                v.tensor_tensor(h[b][R, :, :], h[b][R, :, :], spread(dinv[R, :], D), ALU.mult).then_inc(h_ready, 1)
                for k in range(UNITS):
                    q = UNITS * g + k
                    wait(dve, s_["multiplied"], q + 1)
                    v.tensor_tensor(ally[R, bass.ds(g * (G * D) + k * (SUB * D), SUB * D)].rearrange(
                        "p (t c) -> p t c", c=D),
                                    s_["p_y"][(b + k) % 2][R, 0:SUB * D].rearrange("p (t c) -> p t c", t=SUB),
                                    along(c["b3"][R, :], SUB), ALU.add).then_inc(y_ready, 1)
                st.end()
            over_groups(dve, body)

        @block.tensor
        def _(pe):
            def body(u, b, rows):
                g = 2 * u + b
                s_["b"] = b
                turn_and_multiply(nc, c, pe, s_, g, rows, h[b], h_ready, c["w3"], None, y_ready)
            over_groups(pe, body)

        @block.scalar
        def _(act):
            def body(u, b, rows):
                g = 2 * u + b
                R = slice(0, rows)
                wait(act, dm_ready, g + 1)
                nc.scalar.activation(root[R, :], dm[R, :], ACT.Sqrt).then_inc(rooted, 1)
                turn_copies(nc, act, s_, g, rows)
            over_groups(act, body)


def batch_statistics(nc, c, ally):
    CH = 15
    with ExitStack() as ctx:
        s = Scope(nc, ctx, "bn")
        part = s.sb("part", [P, 2, D])
        part2 = s.sb("part2", [P, CH + 1, D])
        square = [s.sb(f"square{k}", [P, G, D]) for k in range(2)]
        var, root, inv = (s.sb(n, [P, D]) for n in ("var", "root", "inv"))
        ps = s.ps([P, 512])
        stepped, parted, meaned, squared, reduced, vared, rooted = (
            s.sem(n) for n in ("stepped", "parted", "meaned", "squared", "reduced", "vared", "rooted"))
        centred = s.sem("centred")
        block = ctx.enter_context(nc.Block())
        chunks = [(P, k * G * D) for k in range(NG - 1)] + [(TAIL, (NG - 1) * G * D)]

        def chunk(k):
            rows, at = chunks[k]
            return ally[0:rows, at:at + G * D]

        def reduce_chunk(dve, k):
            rows = chunks[k][0]
            dve.wait_ge(squared, k + 1)
            nc.vector.tensor_reduce(part2[0:rows, k, :], square[k % 2][0:rows, :, :].rearrange("p t c -> p c t"), AX,
                                    ALU.add).then_inc(reduced, 1)

        @block.vector
        def _(dve):
            v = nc.vector
            main = (NG - 1) * G * D
            v.tensor_reduce(part[:, 0, :], ally[:, 0:main].rearrange("p (t c) -> p c t", c=D), AX,
                            ALU.add).then_inc(parted, 1)
            v.tensor_reduce(part[0:TAIL, 1, :], ally[0:TAIL, main:main + G * D].rearrange("p (t c) -> p c t", c=D),
                            AX, ALU.add).then_inc(parted, 1)
            dve.wait_ge(meaned, 1)
            v.tensor_scalar(c["mean"][:, :], ps[:, 0:D], 1.0 / N, None, ALU.mult).then_inc(stepped, 1)
            dve.wait_ge(stepped, 1)
            for k in range(NG):
                rows = chunks[k][0]
                y = chunk(k).rearrange("p (t c) -> p t c", c=D)
                v.tensor_tensor(y, y, along(c["mean"][0:rows, :], G), ALU.subtract).then_inc(centred, 1)
                if k:
                    reduce_chunk(dve, k - 1)
            reduce_chunk(dve, NG - 1)
            dve.wait_ge(vared, 1)
            v.tensor_scalar(var[:, :], ps[:, 64:64 + D], 1.0 / N, EPS, ALU.mult, ALU.add).then_inc(stepped, 1)
            dve.wait_ge(rooted, 1)
            v.reciprocal(inv[:, :], root[:, :]).then_inc(stepped, 1)
            dve.wait_ge(stepped, 3)
            v.tensor_tensor(c["scale3"][:, :], inv[:, :], c["gamma3"][:, :], ALU.mult).then_inc(stepped, 1)
            dve.wait_ge(stepped, 4)

        @block.scalar
        def _(act):
            for k in range(NG):
                rows = chunks[k][0]
                act.wait_ge(centred, k + 1)
                wait(act, reduced, k - 1)
                nc.scalar.activation(square[k % 2][0:rows, :, :].rearrange("p t c -> p (t c)"), chunk(k),
                                     ACT.Square).then_inc(squared, 1)
            act.wait_ge(stepped, 2)
            nc.scalar.activation(root[:, :], var[:, :], ACT.Sqrt).then_inc(rooted, 1)

        @block.tensor
        def _(pe):
            pe.wait_ge(parted, 2)
            nc.tensor.matmul(ps[:, 0:D], c["ones"][:, :], part[:, 0, :], start=True, stop=False)
            nc.tensor.matmul(ps[:, 0:D], c["ones"][0:TAIL, :], part[0:TAIL, 1, :], start=False,
                             stop=True).then_inc(meaned, 1)
            pe.wait_ge(reduced, NG)
            for k in range(NG):
                rows = chunks[k][0]
                last = nc.tensor.matmul(ps[:, 64:64 + D], c["ones"][0:rows, :], part2[0:rows, k, :],
                                        start=(k == 0), stop=(k == NG - 1))
            last.then_inc(vared, 1)


def finish(nc, c, d, ally):
    with ExitStack() as ctx:
        s = Scope(nc, ctx, "fin")
        x = [s.sb(f"x{b}", [P, G, D]) for b in range(2)]
        y = s.sb("y", [P, G, D])
        out = [s.sb(f"out{b}", [P, G, D]) for b in range(2)]
        norm = Norm(s, nc, "norm")
        loaded, stored = s.sems("loaded", 2), s.sems("stored", 2)
        stepped, built = s.sem("stepped"), s.sem("built")
        block = ctx.enter_context(nc.Block())

        @block.sync
        def _(sp):
            def body(u, b, rows):
                g = 2 * u + b
                wait(sp, built, g - 1)
                sp.dma_start(x[b][0:rows, :, :].rearrange("p t c -> p (t c)"),
                             group_rows(d["x3"], g, rows, D)).then_inc(loaded[b], 16)
            over_groups(sp, body)

        @block.vector
        def _(dve):
            v = nc.vector

            def body(u, b, rows):
                g = 2 * u + b
                R = slice(0, rows)
                st = Steps(dve, stepped, 3 + NORM_STEPS, g)
                st.did(v.tensor_tensor(y[R, :, :], ally[R, bass.ds(g * (G * D), G * D)].rearrange(
                    "p (t c) -> p t c", c=D), along(c["scale3"][R, :], G), ALU.mult))
                st.wait()
                st.did(v.tensor_tensor(y[R, :, :], y[R, :, :], along(c["beta3"][R, :], G), ALU.add))
                st.wait()
                wait(dve, loaded[b], 16 * (u + 1))
                st.did(v.scalar_tensor_tensor(y[R, :, :], y[R, :, :], 0.0, x[b][R, :, :], ALU.max, ALU.add))
                st.wait()
                wait(dve, stored[b], 16 * u)
                norm.vector(dve, st, g, rows, y[R, :, :], out[b][R, :, :]).then_inc(built, 1)
                st.end()
            over_groups(dve, body)

        @block.scalar
        def _(act):
            def body(u, b, rows):
                g = 2 * u + b
                norm.scalar(act, g, rows)
                wait(act, built, g + 1)
                act.dma_start(group_rows(d["out"], g, rows, D),
                              out[b][0:rows, :, :].rearrange("p t c -> p (t c)")).then_inc(stored[b], 16)
            over_groups(act, body)
            for b in range(2):
                act.wait_ge(stored[b], 16 * (PAIRS + 1))


def gnn_kernel(nc, d, upto=99):
    with ExitStack() as ctx:
        keep = Scope(nc, ctx, "keep")
        PSUM_OF[nc] = ctx.enter_context(nc.psum_tensor("psum", [P, 8, 512], F32))
        c = load_constants(nc, keep, d)
        ZEROS[nc] = c["zeros"]
        stages = [
            lambda: out_degree(nc, c, d, [d["sum0a"], d["sum0b"]]),
            lambda: first_table(nc, c, d),
            lambda: plain_edges(nc, c, d, "gcn", "table0", D + 2, ("sum0a", "sum0b"), D + 1,
                                (("sum1a", "sum1b"), D + 1), True),
            lambda: nodes0(nc, c, d),
            lambda: filter_edges(nc, c, d),
            lambda: nodes1(nc, c, d),
            lambda: relation_edges(nc, c, d),
            lambda: nodes2(nc, c, d),
            lambda: plain_edges(nc, c, d, "last", "table3", D, ("sum3a", "sum3b"), D, None, False),
        ]
        for f in stages[:upto]:
            f()
        if upto >= 99:
            ally = keep.sb("ally", [P, NG * G * D])
            nodes3(nc, c, d, ally)
            batch_statistics(nc, c, ally)
            finish(nc, c, d, ally)


SCRATCH_ROWS = P * 49 * 8


def declare(nc, arrays):
    dt = {"float32": F32, "int32": I32}
    d = {}
    for name, a in arrays.items():
        d[name] = nc.dram_tensor(f"in_{name}", a.shape, dt[a.dtype.name], kind="ExternalInput").ap()
    scratch = dict(outdeg=(RHIGH * RLOW,), indeg=(N,), srctype=(N,), table0=(N, D + 2), table1=(N, D + 2),
                   table2=(N, D), table3=(N, D), x3=(N, D))
    for i, w in enumerate((D + 1, D + 1, D, D)):
        scratch[f"sum{i}a"] = scratch[f"sum{i}b"] = (SCRATCH_ROWS, w)
    for name, shape in scratch.items():
        d[name] = nc.dram_tensor(f"tmp_{name}", shape, F32, kind="Internal").ap()
    d["out"] = nc.dram_tensor("out_0", (N, D), F32, kind="ExternalOutput").ap()
    return d


def lay_out(inputs):
    import numpy as np

    def tile_major(a):
        main = a[:TAIL0].reshape(NG - 1, P, G).transpose(0, 2, 1).reshape(-1)
        tail = a[TAIL0:].reshape(TAIL, G).T.reshape(-1)
        return np.concatenate([main, tail])

    i = {k: np.asarray(v) for k, v in inputs.items()}
    attr = i["edge_attr_40"]
    a = dict(
        x=i["x"], src=i["src"], dst=i["dst"], src_line=tile_major(i["src"]), dst_line=tile_major(i["dst"]),
        attr=attr[:TAIL0].reshape(NG - 1, P, G, NA).transpose(0, 3, 2, 1).reshape((NG - 1) * NA, FULL),
        attr_tail=attr[TAIL0:].reshape(TAIL, G, NA).transpose(2, 1, 0).reshape(NA, TAIL * G),
        rel=i["edge_type_8"], dist=i["edge_weight"], norm=i["edge_weight1"].reshape(-1), z=i["node_type_119"],
        mult=i["node_vec"], w0=i["L0_gnn_W"].T, b0=i["L0_gnn_b"], f1=i["L1_gnn_W1"].T, f1b=i["L1_gnn_b1"],
        f2=i["L1_gnn_W2"].T, f2b=i["L1_gnn_b2"], embT=i["L1_gnn_emb"].T, adT=i["L1_gnn_adaptW"].T,
        gamma1=i["L1_gnn_gamma"], beta1=i["L1_gnn_beta"], r1=i["L2_gnn_weight1"], r2=i["L2_gnn_weight2"],
        rb1=i["L2_gnn_bias1"], rb2=i["L2_gnn_bias2"], w3=i["L3_gnn_W"], b3=i["L3_gnn_b"],
        gamma3=i["L3_gnn_gamma"], beta3=i["L3_gnn_beta"])
    return {k: np.ascontiguousarray(v) for k, v in a.items()}


def kernel(**inputs):
    import concourse.bacc as bacc
    from concourse.bass_utils import run_bass_kernel_spmd

    arrays = lay_out(inputs)
    nc = bacc.Bacc("TRN2", target_bir_lowering=False, num_devices=1)
    d = declare(nc, arrays)
    gnn_kernel(nc, d)
    r = run_bass_kernel_spmd(nc, [{f"in_{k}": v for k, v in arrays.items()}], core_ids=[0])
    return r.results[0]["out_0"]
```

```python
from contextlib import ExitStack

import concourse.bass as bass
from concourse import mybir

P = 128
N = 50000
D = 48
G = 25
SUB = 5
UNITS = G // SUB
FULL = P * G
NG = -(-N // FULL)
TAIL0 = (NG - 1) * FULL
TAIL = (N - TAIL0) // G
PAIRS = NG // 2 - 1
SLOTS = SUB
LAG = 3
NR = 8
RBITS = 9
RLOW = 1 << RBITS
RHIGH = -(-N // RLOW)
NZ = 119
NE = 32
NA = 40
EPS = 1e-5
CUTOFF = 6.0
PI = 3.141592653589793
FAR = -1e30
KX = D + NR + 1
KS = KX + D
CHUNKS = NR * D // P
assert TAIL * G == N - TAIL0 and NG % 2 == 0 and SUB * UNITS == G

F32 = mybir.dt.float32
F16 = mybir.dt.float16
BF16 = mybir.dt.bfloat16
I32 = mybir.dt.int32
ALU = mybir.AluOpType
ACT = mybir.ActivationFunctionType
AX = mybir.AxisListType.X


def over_groups(eng, body):
    body(0, 0, P)
    body(0, 1, P)
    with eng.Fori(1, PAIRS) as u:
        body(u, 0, P)
        body(u, 1, P)
    body(PAIRS, 0, P)
    body(PAIRS, 1, TAIL)


def unit_before(u, b, rows, k):
    if k:
        return u, b, rows, k - 1
    if isinstance(u, int) and u == 0 and b == 0:
        return None
    return u if b else u - 1, 1 - b, P, UNITS - 1


def over_units(eng, early, late, begin=None):
    def body(u, b, rows):
        if begin is not None:
            begin(u, b, rows)
        for k in range(UNITS):
            early(u, b, rows, k)
            before = unit_before(u, b, rows, k)
            if before:
                late(*before)
    over_groups(eng, body)
    late(PAIRS, 1, TAIL, UNITS - 1)


def over_groups_late(eng, early, late):
    def body(u, b, rows):
        early(u, b, rows)
        if not (isinstance(u, int) and u == 0 and b == 0):
            late(u if b else u - 1, 1 - b, P)
    over_groups(eng, body)
    late(PAIRS, 1, TAIL)


def wait(eng, sem, value):
    if not (isinstance(value, int) and value <= 0):
        eng.wait_ge(sem, value)


def hold(eng, sem, value, passed):
    if not (isinstance(value, int) and value <= 0):
        eng.wait_ge(sem, value)
        eng.sem_inc(passed, 1)


def group_rows(dram, g, rows, width=1):
    part = dram[bass.ds(g * FULL, FULL)] if rows == P else dram[TAIL0:N]
    if width == 1 and len(dram.shape) == 1:
        return part.rearrange("(p t) -> p t", t=G)
    return part.rearrange("(p t) c -> p (t c)", t=G)


def group_line(dram, g, rows):
    part = dram[bass.ds(g * FULL, FULL)] if rows == P else dram[TAIL0:N]
    return part.partition_broadcast(rows)


class Steps:

    def __init__(self, eng, sem, per, g):
        self.eng, self.sem, self.per, self.base, self.n = eng, sem, per, g * per, 0

    def did(self, ins):
        ins.then_inc(self.sem, 1)
        self.n += 1

    def wait(self):
        wait(self.eng, self.sem, self.base + self.n)

    def end(self):
        assert self.n == self.per, (self.n, self.per)


def spread(ap, n):
    return ap.unsqueeze(2).broadcast_to([ap.shape[0], ap.shape[1], n])


def along(ap, t):
    return ap.unsqueeze(1).broadcast_to([ap.shape[0], t, ap.shape[1]])


PSUM_OF = {}


class Scope:

    def __init__(self, nc, ctx, tag):
        self.nc, self.ctx, self.tag, self.bank, self.taken = nc, ctx, tag, 0, []
        ctx.callback(self.release)

    def sb(self, name, shape, dt=F32):
        return self.ctx.enter_context(self.nc.sbuf_tensor(f"{self.tag}_{name}", shape, dt))

    def ps(self, shape):
        n = shape[1] if len(shape) == 3 else 1
        part = PSUM_OF[self.nc][0:shape[0], self.bank:self.bank + n, 0:shape[-1]]
        self.bank += n
        assert self.bank <= 8
        return part if len(shape) == 3 else part.rearrange("p b c -> p (b c)")

    def sem(self, name):
        self.taken.append(self.nc.alloc_semaphore(f"{self.tag}_{name}"))
        return self.taken[-1]

    def release(self):
        if self.taken:
            self.nc.clear_and_free_semaphores(self.taken)
            self.nc.all_engine_barrier()

    def sems(self, name, n):
        return [self.sem(f"{name}{i}") for i in range(n)]



def load_constants(nc, keep, d):
    c = {}
    spec = dict(ident=[P, P], before=[P, P], ones=[P, P], spare=[P, 1], w0=[D + 1, D], f1=[NA, D],
                f1b=[D, 1], f2=[D + 1, D], embT=[NE, NZ], adT=[NE, NE], ejT=[NE, NZ], pairs=[NZ, NZ],
                gamma1=[P, D], beta1=[P, D], r1=[KS, NR * D], rest=[KS, NR * D], r2=[P, CHUNKS, D], rb2=[P, D],
                w3=[D, D], b3=[P, D], gamma3=[P, D], beta3=[P, D], farm=[NR, NR * D], zline=[P, NZ],
                rline=[P, NR], mean=[P, D], scale3=[P, D])
    for name, shape in spec.items():
        c[name] = keep.sb(name, shape)
    c["lows"] = keep.sb("lows", [P, RLOW], F16)
    c["highs"] = keep.sb("highs", [P, RHIGH], F16)
    c["identb"] = keep.sb("identb", [P, P], BF16)
    for name in ("r1a", "r1b", "r1c"):
        c[name] = keep.sb(name, [KS, NR * D], BF16)
    c["zeros"] = keep.sb("zeros", [P, 49 * 49])
    with ExitStack() as ctx:
        s = Scope(nc, ctx, "const")
        landed, shaped, made, multiplied, copied = (s.sem(x) for x in
                                                    ("landed", "shaped", "made", "multiplied", "copied"))
        placed, split = s.sem("placed"), s.sem("split")
        pt = s.ps([P, 512])
        block = ctx.enter_context(nc.Block())
        loads = [("f1", d["f1"]), ("f1b", d["f1b"].unsqueeze(1)),
                 ("embT", d["embT"]), ("adT", d["adT"]),
                 ("gamma1", d["gamma1"].partition_broadcast(P)), ("beta1", d["beta1"].partition_broadcast(P)),
                 ("rb2", d["rb2"].partition_broadcast(P)), ("w3", d["w3"]),
                 ("b3", d["b3"].partition_broadcast(P)), ("gamma3", d["gamma3"].partition_broadcast(P)),
                 ("beta3", d["beta3"].partition_broadcast(P))]

        N_LOADS = len(loads) + 5 + 3 * NR

        @block.sync
        def _(sp):
            for name, src in loads:
                sp.dma_start(c[name][:, :], src).then_inc(landed, 16)
            for name in ("w0", "f2"):
                sp.dma_start(c[name][0:D, :], d[name]).then_inc(landed, 16)
                sp.dma_start(c[name][D:D + 1, :], d[name + "b"].unsqueeze(0)).then_inc(landed, 16)
            sp.dma_start(c["r2"][:, :, :], d["r2"].rearrange("r j o -> (r j) o").rearrange("(q a) o -> a q o", a=P)).then_inc(landed, 16)
            for r in range(NR):
                sp.dma_start(c["r1"][0:D, r * D:(r + 1) * D], d["r1"][r]).then_inc(landed, 16)
                sp.dma_start(c["r1"][KX:KS, r * D:(r + 1) * D], d["r1"][r]).then_inc(landed, 16)
                sp.dma_start(c["r1"][KX - 1:KX, r * D:(r + 1) * D],
                             d["rb1"].unsqueeze(0)).then_inc(landed, 16)
            sp.wait_ge(shaped, 7)
            sp.dma_start(c["r1"][D:D + NR, :], c["farm"][:, :]).then_inc(placed, 16)
            sp.wait_ge(split, 5)
            sp.dma_start(c["r1c"][KX:KS, :], c["r1a"][KX:KS, :]).then_inc(placed, 16)
            sp.wait_ge(placed, 32)

        @block.vector
        def _(dve):
            v = nc.vector
            dve.wait_ge(landed, 16 * N_LOADS)
            dve.wait_ge(placed, 16)
            v.tensor_copy(c["r1a"][:, :], c["r1"][:, :]).then_inc(split, 1)
            dve.wait_ge(split, 1)
            v.tensor_tensor(c["rest"][:, :], c["r1"][:, :], c["r1a"][:, :], ALU.subtract).then_inc(split, 1)
            dve.wait_ge(split, 2)
            v.tensor_copy(c["r1b"][:, :], c["rest"][:, :]).then_inc(split, 1)
            dve.wait_ge(split, 3)
            v.tensor_tensor(c["r1c"][:, :], c["rest"][:, :], c["r1b"][:, :], ALU.subtract).then_inc(split, 1)
            dve.wait_ge(shaped, 6)
            v.tensor_copy(c["identb"][:, :], c["ident"][:, :]).then_inc(split, 1)

        @block.gpsimd
        def _(pool):
            g = nc.gpsimd
            g.memset(c["ones"][:, :], 1.0).then_inc(made, 1)
            g.memset(c["zeros"][:, :], 0.0).then_inc(made, 1)
            g.memset(c["farm"][:, :], 0.0).then_inc(made, 1)
            g.iota(c["spare"][:, :], [[1, 1]], base=N, channel_multiplier=1,
                   allow_small_or_imprecise_dtypes=True).then_inc(shaped, 1)
            g.iota(c["lows"][:, :], [[1, RLOW]], base=0, channel_multiplier=0,
                   allow_small_or_imprecise_dtypes=True).then_inc(shaped, 1)
            g.iota(c["highs"][:, :], [[1, RHIGH]], base=0, channel_multiplier=0,
                   allow_small_or_imprecise_dtypes=True).then_inc(shaped, 1)
            g.iota(c["zline"][:, :], [[1, NZ]], base=0, channel_multiplier=0,
                   allow_small_or_imprecise_dtypes=True).then_inc(shaped, 1)
            g.iota(c["rline"][:, :], [[1, NR]], base=0, channel_multiplier=0,
                   allow_small_or_imprecise_dtypes=True).then_inc(shaped, 1)
            pool.wait_ge(made, 3)
            g.affine_select(out=c["ident"][:, :], in_=c["zeros"][:, 0:P], compare_op=ALU.not_equal, fill=1.0,
                            base=0, pattern=[[-1, P]], channel_multiplier=1).then_inc(shaped, 1)
            g.affine_select(out=c["farm"][:, :].rearrange("p (r j) -> p r j", r=NR),
                            in_=c["farm"][:, :].rearrange("p (r j) -> p r j", r=NR),
                            compare_op=ALU.not_equal, fill=FAR, base=0, pattern=[[-1, NR], [0, D]],
                            channel_multiplier=1).then_inc(shaped, 1)
            g.affine_select(out=c["before"][:, :], in_=c["ones"][:, :], compare_op=ALU.is_gt, fill=0.0,
                            base=0, pattern=[[-1, P]], channel_multiplier=1).then_inc(shaped, 1)
            pool.wait_ge(shaped, 8)

        @block.tensor
        def _(pe):
            pe.wait_ge(landed, 16 * N_LOADS)
            nc.tensor.matmul(pt[0:NE, 0:NZ], c["adT"][:, :], c["embT"][:, :], start=True,
                             stop=True).then_inc(multiplied, 1)
            pe.wait_ge(copied, 1)
            nc.tensor.matmul(pt[0:NZ, 128:128 + NZ], c["ejT"][:, :], c["embT"][:, :], start=True,
                             stop=True).then_inc(multiplied, 1)

        @block.scalar
        def _(act):
            act.wait_ge(multiplied, 1)
            nc.scalar.activation(c["ejT"][:, :], pt[0:NE, 0:NZ], ACT.Copy).then_inc(copied, 1)
            act.wait_ge(multiplied, 2)
            nc.scalar.activation(c["pairs"][:, :], pt[0:NZ, 128:128 + NZ], ACT.Copy).then_inc(copied, 1)
            act.wait_ge(copied, 2)
    return c



def clear_sums(nc, eng, sums, width, cleared):
    n = 0
    for copy in sums:
        rows = copy.rearrange("(k p q) c -> k p (q c)", p=P, q=49)
        for k in range(rows.shape[0]):
            eng.dma_start(rows[k], ZEROS[nc][:, 0:49 * width]).then_inc(cleared, 16)
            n += 16
    return n


ZEROS = {}


def out_degree(nc, c, d, sums0):
    with ExitStack() as ctx:
        s = Scope(nc, ctx, "deg")
        key = [s.sb(f"key{b}", [P, G], I32) for b in range(2)]
        part = s.sb("part", [P, 2, G], I32)
        partf = [s.sb(f"partf{b}", [P, 2, G]) for b in range(2)]
        low = [s.sb(f"low{k}", [P, SUB, RLOW], BF16) for k in range(2)]
        high = [s.sb(f"high{k}", [P, SUB, RHIGH], BF16) for k in range(2)]
        count = s.sb("count", [RHIGH, RLOW])
        ps = s.ps([RHIGH, RLOW])
        loaded = s.sems("loaded", 2)
        stepped, hot, used, counted, copied, stored, cleared = (
            s.sem(x) for x in ("stepped", "hot", "used", "counted", "copied", "stored", "cleared"))
        block = ctx.enter_context(nc.Block())

        @block.sync
        def _(sp):
            def body(u, b, rows):
                g = 2 * u + b
                wait(sp, stepped, 4 * (g - 1))
                sp.dma_start(key[b][0:rows, :], group_rows(d["src"], g, rows)).then_inc(loaded[b], 16)
            over_groups(sp, body)
            sp.wait_ge(copied, 1)
            sp.dma_start(d["outdeg"].rearrange("(h l) -> h l", l=RLOW), count[:, :]).then_inc(stored, 16)
            sp.wait_ge(stored, 16)

        @block.scalar
        def _(act):
            n = clear_sums(nc, act, sums0, 49, cleared)
            act.wait_ge(cleared, n)

        @block.vector
        def _(dve):
            v = nc.vector

            def body(u, b, rows):
                g = 2 * u + b
                st = Steps(dve, stepped, 4, g)
                wait(dve, loaded[b], 16 * (u + 1))
                st.did(v.tensor_scalar(part[0:rows, 0, :], key[b][0:rows, :], RBITS, None,
                                       ALU.logical_shift_right))
                st.did(v.tensor_scalar(part[0:rows, 1, :], key[b][0:rows, :], RLOW - 1, None, ALU.bitwise_and))
                st.wait()
                wait(dve, used, 5 * (g - 1))
                st.did(v.tensor_copy(partf[b][0:rows, 0, :], part[0:rows, 0, :]))
                st.did(v.tensor_copy(partf[b][0:rows, 1, :], part[0:rows, 1, :]))
                st.wait()
                for k in range(UNITS):
                    r = (b + k) % 2
                    wait(dve, used, 5 * g + k - 1)
                    for t in range(SUB):
                        col = SUB * k + t
                        v.tensor_scalar(high[r][0:rows, t, :], c["highs"][0:rows, :],
                                        partf[b][0:rows, 0, col:col + 1], None, ALU.is_equal)
                        last = v.tensor_scalar(low[r][0:rows, t, :], c["lows"][0:rows, :],
                                               partf[b][0:rows, 1, col:col + 1], None, ALU.is_equal)
                    last.then_inc(hot, 1)
                st.end()
            over_groups(dve, body)
            dve.wait_ge(counted, 1)
            v.tensor_copy(count[:, :], ps[:, :]).then_inc(copied, 1)

        @block.tensor
        def _(pe):
            def body(u, b, rows):
                g = 2 * u + b
                for k in range(UNITS):
                    r = (b + k) % 2
                    wait(pe, hot, 5 * g + k + 1)
                    for t in range(SUB):
                        first = isinstance(u, int) and u == 0 and b == 0 and k == 0 and t == 0
                        end = rows == TAIL and k == UNITS - 1 and t == SUB - 1
                        last = nc.tensor.matmul(ps[:, :], high[r][0:rows, t, :], low[r][0:rows, t, :],
                                                start=first, stop=end)
                    last.then_inc(used, 1)
            over_groups(pe, body)
            pe.wait_ge(used, UNITS * NG)
            pe.sem_inc(counted, 1)


def first_table(nc, c, d):
    with ExitStack() as ctx:
        s = Scope(nc, ctx, "t0")
        x = [s.sb(f"x{b}", [P, G * D]) for b in range(2)]
        deg = [s.sb(f"deg{b}", [P, G]) for b in range(2)]
        z = [s.sb(f"z{b}", [P, G], I32) for b in range(2)]
        row = [s.sb(f"row{b}", [P, G, D + 2]) for b in range(2)]
        dm = s.sb("dm", [P, G])
        root = s.sb("root", [P, G])
        ci = s.sb("ci", [P, G])
        loaded, stored = s.sems("loaded", 2), s.sems("stored", 2)
        stepped, rooted, built = s.sem("stepped"), s.sem("rooted"), s.sem("built")
        block = ctx.enter_context(nc.Block())

        @block.sync
        def _(sp):
            def body(u, b, rows):
                g = 2 * u + b
                wait(sp, built, g - 1)
                sp.dma_start(x[b][0:rows, :], group_rows(d["x"], g, rows, D)).then_inc(loaded[b], 16)
                sp.dma_start(deg[b][0:rows, :], group_rows(d["outdeg"], g, rows)).then_inc(loaded[b], 16)
                sp.dma_start(z[b][0:rows, :], group_rows(d["z"], g, rows)).then_inc(loaded[b], 16)
            over_groups(sp, body)

        @block.vector
        def _(dve):
            v = nc.vector

            def body(u, b, rows):
                g = 2 * u + b
                st = Steps(dve, stepped, 4, g)
                R = slice(0, rows)
                wait(dve, loaded[b], 48 * (u + 1))
                st.did(v.tensor_scalar_max(dm[R, :], deg[b][R, :], 1.0))
                wait(dve, stored[b], 16 * u)
                st.did(v.tensor_copy(row[b][R, :, D + 1], z[b][R, :]))
                st.did(v.tensor_copy(row[b][R, :, D], c["ones"][R, 0:G]))
                wait(dve, rooted, g + 1)
                st.did(v.reciprocal(ci[R, :], root[R, :]))
                st.wait()
                v.tensor_tensor(row[b][R, :, 0:D], x[b][R, :].rearrange("p (t c) -> p t c", c=D),
                                spread(ci[R, :], D), ALU.mult).then_inc(built, 1)
                st.end()
            over_groups(dve, body)

        @block.scalar
        def _(act):
            def body(u, b, rows):
                g = 2 * u + b
                R = slice(0, rows)
                wait(act, stepped, 4 * g + 1)
                nc.scalar.activation(root[R, :], dm[R, :], ACT.Sqrt).then_inc(rooted, 1)
                wait(act, built, g + 1)
                act.dma_start(group_rows(d["table0"], g, rows, D + 2),
                              row[b][R, :, :].rearrange("p t c -> p (t c)")).then_inc(stored[b], 16)
            over_groups(act, body)
            act.wait_ge(stored[0], 16 * (PAIRS + 1))
            act.wait_ge(stored[1], 16 * (PAIRS + 1))


class EdgeStage:

    def __init__(self, nc, ctx, c, d, tag, *, table, width, source, target, sums, out_width, clear):
        self.nc, self.c, self.d = nc, c, d
        self.table, self.width, self.sums, self.out_width = d[table], width, [d[x] for x in sums], out_width
        self.source, self.target, self.clear = source, target, clear
        s = self.s = Scope(nc, ctx, tag)
        self.take = [s.sb(f"take{b}", [P, G], I32) for b in range(2)]
        self.key = [s.sb(f"key{b}", [P, G], I32) for b in range(2)]
        self.line = [s.sb(f"line{b}", [P, FULL], I32) for b in range(2)]
        self.keyf = [s.sb(f"keyf{b}", [P, G]) for b in range(2)]
        self.keyd = [s.sb(f"keyd{b}", [P, G]) for b in range(2)]
        self.put = [s.sb(f"put{b}", [P, G], I32) for b in range(2)]
        self.same = [s.sb(f"same{k}", [P, SUB * P]) for k in range(SLOTS)]
        self.earlier = s.sb("earlier", [P, SUB, P])
        self.nearlier = s.sb("nearlier", [P, SUB])
        self.putd = s.sb("putd", [P, SUB])
        self.total = [s.sb(f"total{k}", [P, SUB, out_width]) for k in range(SLOTS)]
        self.psum = s.ps([P, 512])
        self.take_loaded = s.sems("take_loaded", 2)
        self.keys_loaded = s.sems("keys_loaded", 2)
        self.gathered = s.sems("gathered", SLOTS)
        self.added = s.sems("added", 2)
        self.put_ready = s.sem("put_ready")
        self.same_ready = s.sem("same_ready")
        self.summed = s.sem("summed")
        self.total_ready = s.sem("total_ready")
        self.keyed = s.sem("keyed")
        self.passed = s.sem("passed")
        self.cleared = s.sem("cleared")

    def load_indices(self, sp, u, b, rows):
        g = 2 * u + b
        wait(sp, self.gathered[SLOTS - 1], 16 * SUB * (g - 1))
        sp.dma_start(self.take[b][0:rows, :], group_rows(self.d[self.source], g, rows)).then_inc(
            self.take_loaded[b], 16)
        wait(sp, self.put_ready, UNITS * (g - 1))
        sp.dma_start(self.key[b][0:rows, :], group_rows(self.d[self.target], g, rows)).then_inc(
            self.keys_loaded[b], 16)
        sp.dma_start(self.line[b][0:rows, 0:rows * G], group_line(self.d[self.target + "_line"], g, rows)).then_inc(
            self.keys_loaded[b], 16)

    def before_gather(self, pool, u, b, rows, k, freed):
        g = 2 * u + b
        if k == 0:
            hold(pool, self.take_loaded[b], 16 * (u + 1), self.passed)
        hold(pool, freed, UNITS * g + k - (SLOTS - 1), self.passed)

    def gather(self, b, rows, k, t, into):
        col = SUB * k + t
        self.nc.gpsimd.indirect_dma_start(
            out=into[k][0:rows, t, 0:self.width], out_offset=None, in_=self.table,
            in_offset=bass.IndirectOffsetOnAxis(ap=self.take[b][0:rows, col:col + 1], axis=0),
        ).then_inc(self.gathered[k], 16)

    def before_scatter(self, pool, u, b, rows, k):
        g = 2 * u + b
        hold(pool, self.put_ready, UNITS * g + k + 1, self.passed)
        hold(pool, self.total_ready, UNITS * g + k + 1, self.passed)

    def scatter(self, pool, u, b, rows, k, t):
        col = SUB * k + t
        copy = (b + col) % 2
        hold(pool, self.added[copy], 16 * (G * u + (G * b + col) // 2), self.passed)
        self.nc.gpsimd.indirect_dma_start(
            out=self.sums[copy], in_=self.total[k][0:rows, t, :], in_offset=None,
            out_offset=bass.IndirectOffsetOnAxis(ap=self.put[b][0:rows, col:col + 1], axis=0),
            compute_op=ALU.add).then_inc(self.added[copy], 16)

    def pool_program(self, pool, into, freed, lag=LAG):
        def body(u, b, rows):
            first = isinstance(u, int) and u == 0 and b == 0
            for k in range(UNITS):
                if k >= lag:
                    late = (u, b, rows, k - lag)
                elif not first:
                    late = (u if b else u - 1, 1 - b, P, k - lag + UNITS)
                else:
                    late = None
                self.before_gather(pool, u, b, rows, k, freed)
                self.gather(b, rows, k, 0, into)
                if late:
                    self.before_scatter(pool, *late)
                for t in range(SUB):
                    if t:
                        self.gather(b, rows, k, t, into)
                    if late:
                        self.scatter(pool, *late, t)
        over_groups(pool, body)
        for k in range(UNITS - lag, UNITS):
            self.before_scatter(pool, PAIRS, 1, TAIL, k)
            for t in range(SUB):
                self.scatter(pool, PAIRS, 1, TAIL, k, t)
        for copy in range(2):
            pool.wait_ge(self.added[copy], 16 * G * NG // 2)

    KEY_STEPS = 2 + 4 * UNITS

    def key_group(self, dve, st, u, b, rows):
        g = 2 * u + b
        v, R = self.nc.vector, slice(0, rows)
        wait(dve, self.keys_loaded[b], 32 * (u + 1))
        st.did(v.tensor_copy(self.keyf[b][R, :], self.key[b][R, :]))
        st.wait()
        st.did(v.tensor_scalar(self.keyd[b][R, :], self.keyf[b][R, :], self.c["spare"][R, 0:1], None, ALU.subtract))
        st.wait()
        for copy in range(2):
            wait(dve, self.added[copy], 16 * (G * u + (G * (b - 1) + 1 - copy) // 2))

    def same_unit(self, dve, st, u, b, rows, k):
        g = 2 * u + b
        v, R = self.nc.vector, slice(0, rows)
        wait(dve, self.summed, UNITS * g + k - (SLOTS - 1))
        for t in range(SUB):
            col = SUB * k + t
            last = v.tensor_scalar(self.same[k][R, t * rows:(t + 1) * rows],
                                   self.line[b][R, col * rows:(col + 1) * rows],
                                   self.keyf[b][R, col:col + 1], None, ALU.is_equal)
        last.then_inc(self.same_ready, 1)
        wait(dve, self.same_ready, UNITS * g + k + 1)
        cols = slice(SUB * k, SUB * (k + 1))
        st.did(v.tensor_tensor(self.earlier[R, :, R], self.same[k][R, 0:SUB * rows].rearrange("p (t e) -> p t e", t=SUB),
                               along(self.c["before"][R, R], SUB), ALU.mult))
        st.wait()
        st.did(v.tensor_reduce(self.nearlier[R, :], self.earlier[R, :, R], AX, ALU.add))
        st.wait()
        st.did(v.tensor_scalar(self.nearlier[R, :], self.nearlier[R, :], 0.0, None, ALU.is_equal))
        st.wait()
        st.did(v.tensor_tensor(self.putd[R, :], self.nearlier[R, :], self.keyd[b][R, cols], ALU.mult))
        st.wait()
        v.tensor_scalar(self.put[b][R, cols], self.putd[R, :], self.c["spare"][R, 0:1], None,
                        ALU.add).then_inc(self.put_ready, 1)

    def sum_unit(self, pe, u, b, rows, k, messages):
        g = 2 * u + b
        W, R = self.out_width, slice(0, rows)
        wait(pe, self.same_ready, UNITS * g + k + 1)
        wait(pe, self.total_ready, UNITS * g + k)
        for t in range(SUB):
            last = self.nc.tensor.matmul(self.psum[R, t * W:(t + 1) * W], self.same[k][R, t * rows:(t + 1) * rows],
                                         messages[R, t, 0:W], start=True, stop=True)
        last.then_inc(self.summed, 1)

    def copy_unit(self, act, u, b, rows, k):
        g = 2 * u + b
        R = slice(0, rows)
        wait(act, self.summed, UNITS * g + k + 1)
        J = G * b + SUB * k + SUB - G
        for copy in range(2):
            wait(act, self.added[copy], 16 * (G * u + (J + 1 - copy) // 2))
        self.nc.scalar.activation(self.total[k][R, :, :].rearrange("p t c -> p (t c)"),
                                  self.psum[R, 0:SUB * self.out_width], ACT.Copy).then_inc(self.total_ready, 1)

    def clear_next(self, act):
        if self.clear is None:
            return 0
        names, width = self.clear
        return clear_sums(self.nc, act, [self.d[x] for x in names], width, self.cleared)


def plain_edges(nc, c, d, tag, table, width, sums, out_width, clear, types):
    with ExitStack() as ctx:
        e = EdgeStage(nc, ctx, c, d, tag, table=table, width=width, source="src", target="dst", sums=sums,
                      out_width=out_width, clear=clear)
        rows_of = [e.s.sb(f"rows{k}", [P, SUB, width]) for k in range(SLOTS)]
        kind = [e.s.sb(f"kind{b}", [P, G]) for b in range(2)]
        kind_taken = e.s.sem("kind_taken")
        kind_stored = e.s.sems("kind_stored", 2)
        block = ctx.enter_context(nc.Block())

        @block.sync
        def _(sp):
            over_groups(sp, lambda u, b, rows: e.load_indices(sp, u, b, rows))

        @block.gpsimd
        def _(pool):
            e.pool_program(pool, rows_of, e.total_ready)

        @block.vector
        def _(dve):
            def body(u, b, rows):
                st = Steps(dve, e.keyed, e.KEY_STEPS, 2 * u + b)
                e.key_group(dve, st, u, b, rows)
                for k in range(UNITS):
                    e.same_unit(dve, st, u, b, rows, k)
                st.end()
            over_groups(dve, body)

        @block.tensor
        def _(pe):
            def body(u, b, rows):
                for k in range(UNITS):
                    wait(pe, e.gathered[k], 16 * SUB * (2 * u + b + 1))
                    e.sum_unit(pe, u, b, rows, k, rows_of[k])
            over_groups(pe, body)

        @block.scalar
        def _(act):
            n = e.clear_next(act)

            def body(u, b, rows):
                g = 2 * u + b
                if types:
                    wait(act, kind_stored[b], 16 * u)
                for k in range(UNITS):
                    if types:
                        wait(act, e.gathered[k], 16 * SUB * (g + 1))
                        nc.scalar.activation(kind[b][0:rows, SUB * k:SUB * (k + 1)],
                                             rows_of[k][0:rows, :, width - 1], ACT.Copy).then_inc(kind_taken, 1)
                    e.copy_unit(act, u, b, rows, k)
                if types:
                    wait(act, kind_taken, UNITS * (g + 1))
                    act.dma_start(group_rows(d["srctype"], g, rows), kind[b][0:rows, :]).then_inc(kind_stored[b], 16)
            over_groups(act, body)
            if types:
                for b in range(2):
                    act.wait_ge(kind_stored[b], 16 * (PAIRS + 1))
            wait(act, e.cleared, n)


def filter_edges(nc, c, d):
    W1 = D + 2
    A, B = 3, SUB - 3
    with ExitStack() as ctx:
        e = EdgeStage(nc, ctx, c, d, "flt", table="table1", width=W1, source="dst", target="src",
                      sums=("sum1a", "sum1b"), out_width=D + 1, clear=(("sum2a", "sum2b"), D))
        s = e.s
        rows_of = [s.sb(f"rows{k}", [P, SUB, W1]) for k in range(SLOTS)]
        attr = [s.sb(f"attr{b}", [NA, FULL]) for b in range(2)]
        dist = [s.sb(f"dist{b}", [P, G]) for b in range(2)]
        kind = [s.sb(f"kind{b}", [P, G]) for b in range(2)]
        near = s.sb("near", [P, G])
        sine = s.sb("sine", [P, G])
        inside = s.sb("inside", [P, G])
        cut = [s.sb(f"cut{b}", [P, G]) for b in range(2)]
        hot_d = s.sb("hot_d", [P, SUB, NZ])
        hot_s = s.sb("hot_s", [P, SUB, NZ])
        hot_dT = s.sb("hot_dT", [NZ, SUB * P])
        hidden = s.sb("hidden", [D + 1, SUB * P])
        picked = s.sb("picked", [P, SUB, NZ])
        logit = s.sb("logit", [P, SUB])
        weight = s.sb("weight", [P, SUB])
        hw = s.sb("hw", [P, SUB, D])
        gated = s.sb("gated", [P, SUB, D])
        message = [s.sb(f"message{k}", [P, SUB, D + 1]) for k in range(2)]
        p_hidden = s.ps([P, 2, 512])
        p_hot = s.ps([P, 2, 512])
        p_pair = s.ps([P, 2, 512])
        p_gate = s.ps([P, 512])
        linear_loaded = s.sems("linear_loaded", 2)
        pe_passed = s.sem("pe_passed")
        near_ready, sine_ready, hot_ready, hidden_mult, hidden_ready = (
            s.sem(x) for x in ("near_ready", "sine_ready", "hot_ready", "hidden_mult", "hidden_ready"))
        turned, turned_copied, pair_ready, gate_ready, message_ready = (
            s.sem(x) for x in ("turned", "turned_copied", "pair_ready", "gate_ready", "message_ready"))
        messaged, prepared, ones_placed = s.sem("messaged"), s.sem("prepared"), s.sem("ones_placed")
        block = ctx.enter_context(nc.Block())

        @block.sync
        def _(sp):
            sp.dma_start(hidden[D:D + 1, :].rearrange("p (t e) -> p t e", t=SUB),
                         along(c["ones"][0:1, :], SUB)).then_inc(ones_placed, 16)

            def body(u, b, rows):
                g = 2 * u + b
                e.load_indices(sp, u, b, rows)
                wait(sp, message_ready, UNITS * (g - 1))
                wait(sp, gate_ready, UNITS * (g - 1))
                if rows == P:
                    sp.dma_start(attr[b][:, :], d["attr"][bass.ds(g * NA, NA), :]).then_inc(linear_loaded[b], 16)
                else:
                    sp.dma_start(attr[b][:, 0:rows * G], d["attr_tail"]).then_inc(linear_loaded[b], 16)
                sp.dma_start(dist[b][0:rows, :], group_rows(d["dist"], g, rows)).then_inc(linear_loaded[b], 16)
                sp.dma_start(kind[b][0:rows, :], group_rows(d["srctype"], g, rows)).then_inc(linear_loaded[b], 16)
            over_groups(sp, body)

        @block.gpsimd
        def _(pool):
            e.pool_program(pool, rows_of, message_ready)

        @block.vector
        def _(dve):
            v = nc.vector

            steps = [None]

            def begin(u, b, rows):
                g = 2 * u + b
                R = slice(0, rows)
                st = steps[0] = Steps(dve, e.keyed, e.KEY_STEPS + 4, g)
                e.key_group(dve, st, u, b, rows)
                wait(dve, linear_loaded[b], 48 * (u + 1))
                v.tensor_scalar(near[R, :], dist[b][R, :], CUTOFF, PI / (2 * CUTOFF), ALU.min,
                                ALU.mult).then_inc(near_ready, 1)
                st.did(v.tensor_scalar(inside[R, :], dist[b][R, :], CUTOFF, None, ALU.is_lt))
                wait(dve, sine_ready, g + 1)
                st.did(v.tensor_tensor(cut[b][R, :], sine[R, :], sine[R, :], ALU.mult))
                st.wait()
                st.did(v.tensor_scalar(cut[b][R, :], cut[b][R, :], -1.0, 1.0, ALU.mult, ALU.add))
                st.wait()
                st.did(v.tensor_tensor(cut[b][R, :], cut[b][R, :], inside[R, :], ALU.mult))

            def hot_rows(u, b, rows, k):
                q = UNITS * (2 * u + b) + k
                R = slice(0, rows)
                wait(dve, e.gathered[k], 16 * SUB * (2 * u + b + 1))
                wait(dve, turned, q)
                v.tensor_tensor(hot_d[R, :, :], spread(rows_of[k][R, :, W1 - 1], NZ), along(c["zline"][R, :], SUB),
                                ALU.is_equal).then_inc(hot_ready, 1)

            def messages(u, b, rows, k):
                q = UNITS * (2 * u + b) + k
                R = slice(0, rows)
                st = Steps(dve, messaged, 5, q)
                wait(dve, pair_ready, q + 1)
                wait(dve, prepared, 3 * (q + 1))
                st.did(v.tensor_tensor(picked[R, 0:A, :], p_pair[R, 0, 0:A * NZ].rearrange("p (t z) -> p t z", t=A),
                                       hot_s[R, 0:A, :], ALU.mult))
                st.did(v.tensor_tensor(picked[R, A:SUB, :], p_pair[R, 1, 0:B * NZ].rearrange("p (t z) -> p t z", t=B),
                                       hot_s[R, A:SUB, :], ALU.mult))
                st.wait()
                st.did(v.tensor_reduce(logit[R, :], picked[R, :, :], AX, ALU.add))
                st.wait()
                wait(dve, gate_ready, q + 1)
                st.did(v.tensor_tensor(gated[R, :, :], p_gate[R, 0:SUB * D].rearrange("p (t c) -> p t c", t=SUB),
                                       spread(logit[R, :], D), ALU.add))
                m = message[(b + k) % 2]
                wait(dve, e.summed, q - 1)
                st.did(v.tensor_copy(m[R, :, D], rows_of[k][R, :, D]))
                st.wait()
                st.end()
                v.tensor_tensor(m[R, :, 0:D], gated[R, :, :], hw[R, :, :], ALU.mult).then_inc(message_ready, 1)

            def prepare(u, b, rows, k):
                q = UNITS * (2 * u + b) + k
                R = slice(0, rows)
                cols = slice(SUB * k, SUB * (k + 1))
                wait(dve, e.keyed, (2 * u + b) * steps[0].per + steps[0].n)
                wait(dve, message_ready, q)
                v.tensor_tensor(hot_s[R, :, :], spread(kind[b][R, cols], NZ), along(c["zline"][R, :], SUB),
                                ALU.is_equal).then_inc(prepared, 1)
                v.tensor_tensor(weight[R, :], cut[b][R, cols], rows_of[k][R, :, D], ALU.mult).then_inc(prepared, 1)
                wait(dve, prepared, 3 * q + 2)
                v.tensor_tensor(hw[R, :, :], rows_of[k][R, :, 0:D], spread(weight[R, :], D),
                                ALU.mult).then_inc(prepared, 1)

            def body(u, b, rows):
                begin(u, b, rows)
                for k in range(UNITS):
                    hot_rows(u, b, rows, k)
                    before = unit_before(u, b, rows, k)
                    if before:
                        messages(*before)
                    prepare(u, b, rows, k)
                    e.same_unit(dve, steps[0], u, b, rows, k)
                steps[0].end()
            over_groups(dve, body)
            messages(PAIRS, 1, TAIL, UNITS - 1)

        @block.tensor
        def _(pe):
            pe.wait_ge(ones_placed, 16)

            def turn(u, b, rows, k):
                q = UNITS * (2 * u + b) + k
                R = slice(0, rows)
                wait(pe, hot_ready, q + 1)
                wait(pe, turned_copied, q)
                for t in range(SUB):
                    bank, o = (0, t) if t < A else (1, t - A)
                    last = nc.tensor.transpose(p_hot[0:NZ, bank, o * rows:(o + 1) * rows], hot_d[R, t, :],
                                               c["ident"][R, R])
                last.then_inc(turned, 1)

            def products(u, b, rows, k):
                q = UNITS * (2 * u + b) + k
                R = slice(0, rows)
                hold(pe, linear_loaded[b], 48 * (u + 1), pe_passed)
                hold(pe, hidden_ready, q, pe_passed)
                for bank, t0, n in ((0, 0, A), (1, A, B)):
                    at = (SUB * k + t0) * rows
                    last = nc.tensor.matmul(p_hidden[0:D, bank, 0:n * rows], c["f1"][:, :],
                                            attr[b][:, at:at + n * rows], start=True, stop=True)
                last.then_inc(hidden_mult, 1)
                wait(pe, turned_copied, q + 1)
                wait(pe, message_ready, q)
                for t in range(SUB):
                    bank, o = (0, t) if t < A else (1, t - A)
                    last = nc.tensor.matmul(p_pair[R, bank, o * NZ:(o + 1) * NZ],
                                            hot_dT[:, t * rows:(t + 1) * rows], c["pairs"][:, :],
                                            start=True, stop=True)
                last.then_inc(pair_ready, 1)
                wait(pe, hidden_ready, q + 1)
                for t in range(SUB):
                    last = nc.tensor.matmul(p_gate[R, t * D:(t + 1) * D], hidden[:, t * rows:(t + 1) * rows],
                                            c["f2"][:, :], start=True, stop=True)
                last.then_inc(gate_ready, 1)

            def body(u, b, rows):
                for k in range(UNITS):
                    turn(u, b, rows, k)
                    before = unit_before(u, b, rows, k)
                    if before:
                        pu, pb, prows, pk = before
                        wait(pe, message_ready, UNITS * (2 * pu + pb) + pk + 1)
                        e.sum_unit(pe, *before, message[(pb + pk) % 2])
                    products(u, b, rows, k)
            over_groups(pe, body)
            wait(pe, message_ready, UNITS * NG)
            e.sum_unit(pe, PAIRS, 1, TAIL, UNITS - 1, message[UNITS % 2])

        @block.scalar
        def _(act):
            n = e.clear_next(act)

            def begin(u, b, rows):
                wait(act, near_ready, 2 * u + b + 1)
                nc.scalar.activation(sine[0:rows, :], near[0:rows, :], ACT.Sin).then_inc(sine_ready, 1)

            def copies(u, b, rows, k):
                q = UNITS * (2 * u + b) + k
                wait(act, turned, q + 1)
                wait(act, pair_ready, q)
                nc.scalar.activation(hot_dT[:, 0:A * rows], p_hot[0:NZ, 0, 0:A * rows], ACT.Copy)
                nc.scalar.activation(hot_dT[:, A * rows:SUB * rows], p_hot[0:NZ, 1, 0:B * rows],
                                     ACT.Copy).then_inc(turned_copied, 1)
                wait(act, hidden_mult, q + 1)
                wait(act, gate_ready, q)
                nc.scalar.activation(hidden[0:D, 0:A * rows], p_hidden[0:D, 0, 0:A * rows], ACT.Silu,
                                     bias=c["f1b"][:, 0:1])
                nc.scalar.activation(hidden[0:D, A * rows:SUB * rows], p_hidden[0:D, 1, 0:B * rows], ACT.Silu,
                                     bias=c["f1b"][:, 0:1]).then_inc(hidden_ready, 1)

            over_units(act, copies, lambda u, b, rows, k: e.copy_unit(act, u, b, rows, k), begin)
            wait(act, e.cleared, n)


def relation_edges(nc, c, d):
    A, B = 3, SUB - 3
    with ExitStack() as ctx:
        e = EdgeStage(nc, ctx, c, d, "rel", table="table2", width=D, source="src", target="dst",
                      sums=("sum2a", "sum2b"), out_width=D, clear=(("sum3a", "sum3b"), D))
        s = e.s
        rows_of = [s.sb(f"rows{k}", [P, SUB, D]) for k in range(SLOTS)]
        parts = [[s.sb(f"parts{i}{k}", [P, SUB, KS + 1], BF16) for k in range(2)] for i in range(2)]
        rest = s.sb("rest", [P, SUB, D])
        norm = [s.sb(f"norm{b}", [P, G]) for b in range(2)]
        rel = [s.sb(f"rel{b}", [P, G], I32) for b in range(2)]
        relf = s.sb("relf", [P, G])
        xT = [s.sb(f"xT{i}", [KS, SUB * P], BF16) for i in range(2)]
        h1 = [s.sb(f"h1_{ch}", [P, SUB * P]) for ch in range(CHUNKS)]
        message = [s.sb(f"message{k}", [P, SUB, D]) for k in range(2)]
        p_x = [s.ps([P, 512]).bitcast(BF16) for i in range(2)]
        p_h1 = [s.ps([P, 2, 512]) for q in range(2)]
        p_h2 = s.ps([P, 512])
        linear_loaded = s.sems("linear_loaded", 2)
        pe_passed = s.sem("pe_passed")
        ones_ready, parted, turned, turned_copied, h2_ready, message_ready = (
            s.sem(x) for x in ("ones_ready", "parted", "turned", "turned_copied", "h2_ready", "message_ready"))
        rows_read = s.sem("rows_read")
        h1_mult = s.sem("h1_mult")
        h1_ready_a, h1_ready_b = s.sem("h1_ready_a"), s.sem("h1_ready_b")
        block = ctx.enter_context(nc.Block())

        @block.sync
        def _(sp):
            def body(u, b, rows):
                g = 2 * u + b
                e.load_indices(sp, u, b, rows)
                wait(sp, message_ready, UNITS * (g - 1))
                sp.dma_start(norm[b][0:rows, :], group_rows(d["norm"], g, rows)).then_inc(linear_loaded[b], 16)
                sp.dma_start(rel[b][0:rows, :], group_rows(d["rel"], g, rows)).then_inc(linear_loaded[b], 16)
            over_groups(sp, body)

        @block.gpsimd
        def _(pool):
            e.pool_program(pool, rows_of, rows_read, lag=LAG + 1)

        @block.vector
        def _(dve):
            v = nc.vector
            for i in range(2):
                for k in range(2):
                    v.tensor_copy(parts[i][k][:, :, KX - 1], c["ones"][:, 0:SUB]).then_inc(ones_ready, 1)
            dve.wait_ge(ones_ready, 4)

            def relus(u, b, rows, k):
                q = UNITS * (2 * u + b) + k
                wait(dve, h2_ready, q)
                for ch in range(CHUNKS):
                    wait(dve, h1_mult, CHUNKS * q + ch + 1)
                    v.tensor_scalar_max(h1[ch][:, A * rows:SUB * rows], p_h1[(b + k + ch) % 2][:, 1, 0:B * rows],
                                        0.0).then_inc(h1_ready_b, 1)

            def split_rows(u, b, rows, k):
                g = 2 * u + b
                q = UNITS * g + k
                R = slice(0, rows)
                first, second = parts[0][(b + k) % 2], parts[1][(b + k) % 2]
                wait(dve, turned, q - 1)
                for part in (first, second):
                    v.tensor_tensor(part[R, :, D:D + NR], spread(relf[R, SUB * k:SUB * (k + 1)], NR),
                                    along(c["rline"][R, :], SUB), ALU.not_equal).then_inc(parted, 1)
                wait(dve, e.gathered[k], 16 * SUB * (g + 1))
                x = rows_of[k][R, :, :]
                v.tensor_copy(first[R, :, 0:D], x).then_inc(parted, 1)
                wait(dve, parted, 6 * q + 3)
                v.tensor_tensor(rest[R, :, :], x, first[R, :, 0:D], ALU.subtract).then_inc(rows_read, 1)
                wait(dve, rows_read, q + 1)
                v.tensor_copy(second[R, :, 0:D], first[R, :, 0:D]).then_inc(parted, 1)
                v.tensor_copy(first[R, :, KX:KS], rest[R, :, :]).then_inc(parted, 1)
                wait(dve, parted, 6 * q + 5)
                v.tensor_tensor(second[R, :, KX:KS], rest[R, :, :], first[R, :, KX:KS],
                                ALU.subtract).then_inc(parted, 1)

            def message_of(u, b, rows, k):
                q = UNITS * (2 * u + b) + k
                R = slice(0, rows)
                wait(dve, h2_ready, q + 1)
                wait(dve, e.summed, q - 1)
                v.tensor_tensor(message[(b + k) % 2][R, :, :],
                                p_h2[R, 0:SUB * D].rearrange("p (t c) -> p t c", t=SUB),
                                spread(norm[b][R, SUB * k:SUB * (k + 1)], D), ALU.mult).then_inc(message_ready, 1)

            def body(u, b, rows):
                g = 2 * u + b
                R = slice(0, rows)
                st = Steps(dve, e.keyed, e.KEY_STEPS + 1, g)
                e.key_group(dve, st, u, b, rows)
                wait(dve, linear_loaded[b], 32 * (u + 1))
                st.did(v.tensor_copy(relf[R, :], rel[b][R, :]))
                st.wait()
                for k in range(UNITS):
                    split_rows(u, b, rows, k)
                    before = unit_before(u, b, rows, k)
                    if before:
                        before2 = unit_before(*before)
                        if before2:
                            message_of(*before2)
                        relus(*before)
                    e.same_unit(dve, st, u, b, rows, k)
                st.end()
            over_groups(dve, body)
            message_of(PAIRS, 1, TAIL, UNITS - 2)
            relus(PAIRS, 1, TAIL, UNITS - 1)
            message_of(PAIRS, 1, TAIL, UNITS - 1)

        @block.tensor
        def _(pe):
            pe.wait_ge(ones_ready, 4)

            def turn(u, b, rows, k):
                g = 2 * u + b
                q = UNITS * g + k
                R = slice(0, rows)
                hold(pe, parted, 6 * (q + 1), pe_passed)
                hold(pe, turned_copied, 2 * q, pe_passed)
                for i in range(2):
                    for t in range(SUB):
                        last = nc.tensor.transpose(p_x[i][0:KS, t * rows:(t + 1) * rows],
                                                   parts[i][(b + k) % 2][R, t, 0:KS], c["identb"][R, R])
                last.then_inc(turned, 1)

            def first_products(u, b, rows, k):
                q = UNITS * (2 * u + b) + k
                wait(pe, turned_copied, 2 * (q + 1))
                for ch in range(CHUNKS):
                    wait(pe, h1_ready_a, CHUNKS * q + ch - 1)
                    wait(pe, h1_ready_b, CHUNKS * q + ch - 1)
                    for i, (weight, x) in enumerate((("r1a", xT[0]), ("r1b", xT[0]), ("r1c", xT[1]))):
                        for bank, t0, n in ((0, 0, A), (1, A, B)):
                            last = nc.tensor.matmul(p_h1[(b + k + ch) % 2][:, bank, 0:n * rows],
                                                    c[weight][:, ch * P:(ch + 1) * P],
                                                    x[:, t0 * rows:(t0 + n) * rows], start=(i == 0), stop=(i == 2))
                    last.then_inc(h1_mult, 1)

            def second_products(u, b, rows, k):
                q = UNITS * (2 * u + b) + k
                R = slice(0, rows)
                wait(pe, message_ready, q)
                wait(pe, h1_ready_a, CHUNKS * (q + 1))
                wait(pe, h1_ready_b, CHUNKS * (q + 1))
                for t in range(SUB):
                    for ch in range(CHUNKS):
                        last = nc.tensor.matmul(p_h2[R, t * D:(t + 1) * D], h1[ch][:, t * rows:(t + 1) * rows],
                                                c["r2"][:, ch, :], start=(ch == 0), stop=(ch == CHUNKS - 1))
                last.then_inc(h2_ready, 1)

            def sums(u, b, rows, k):
                wait(pe, message_ready, UNITS * (2 * u + b) + k + 1)
                e.sum_unit(pe, u, b, rows, k, message[(b + k) % 2])

            def body(u, b, rows):
                for k in range(UNITS):
                    turn(u, b, rows, k)
                    before = unit_before(u, b, rows, k)
                    if before:
                        second_products(*before)
                    first_products(u, b, rows, k)
                    if before:
                        sums(*before)
            over_groups(pe, body)
            second_products(PAIRS, 1, TAIL, UNITS - 1)
            sums(PAIRS, 1, TAIL, UNITS - 1)

        @block.scalar
        def _(act):
            n = e.clear_next(act)

            def copies(u, b, rows, k):
                q = UNITS * (2 * u + b) + k
                wait(act, turned, q + 1)
                wait(act, h1_mult, CHUNKS * q)
                for i in range(2):
                    nc.scalar.activation(xT[i][:, 0:SUB * rows], p_x[i][0:KS, 0:SUB * rows],
                                         ACT.Copy).then_inc(turned_copied, 1)
                wait(act, h2_ready, q)
                for ch in range(CHUNKS):
                    wait(act, h1_mult, CHUNKS * q + ch + 1)
                    nc.scalar.activation(h1[ch][:, 0:A * rows], p_h1[(b + k + ch) % 2][:, 0, 0:A * rows],
                                         ACT.Relu).then_inc(h1_ready_a, 1)

            over_units(act, copies, lambda u, b, rows, k: e.copy_unit(act, u, b, rows, k))
            wait(act, e.cleared, n)


class Norm:

    STEPS = 6

    def __init__(self, s, nc, tag):
        self.nc = nc
        self.total = s.sb(tag + "_total", [P, G])
        self.mean = s.sb(tag + "_mean", [P, G])
        self.centred = s.sb(tag + "_centred", [P, G, D])
        self.square = s.sb(tag + "_square", [P, G, D])
        self.spread = s.sb(tag + "_spread", [P, G])
        self.var = s.sb(tag + "_var", [P, G])
        self.root = s.sb(tag + "_root", [P, G])
        self.inv = s.sb(tag + "_inv", [P, G])
        self.centred_ready = s.sem(tag + "_centred_ready")
        self.squared = s.sem(tag + "_squared")
        self.var_ready = s.sem(tag + "_var_ready")
        self.rooted = s.sem(tag + "_rooted")

    def vector(self, dve, st, g, rows, x, out):
        v, R = self.nc.vector, slice(0, rows)
        st.did(v.tensor_reduce(self.total[R, :], x, AX, ALU.add))
        st.wait()
        st.did(v.tensor_scalar(self.mean[R, :], self.total[R, :], 1.0 / D, None, ALU.mult))
        st.wait()
        v.tensor_tensor(self.centred[R, :, :], x, spread(self.mean[R, :], D), ALU.subtract).then_inc(
            self.centred_ready, 1)
        wait(dve, self.squared, g + 1)
        st.did(v.tensor_reduce(self.spread[R, :], self.square[R, :, :], AX, ALU.add))
        st.wait()
        v.tensor_scalar(self.var[R, :], self.spread[R, :], 1.0 / D, EPS, ALU.mult, ALU.add).then_inc(
            self.var_ready, 1)
        wait(dve, self.rooted, g + 1)
        st.did(v.reciprocal(self.inv[R, :], self.root[R, :]))
        st.wait()
        last = v.tensor_tensor(out, self.centred[R, :, :], spread(self.inv[R, :], D), ALU.mult)
        self.n = 4
        return last

    def scalar(self, act, g, rows):
        R = slice(0, rows)
        wait(act, self.centred_ready, g + 1)
        self.nc.scalar.activation(self.square[R, :, :], self.centred[R, :, :], ACT.Square).then_inc(self.squared, 1)
        wait(act, self.var_ready, g + 1)
        self.nc.scalar.activation(self.root[R, :], self.var[R, :], ACT.Sqrt).then_inc(self.rooted, 1)


NORM_STEPS = 4


def turn_and_multiply(nc, c, pe, s_, g, rows, x, width, x_ready, weight, units_done):
    R = slice(0, rows)
    A = 3
    for k in range(UNITS):
        q = UNITS * g + k
        if k == 0:
            hold(pe, x_ready, g + 1, s_["pe_passed"])
        hold(pe, s_["turned_copied"], q, s_["pe_passed"])
        for t in range(SUB):
            bank, o = (0, t) if t < A else (1, t - A)
            last = nc.tensor.transpose(s_["p_x"][0:width, bank, o * rows:(o + 1) * rows], x[R, SUB * k + t, :],
                                       c["ident"][R, R])
        last.then_inc(s_["turned"], 1)
        wait(pe, s_["turned_copied"], q + 1)
        wait(pe, units_done, q - 1)
        p_y = s_["p_y"][(s_["b"] + k) % 2]
        for t in range(SUB):
            last = nc.tensor.matmul(p_y[R, t * D:(t + 1) * D], s_["xT"][k % 2][0:width, t * rows:(t + 1) * rows],
                                    weight[:, :], start=True, stop=True)
        last.then_inc(s_["multiplied"], 1)


def turn_copies(nc, act, s_, g, rows, width):
    A, B = 3, SUB - 3
    for k in range(UNITS):
        q = UNITS * g + k
        wait(act, s_["turned"], q + 1)
        wait(act, s_["multiplied"], q - 1)
        xT = s_["xT"][k % 2]
        nc.scalar.activation(xT[0:width, 0:A * rows], s_["p_x"][0:width, 0, 0:A * rows], ACT.Copy)
        nc.scalar.activation(xT[0:width, A * rows:SUB * rows], s_["p_x"][0:width, 1, 0:B * rows],
                             ACT.Copy).then_inc(s_["turned_copied"], 1)


def turn_memory(s):
    s_ = dict(p_x=s.ps([P, 2, 512]), p_y=[s.ps([P, 512]) for i in range(2)],
              xT=[s.sb(f"xT{i}", [D + 1, SUB * P]) for i in range(2)])
    for x in ("turned", "turned_copied", "multiplied", "pe_passed"):
        s_[x] = s.sem(x)
    return s_


def nodes0(nc, c, d):
    W = D + 1
    with ExitStack() as ctx:
        s = Scope(nc, ctx, "n0")
        sa = [s.sb(f"sa{b}", [P, G * W]) for b in range(2)]
        sb_ = [s.sb(f"sb{b}", [P, G * W]) for b in range(2)]
        x = [s.sb(f"x{b}", [P, G, D]) for b in range(2)]
        z = [s.sb(f"z{b}", [P, G], I32) for b in range(2)]
        mult = [s.sb(f"mult{b}", [P, G]) for b in range(2)]
        total = s.sb("total", [P, G, W])
        deg = [s.sb(f"deg{b}", [P, G]) for b in range(2)]
        dm, root, cj, alone = (s.sb(n, [P, G]) for n in ("dm", "root", "cj", "alone"))
        own = s.sb("own", [P, G, D])
        h = [s.sb(f"h{b}", [P, G, W]) for b in range(2)]
        y = s.sb("y", [P, G, D])
        row = [s.sb(f"row{b}", [P, G, D + 2]) for b in range(2)]
        norm = Norm(s, nc, "norm")
        s_ = turn_memory(s)
        loaded, stored = s.sems("loaded", 2), s.sems("stored", 2)
        ones_ready = s.sem("ones_ready")
        stepped, dm_ready, rooted, h_ready, y_ready, built = (
            s.sem(n) for n in ("stepped", "dm_ready", "rooted", "h_ready", "y_ready", "built"))
        block = ctx.enter_context(nc.Block())

        @block.sync
        def _(sp):
            def body(u, b, rows):
                g = 2 * u + b
                R = slice(0, rows)
                wait(sp, built, g - 1)
                for dst, src, w in ((sa[b][R, :], d["sum0a"], W), (sb_[b][R, :], d["sum0b"], W),
                                    (x[b][R, :, :].rearrange("p t c -> p (t c)"), d["x"], D), (z[b][R, :], d["z"], 1),
                                    (mult[b][R, :], d["mult"], 1)):
                    sp.dma_start(dst, group_rows(src, g, rows, w)).then_inc(loaded[b], 16)
            over_groups(sp, body)

        @block.vector
        def _(dve):
            v = nc.vector
            for b in range(2):
                v.tensor_copy(h[b][:, :, D], c["ones"][:, 0:G]).then_inc(ones_ready, 1)

            def body(u, b, rows):
                g = 2 * u + b
                R = slice(0, rows)
                st = Steps(dve, stepped, 8 + NORM_STEPS, g)
                wait(dve, loaded[b], 80 * (u + 1))
                st.did(v.tensor_tensor(total[R, :, :].rearrange("p t c -> p (t c)"), sa[b][R, :], sb_[b][R, :], ALU.add))
                st.wait()
                v.tensor_scalar_max(dm[R, :], total[R, :, D], 1.0).then_inc(dm_ready, 1)
                wait(dve, stored[b], 32 * u)
                st.did(v.tensor_copy(deg[b][R, :], total[R, :, D]))
                st.did(v.tensor_scalar(alone[R, :], total[R, :, D], 0.0, None, ALU.is_equal))
                st.did(v.tensor_copy(row[b][R, :, D + 1], z[b][R, :]))
                st.did(v.tensor_copy(row[b][R, :, D], mult[b][R, :]))
                st.wait()
                st.did(v.tensor_tensor(own[R, :, :], x[b][R, :, :], spread(alone[R, :], D), ALU.mult))
                wait(dve, rooted, g + 1)
                st.did(v.reciprocal(cj[R, :], root[R, :]))
                st.wait()
                st.did(v.tensor_tensor(h[b][R, :, 0:D], total[R, :, 0:D], spread(cj[R, :], D), ALU.mult))
                st.wait()
                v.tensor_tensor(h[b][R, :, 0:D], h[b][R, :, 0:D], own[R, :, :], ALU.add).then_inc(h_ready, 1)
                for k in range(UNITS):
                    q = UNITS * g + k
                    cols = slice(SUB * k, SUB * (k + 1))
                    wait(dve, s_["multiplied"], q + 1)
                    v.scalar_tensor_tensor(y[R, cols, :], s_["p_y"][(b + k) % 2][R, 0:SUB * D].rearrange(
                        "p (t c) -> p t c", t=SUB), 0.0, x[b][R, cols, :], ALU.max, ALU.add).then_inc(y_ready, 1)
                wait(dve, y_ready, UNITS * (g + 1))
                norm.vector(dve, st, g, rows, y[R, :, :], row[b][R, :, 0:D]).then_inc(built, 1)
                st.end()
            over_groups(dve, body)

        @block.tensor
        def _(pe):
            pe.wait_ge(ones_ready, 2)

            def body(u, b, rows):
                g = 2 * u + b
                s_["b"] = b
                turn_and_multiply(nc, c, pe, s_, g, rows, h[b], W, h_ready, c["w0"], y_ready)
            over_groups(pe, body)

        @block.scalar
        def _(act):
            def body(u, b, rows):
                g = 2 * u + b
                R = slice(0, rows)
                wait(act, dm_ready, g + 1)
                nc.scalar.activation(root[R, :], dm[R, :], ACT.Sqrt).then_inc(rooted, 1)
                turn_copies(nc, act, s_, g, rows, W)
                norm.scalar(act, g, rows)
                wait(act, built, g + 1)
                act.dma_start(group_rows(d["table1"], g, rows, D + 2),
                              row[b][R, :, :].rearrange("p t c -> p (t c)")).then_inc(stored[b], 16)
                act.dma_start(group_rows(d["indeg"], g, rows), deg[b][R, :]).then_inc(stored[b], 16)
            over_groups(act, body)
            for b in range(2):
                act.wait_ge(stored[b], 32 * (PAIRS + 1))


def nodes1(nc, c, d):
    W = D + 1
    with ExitStack() as ctx:
        s = Scope(nc, ctx, "n1")
        sa = [s.sb(f"sa{b}", [P, G * W]) for b in range(2)]
        sb_ = [s.sb(f"sb{b}", [P, G * W]) for b in range(2)]
        x = [s.sb(f"x{b}", [P, G, D + 2]) for b in range(2)]
        total = s.sb("total", [P, G, W])
        share = s.sb("share", [P, G])
        y = s.sb("y", [P, G, D])
        y2 = s.sb("y2", [P, G, D])
        out = [s.sb(f"out{b}", [P, G, D]) for b in range(2)]
        norm, norm2 = Norm(s, nc, "norm"), Norm(s, nc, "norm2")
        loaded, stored = s.sems("loaded", 2), s.sems("stored", 2)
        stepped, built = s.sem("stepped"), s.sem("built")
        block = ctx.enter_context(nc.Block())

        @block.sync
        def _(sp):
            def body(u, b, rows):
                g = 2 * u + b
                R = slice(0, rows)
                wait(sp, built, g - 1)
                for dst, src, w in ((sa[b][R, :], d["sum1a"], W), (sb_[b][R, :], d["sum1b"], W),
                                    (x[b][R, :, :].rearrange("p t c -> p (t c)"), d["table1"], D + 2)):
                    sp.dma_start(dst, group_rows(src, g, rows, w)).then_inc(loaded[b], 16)
            over_groups(sp, body)

        @block.vector
        def _(dve):
            v = nc.vector

            def body(u, b, rows):
                g = 2 * u + b
                R = slice(0, rows)
                st = Steps(dve, stepped, 9 + 2 * NORM_STEPS, g)
                wait(dve, loaded[b], 48 * (u + 1))
                st.did(v.tensor_tensor(total[R, :, :].rearrange("p t c -> p (t c)"), sa[b][R, :], sb_[b][R, :], ALU.add))
                st.wait()
                st.did(v.tensor_scalar_max(share[R, :], total[R, :, D], 1e-8))
                st.wait()
                st.did(v.reciprocal(share[R, :], share[R, :]))
                st.wait()
                st.did(v.tensor_tensor(y[R, :, :], total[R, :, 0:D], spread(share[R, :], D), ALU.mult))
                st.wait()
                st.did(v.tensor_tensor(y[R, :, :], y[R, :, :], x[b][R, :, 0:D], ALU.add))
                st.wait()
                st.did(norm.vector(dve, st, g, rows, y[R, :, :], y2[R, :, :]))
                st.wait()
                st.did(v.tensor_tensor(y[R, :, :], y2[R, :, :], along(c["gamma1"][R, :], G), ALU.mult))
                st.wait()
                st.did(v.tensor_tensor(y2[R, :, :], x[b][R, :, 0:D], along(c["beta1"][R, :], G), ALU.add))
                st.wait()
                st.did(v.tensor_tensor(y[R, :, :], y[R, :, :], y2[R, :, :], ALU.add))
                st.wait()
                wait(dve, stored[b], 16 * u)
                norm2.vector(dve, st, g, rows, y[R, :, :], out[b][R, :, :]).then_inc(built, 1)
                st.end()
            over_groups(dve, body)

        @block.scalar
        def _(act):
            def body(u, b, rows):
                g = 2 * u + b
                norm.scalar(act, g, rows)
                norm2.scalar(act, g, rows)
                wait(act, built, g + 1)
                act.dma_start(group_rows(d["table2"], g, rows, D),
                              out[b][0:rows, :, :].rearrange("p t c -> p (t c)")).then_inc(stored[b], 16)
            over_groups(act, body)
            for b in range(2):
                act.wait_ge(stored[b], 16 * (PAIRS + 1))


def nodes2(nc, c, d):
    with ExitStack() as ctx:
        s = Scope(nc, ctx, "n2")
        sa = [s.sb(f"sa{b}", [P, G, D]) for b in range(2)]
        sb_ = [s.sb(f"sb{b}", [P, G, D]) for b in range(2)]
        x = [s.sb(f"x{b}", [P, G, D]) for b in range(2)]
        deg = [s.sb(f"deg{b}", [P, G]) for b in range(2)]
        y = s.sb("y", [P, G, D])
        dm, root, dinv = (s.sb(n, [P, G]) for n in ("dm", "root", "dinv"))
        out = [s.sb(f"out{b}", [P, G, D]) for b in range(2)]
        row = [s.sb(f"row{b}", [P, G, D]) for b in range(2)]
        norm = Norm(s, nc, "norm")
        loaded, stored = s.sems("loaded", 2), s.sems("stored", 2)
        stepped, dm_ready, rooted, built = (s.sem(n) for n in ("stepped", "dm_ready", "rooted", "built"))
        block = ctx.enter_context(nc.Block())

        @block.sync
        def _(sp):
            def body(u, b, rows):
                g = 2 * u + b
                R = slice(0, rows)
                wait(sp, built, g - 1)
                for dst, src in ((sa[b], d["sum2a"]), (sb_[b], d["sum2b"]), (x[b], d["table2"])):
                    sp.dma_start(dst[R, :, :].rearrange("p t c -> p (t c)"), group_rows(src, g, rows, D)).then_inc(
                        loaded[b], 16)
                sp.dma_start(deg[b][R, :], group_rows(d["indeg"], g, rows)).then_inc(loaded[b], 16)
            over_groups(sp, body)

        @block.vector
        def _(dve):
            v = nc.vector

            def body(u, b, rows):
                g = 2 * u + b
                R = slice(0, rows)
                st = Steps(dve, stepped, 5 + NORM_STEPS, g)
                wait(dve, loaded[b], 64 * (u + 1))
                v.tensor_scalar_add(dm[R, :], deg[b][R, :], 1.0).then_inc(dm_ready, 1)
                st.did(v.tensor_tensor(y[R, :, :], sa[b][R, :, :], sb_[b][R, :, :], ALU.add))
                st.wait()
                st.did(v.tensor_tensor(y[R, :, :], y[R, :, :], along(c["rb2"][R, :], G), ALU.add))
                st.wait()
                st.did(v.scalar_tensor_tensor(y[R, :, :], y[R, :, :], 0.0, x[b][R, :, :], ALU.max, ALU.add))
                st.wait()
                wait(dve, stored[b], 32 * u)
                st.did(norm.vector(dve, st, g, rows, y[R, :, :], out[b][R, :, :]))
                wait(dve, rooted, g + 1)
                st.did(v.reciprocal(dinv[R, :], root[R, :]))
                st.wait()
                v.tensor_tensor(row[b][R, :, :], out[b][R, :, :], spread(dinv[R, :], D), ALU.mult).then_inc(built, 1)
                st.end()
            over_groups(dve, body)

        @block.scalar
        def _(act):
            def body(u, b, rows):
                g = 2 * u + b
                R = slice(0, rows)
                wait(act, dm_ready, g + 1)
                nc.scalar.activation(root[R, :], dm[R, :], ACT.Sqrt).then_inc(rooted, 1)
                norm.scalar(act, g, rows)
                wait(act, built, g + 1)
                for dst, src in ((d["x3"], out[b]), (d["table3"], row[b])):
                    act.dma_start(group_rows(dst, g, rows, D),
                                  src[R, :, :].rearrange("p t c -> p (t c)")).then_inc(stored[b], 16)
            over_groups(act, body)
            for b in range(2):
                act.wait_ge(stored[b], 32 * (PAIRS + 1))


def nodes3(nc, c, d, ally):
    with ExitStack() as ctx:
        s = Scope(nc, ctx, "n3")
        sa = [s.sb(f"sa{b}", [P, G, D]) for b in range(2)]
        sb_ = [s.sb(f"sb{b}", [P, G, D]) for b in range(2)]
        x = [s.sb(f"x{b}", [P, G, D]) for b in range(2)]
        deg = [s.sb(f"deg{b}", [P, G]) for b in range(2)]
        h = [s.sb(f"h{b}", [P, G, D]) for b in range(2)]
        dm, root, dinv = (s.sb(n, [P, G]) for n in ("dm", "root", "dinv"))
        s_ = turn_memory(s)
        loaded = s.sems("loaded", 2)
        stepped, dm_ready, rooted, h_ready, y_ready = (
            s.sem(n) for n in ("stepped", "dm_ready", "rooted", "h_ready", "y_ready"))
        block = ctx.enter_context(nc.Block())

        @block.sync
        def _(sp):
            def body(u, b, rows):
                g = 2 * u + b
                R = slice(0, rows)
                wait(sp, h_ready, g - 1)
                for dst, src in ((sa[b], d["sum3a"]), (sb_[b], d["sum3b"]), (x[b], d["table3"])):
                    sp.dma_start(dst[R, :, :].rearrange("p t c -> p (t c)"), group_rows(src, g, rows, D)).then_inc(
                        loaded[b], 16)
                sp.dma_start(deg[b][R, :], group_rows(d["indeg"], g, rows)).then_inc(loaded[b], 16)
            over_groups(sp, body)

        @block.vector
        def _(dve):
            v = nc.vector

            def body(u, b, rows):
                g = 2 * u + b
                R = slice(0, rows)
                st = Steps(dve, stepped, 3, g)
                wait(dve, loaded[b], 64 * (u + 1))
                v.tensor_scalar_add(dm[R, :], deg[b][R, :], 1.0).then_inc(dm_ready, 1)
                wait(dve, s_["multiplied"], UNITS * (g - 1))
                st.did(v.tensor_tensor(h[b][R, :, :], sa[b][R, :, :], sb_[b][R, :, :], ALU.add))
                st.wait()
                st.did(v.tensor_tensor(h[b][R, :, :], h[b][R, :, :], x[b][R, :, :], ALU.add))
                wait(dve, rooted, g + 1)
                st.did(v.reciprocal(dinv[R, :], root[R, :]))
                st.wait()
                v.tensor_tensor(h[b][R, :, :], h[b][R, :, :], spread(dinv[R, :], D), ALU.mult).then_inc(h_ready, 1)
                for k in range(UNITS):
                    q = UNITS * g + k
                    wait(dve, s_["multiplied"], q + 1)
                    v.tensor_tensor(ally[R, bass.ds(g * (G * D) + k * (SUB * D), SUB * D)].rearrange(
                        "p (t c) -> p t c", c=D),
                                    s_["p_y"][(b + k) % 2][R, 0:SUB * D].rearrange("p (t c) -> p t c", t=SUB),
                                    along(c["b3"][R, :], SUB), ALU.add).then_inc(y_ready, 1)
                st.end()
            over_groups(dve, body)

        @block.tensor
        def _(pe):
            def body(u, b, rows):
                g = 2 * u + b
                s_["b"] = b
                turn_and_multiply(nc, c, pe, s_, g, rows, h[b], D, h_ready, c["w3"], y_ready)
            over_groups(pe, body)

        @block.scalar
        def _(act):
            def body(u, b, rows):
                g = 2 * u + b
                R = slice(0, rows)
                wait(act, dm_ready, g + 1)
                nc.scalar.activation(root[R, :], dm[R, :], ACT.Sqrt).then_inc(rooted, 1)
                turn_copies(nc, act, s_, g, rows, D)
            over_groups(act, body)


def batch_statistics(nc, c, ally):
    CH = 15
    with ExitStack() as ctx:
        s = Scope(nc, ctx, "bn")
        part = s.sb("part", [P, 2, D])
        part2 = s.sb("part2", [P, CH + 1, D])
        square = [s.sb(f"square{k}", [P, G, D]) for k in range(2)]
        var, root, inv = (s.sb(n, [P, D]) for n in ("var", "root", "inv"))
        ps = s.ps([P, 512])
        stepped, parted, meaned, squared, reduced, vared, rooted = (
            s.sem(n) for n in ("stepped", "parted", "meaned", "squared", "reduced", "vared", "rooted"))
        centred = s.sem("centred")
        block = ctx.enter_context(nc.Block())
        chunks = [(P, k * G * D) for k in range(NG - 1)] + [(TAIL, (NG - 1) * G * D)]

        def chunk(k):
            rows, at = chunks[k]
            return ally[0:rows, at:at + G * D]

        def reduce_chunk(dve, k):
            rows = chunks[k][0]
            dve.wait_ge(squared, k + 1)
            nc.vector.tensor_reduce(part2[0:rows, k, :], square[k % 2][0:rows, :, :].rearrange("p t c -> p c t"), AX,
                                    ALU.add).then_inc(reduced, 1)

        @block.vector
        def _(dve):
            v = nc.vector
            main = (NG - 1) * G * D
            v.tensor_reduce(part[:, 0, :], ally[:, 0:main].rearrange("p (t c) -> p c t", c=D), AX,
                            ALU.add).then_inc(parted, 1)
            v.tensor_reduce(part[0:TAIL, 1, :], ally[0:TAIL, main:main + G * D].rearrange("p (t c) -> p c t", c=D),
                            AX, ALU.add).then_inc(parted, 1)
            dve.wait_ge(meaned, 1)
            v.tensor_scalar(c["mean"][:, :], ps[:, 0:D], 1.0 / N, None, ALU.mult).then_inc(stepped, 1)
            dve.wait_ge(stepped, 1)
            for k in range(NG):
                rows = chunks[k][0]
                y = chunk(k).rearrange("p (t c) -> p t c", c=D)
                v.tensor_tensor(y, y, along(c["mean"][0:rows, :], G), ALU.subtract).then_inc(centred, 1)
                if k:
                    reduce_chunk(dve, k - 1)
            reduce_chunk(dve, NG - 1)
            dve.wait_ge(vared, 1)
            v.tensor_scalar(var[:, :], ps[:, 64:64 + D], 1.0 / N, EPS, ALU.mult, ALU.add).then_inc(stepped, 1)
            dve.wait_ge(rooted, 1)
            v.reciprocal(inv[:, :], root[:, :]).then_inc(stepped, 1)
            dve.wait_ge(stepped, 3)
            v.tensor_tensor(c["scale3"][:, :], inv[:, :], c["gamma3"][:, :], ALU.mult).then_inc(stepped, 1)
            dve.wait_ge(stepped, 4)

        @block.scalar
        def _(act):
            for k in range(NG):
                rows = chunks[k][0]
                act.wait_ge(centred, k + 1)
                wait(act, reduced, k - 1)
                nc.scalar.activation(square[k % 2][0:rows, :, :].rearrange("p t c -> p (t c)"), chunk(k),
                                     ACT.Square).then_inc(squared, 1)
            act.wait_ge(stepped, 2)
            nc.scalar.activation(root[:, :], var[:, :], ACT.Sqrt).then_inc(rooted, 1)

        @block.tensor
        def _(pe):
            pe.wait_ge(parted, 2)
            nc.tensor.matmul(ps[:, 0:D], c["ones"][:, :], part[:, 0, :], start=True, stop=False)
            nc.tensor.matmul(ps[:, 0:D], c["ones"][0:TAIL, :], part[0:TAIL, 1, :], start=False,
                             stop=True).then_inc(meaned, 1)
            pe.wait_ge(reduced, NG)
            for k in range(NG):
                rows = chunks[k][0]
                last = nc.tensor.matmul(ps[:, 64:64 + D], c["ones"][0:rows, :], part2[0:rows, k, :],
                                        start=(k == 0), stop=(k == NG - 1))
            last.then_inc(vared, 1)


def finish(nc, c, d, ally):
    with ExitStack() as ctx:
        s = Scope(nc, ctx, "fin")
        x = [s.sb(f"x{b}", [P, G, D]) for b in range(2)]
        y = s.sb("y", [P, G, D])
        out = [s.sb(f"out{b}", [P, G, D]) for b in range(2)]
        norm = Norm(s, nc, "norm")
        loaded, stored = s.sems("loaded", 2), s.sems("stored", 2)
        stepped, built = s.sem("stepped"), s.sem("built")
        block = ctx.enter_context(nc.Block())

        @block.sync
        def _(sp):
            def body(u, b, rows):
                g = 2 * u + b
                wait(sp, built, g - 1)
                sp.dma_start(x[b][0:rows, :, :].rearrange("p t c -> p (t c)"),
                             group_rows(d["x3"], g, rows, D)).then_inc(loaded[b], 16)
            over_groups(sp, body)

        @block.vector
        def _(dve):
            v = nc.vector

            def body(u, b, rows):
                g = 2 * u + b
                R = slice(0, rows)
                st = Steps(dve, stepped, 3 + NORM_STEPS, g)
                st.did(v.tensor_tensor(y[R, :, :], ally[R, bass.ds(g * (G * D), G * D)].rearrange(
                    "p (t c) -> p t c", c=D), along(c["scale3"][R, :], G), ALU.mult))
                st.wait()
                st.did(v.tensor_tensor(y[R, :, :], y[R, :, :], along(c["beta3"][R, :], G), ALU.add))
                st.wait()
                wait(dve, loaded[b], 16 * (u + 1))
                st.did(v.scalar_tensor_tensor(y[R, :, :], y[R, :, :], 0.0, x[b][R, :, :], ALU.max, ALU.add))
                st.wait()
                wait(dve, stored[b], 16 * u)
                norm.vector(dve, st, g, rows, y[R, :, :], out[b][R, :, :]).then_inc(built, 1)
                st.end()
            over_groups(dve, body)

        @block.scalar
        def _(act):
            def body(u, b, rows):
                g = 2 * u + b
                norm.scalar(act, g, rows)
                wait(act, built, g + 1)
                act.dma_start(group_rows(d["out"], g, rows, D),
                              out[b][0:rows, :, :].rearrange("p t c -> p (t c)")).then_inc(stored[b], 16)
            over_groups(act, body)
            for b in range(2):
                act.wait_ge(stored[b], 16 * (PAIRS + 1))


def gnn_kernel(nc, d, upto=99):
    with ExitStack() as ctx:
        keep = Scope(nc, ctx, "keep")
        PSUM_OF[nc] = ctx.enter_context(nc.psum_tensor("psum", [P, 8, 512], F32))
        c = load_constants(nc, keep, d)
        ZEROS[nc] = c["zeros"]
        stages = [
            lambda: out_degree(nc, c, d, [d["sum0a"], d["sum0b"]]),
            lambda: first_table(nc, c, d),
            lambda: plain_edges(nc, c, d, "gcn", "table0", D + 2, ("sum0a", "sum0b"), D + 1,
                                (("sum1a", "sum1b"), D + 1), True),
            lambda: nodes0(nc, c, d),
            lambda: filter_edges(nc, c, d),
            lambda: nodes1(nc, c, d),
            lambda: relation_edges(nc, c, d),
            lambda: nodes2(nc, c, d),
            lambda: plain_edges(nc, c, d, "last", "table3", D, ("sum3a", "sum3b"), D, None, False),
        ]
        for f in stages[:upto]:
            f()
        if upto >= 99:
            ally = keep.sb("ally", [P, NG * G * D])
            nodes3(nc, c, d, ally)
            batch_statistics(nc, c, ally)
            finish(nc, c, d, ally)


SCRATCH_ROWS = P * 49 * 8


def declare(nc, arrays):
    dt = {"float32": F32, "int32": I32}
    d = {}
    for name, a in arrays.items():
        d[name] = nc.dram_tensor(f"in_{name}", a.shape, dt[a.dtype.name], kind="ExternalInput").ap()
    scratch = dict(outdeg=(RHIGH * RLOW,), indeg=(N,), srctype=(N,), table0=(N, D + 2), table1=(N, D + 2),
                   table2=(N, D), table3=(N, D), x3=(N, D))
    for i, w in enumerate((D + 1, D + 1, D, D)):
        scratch[f"sum{i}a"] = scratch[f"sum{i}b"] = (SCRATCH_ROWS, w)
    for name, shape in scratch.items():
        d[name] = nc.dram_tensor(f"tmp_{name}", shape, F32, kind="Internal").ap()
    d["out"] = nc.dram_tensor("out_0", (N, D), F32, kind="ExternalOutput").ap()
    return d


def lay_out(inputs):
    import numpy as np

    def tile_major(a):
        main = a[:TAIL0].reshape(NG - 1, P, G).transpose(0, 2, 1).reshape(-1)
        tail = a[TAIL0:].reshape(TAIL, G).T.reshape(-1)
        return np.concatenate([main, tail])

    i = {k: np.asarray(v) for k, v in inputs.items()}
    attr = i["edge_attr_40"]
    a = dict(
        x=i["x"], src=i["src"], dst=i["dst"], src_line=tile_major(i["src"]), dst_line=tile_major(i["dst"]),
        attr=attr[:TAIL0].reshape(NG - 1, P, G, NA).transpose(0, 3, 2, 1).reshape((NG - 1) * NA, FULL),
        attr_tail=attr[TAIL0:].reshape(TAIL, G, NA).transpose(2, 1, 0).reshape(NA, TAIL * G),
        rel=i["edge_type_8"], dist=i["edge_weight"], norm=i["edge_weight1"].reshape(-1), z=i["node_type_119"],
        mult=i["node_vec"], w0=i["L0_gnn_W"].T, w0b=i["L0_gnn_b"], f1=i["L1_gnn_W1"].T, f1b=i["L1_gnn_b1"],
        f2=i["L1_gnn_W2"].T, f2b=i["L1_gnn_b2"], embT=i["L1_gnn_emb"].T, adT=i["L1_gnn_adaptW"].T,
        gamma1=i["L1_gnn_gamma"], beta1=i["L1_gnn_beta"], r1=i["L2_gnn_weight1"], r2=i["L2_gnn_weight2"],
        rb1=i["L2_gnn_bias1"], rb2=i["L2_gnn_bias2"], w3=i["L3_gnn_W"], b3=i["L3_gnn_b"],
        gamma3=i["L3_gnn_gamma"], beta3=i["L3_gnn_beta"])
    return {k: np.ascontiguousarray(v) for k, v in a.items()}


def kernel(**inputs):
    import concourse.bacc as bacc
    from concourse.bass_utils import run_bass_kernel_spmd

    arrays = lay_out(inputs)
    nc = bacc.Bacc("TRN2", target_bir_lowering=False, num_devices=1)
    d = declare(nc, arrays)
    gnn_kernel(nc, d)
    r = run_bass_kernel_spmd(nc, [{f"in_{k}": v for k, v in arrays.items()}], core_ids=[0])
    return r.results[0]["out_0"]
```

```python
from contextlib import ExitStack

import concourse.bass as bass
from concourse import mybir

P = 128
N = 50000
D = 48
G = 25
SUB = 5
UNITS = G // SUB
FULL = P * G
NG = -(-N // FULL)
TAIL0 = (NG - 1) * FULL
TAIL = (N - TAIL0) // G
PAIRS = NG // 2 - 1
SLOTS = SUB
LAG = 3
NR = 8
RBITS = 9
RLOW = 1 << RBITS
RHIGH = -(-N // RLOW)
NZ = 119
NE = 32
NA = 40
EPS = 1e-5
CUTOFF = 6.0
PI = 3.141592653589793
FAR = -1e30
KX = D + NR + 1
KS = KX + D
CHUNKS = NR * D // P
assert TAIL * G == N - TAIL0 and NG % 2 == 0 and SUB * UNITS == G

F32 = mybir.dt.float32
F16 = mybir.dt.float16
BF16 = mybir.dt.bfloat16
I32 = mybir.dt.int32
ALU = mybir.AluOpType
ACT = mybir.ActivationFunctionType
AX = mybir.AxisListType.X


def over_groups(eng, body, peeled=1):
    for u in range(peeled):
        body(u, 0, P)
        body(u, 1, P)
    with eng.Fori(peeled, PAIRS) as u:
        body(u, 0, P)
        body(u, 1, P)
    body(PAIRS, 0, P)
    body(PAIRS, 1, TAIL)


def unit_before(u, b, rows, k):
    if k:
        return u, b, rows, k - 1
    if isinstance(u, int) and u == 0 and b == 0:
        return None
    return u if b else u - 1, 1 - b, P, UNITS - 1


def over_units(eng, early, late, begin=None):
    def body(u, b, rows):
        if begin is not None:
            begin(u, b, rows)
        for k in range(UNITS):
            early(u, b, rows, k)
            before = unit_before(u, b, rows, k)
            if before:
                late(*before)
    over_groups(eng, body)
    late(PAIRS, 1, TAIL, UNITS - 1)


def group_before(u, b, rows, lag):
    if isinstance(u, int):
        g = 2 * u + b - lag
        return (g // 2, g % 2, TAIL if g == NG - 1 else P) if 0 <= g < NG else None
    return ((u, b, rows), (u if b else u - 1, 1 - b, P), (u - 1, b, P))[lag]


def over_lagged(eng, steps):
    def body(u, b, rows):
        for lag, step in steps:
            at = group_before(u, b, rows, lag)
            if at:
                step(*at)
    over_groups(eng, body, peeled=2)
    for g in range(NG, NG + max(lag for lag, _ in steps)):
        body(g // 2, g % 2, P)


def wait(eng, sem, value):
    if not (isinstance(value, int) and value <= 0):
        eng.wait_ge(sem, value)


def hold(eng, sem, value, passed):
    if not (isinstance(value, int) and value <= 0):
        eng.wait_ge(sem, value)
        eng.sem_inc(passed, 1)


def group_rows(dram, g, rows, width=1):
    part = dram[bass.ds(g * FULL, FULL)] if rows == P else dram[TAIL0:N]
    if width == 1 and len(dram.shape) == 1:
        return part.rearrange("(p t) -> p t", t=G)
    return part.rearrange("(p t) c -> p (t c)", t=G)


def group_line(dram, g, rows):
    part = dram[bass.ds(g * FULL, FULL)] if rows == P else dram[TAIL0:N]
    return part.partition_broadcast(rows)


class Steps:

    def __init__(self, eng, sem, per, g):
        self.eng, self.sem, self.per, self.base, self.n = eng, sem, per, g * per, 0

    def did(self, ins):
        ins.then_inc(self.sem, 1)
        self.n += 1

    def wait(self):
        wait(self.eng, self.sem, self.base + self.n)

    def end(self):
        assert self.n == self.per, (self.n, self.per)


def spread(ap, n):
    return ap.unsqueeze(2).broadcast_to([ap.shape[0], ap.shape[1], n])


def along(ap, t):
    return ap.unsqueeze(1).broadcast_to([ap.shape[0], t, ap.shape[1]])


PSUM_OF = {}


class Scope:

    def __init__(self, nc, ctx, tag):
        self.nc, self.ctx, self.tag, self.bank, self.taken = nc, ctx, tag, 0, []
        ctx.callback(self.release)

    def sb(self, name, shape, dt=F32):
        return self.ctx.enter_context(self.nc.sbuf_tensor(f"{self.tag}_{name}", shape, dt))

    def ps(self, shape):
        n = shape[1] if len(shape) == 3 else 1
        part = PSUM_OF[self.nc][0:shape[0], self.bank:self.bank + n, 0:shape[-1]]
        self.bank += n
        assert self.bank <= 8
        return part if len(shape) == 3 else part.rearrange("p b c -> p (b c)")

    def sem(self, name):
        self.taken.append(self.nc.alloc_semaphore(f"{self.tag}_{name}"))
        return self.taken[-1]

    def release(self):
        if self.taken:
            self.nc.clear_and_free_semaphores(self.taken)
            self.nc.all_engine_barrier()

    def sems(self, name, n):
        return [self.sem(f"{name}{i}") for i in range(n)]



def load_constants(nc, keep, d):
    c = {}
    spec = dict(ident=[P, P], before=[P, P], ones=[P, P], spare=[P, 1], w0=[2 * (D + 1), 2 * D], f1=[NA, D],
                f1b=[D, 1], f2=[D + 1, D], embT=[NE, NZ], adT=[NE, NE], ejT=[NE, NZ], pairs=[NZ, NZ],
                gamma1=[P, D], beta1=[P, D], r1=[KS, NR * D], rest=[KS, NR * D], r2=[P, CHUNKS, D], rb2=[P, D],
                w3=[2 * (D + 1), 2 * D], gamma3=[P, D], beta3=[P, D], farm=[NR, NR * D], zline=[P, NZ],
                rline=[P, NR], mean=[P, D], scale3=[P, D])
    for name, shape in spec.items():
        c[name] = keep.sb(name, shape)
    c["lows"] = keep.sb("lows", [P, RLOW], F16)
    c["highs"] = keep.sb("highs", [P, RHIGH], F16)
    c["identb"] = keep.sb("identb", [P, P], BF16)
    for name in ("r1a", "r1b", "r1c"):
        c[name] = keep.sb(name, [KS, NR * D], BF16)
    c["zeros"] = keep.sb("zeros", [P, 49 * 49])
    with ExitStack() as ctx:
        s = Scope(nc, ctx, "const")
        landed, shaped, made, multiplied, copied = (s.sem(x) for x in
                                                    ("landed", "shaped", "made", "multiplied", "copied"))
        placed, split, emptied = s.sem("placed"), s.sem("split"), s.sem("emptied")
        pt = s.ps([P, 512])
        block = ctx.enter_context(nc.Block())
        loads = [("f1", d["f1"]), ("f1b", d["f1b"].unsqueeze(1)),
                 ("embT", d["embT"]), ("adT", d["adT"]),
                 ("gamma1", d["gamma1"].partition_broadcast(P)), ("beta1", d["beta1"].partition_broadcast(P)),
                 ("rb2", d["rb2"].partition_broadcast(P)), ("gamma3", d["gamma3"].partition_broadcast(P)),
                 ("beta3", d["beta3"].partition_broadcast(P))]

        N_LOADS = len(loads) + 11 + 3 * NR

        @block.sync
        def _(sp):
            for name, src in loads:
                sp.dma_start(c[name][:, :], src).then_inc(landed, 16)
            sp.wait_ge(emptied, 2)
            for name, block in (("f2", 0), ("w0", 0), ("w0", 1), ("w3", 0), ("w3", 1)):
                top, cols = block * (D + 1), slice(block * D, (block + 1) * D)
                sp.dma_start(c[name][top:top + D, cols], d[name]).then_inc(landed, 16)
                sp.dma_start(c[name][top + D:top + D + 1, cols], d[name + "b"].unsqueeze(0)).then_inc(landed, 16)
            sp.dma_start(c["r2"][:, :, :], d["r2"].rearrange("r j o -> (r j) o").rearrange("(q a) o -> a q o", a=P)).then_inc(landed, 16)
            for r in range(NR):
                sp.dma_start(c["r1"][0:D, r * D:(r + 1) * D], d["r1"][r]).then_inc(landed, 16)
                sp.dma_start(c["r1"][KX:KS, r * D:(r + 1) * D], d["r1"][r]).then_inc(landed, 16)
                sp.dma_start(c["r1"][KX - 1:KX, r * D:(r + 1) * D],
                             d["rb1"].unsqueeze(0)).then_inc(landed, 16)
            sp.wait_ge(shaped, 7)
            sp.dma_start(c["r1"][D:D + NR, :], c["farm"][:, :]).then_inc(placed, 16)
            sp.wait_ge(split, 5)
            sp.dma_start(c["r1c"][KX:KS, :], c["r1a"][KX:KS, :]).then_inc(placed, 16)
            sp.wait_ge(placed, 32)

        @block.vector
        def _(dve):
            v = nc.vector
            dve.wait_ge(landed, 16 * N_LOADS)
            dve.wait_ge(placed, 16)
            v.tensor_copy(c["r1a"][:, :], c["r1"][:, :]).then_inc(split, 1)
            dve.wait_ge(split, 1)
            v.tensor_tensor(c["rest"][:, :], c["r1"][:, :], c["r1a"][:, :], ALU.subtract).then_inc(split, 1)
            dve.wait_ge(split, 2)
            v.tensor_copy(c["r1b"][:, :], c["rest"][:, :]).then_inc(split, 1)
            dve.wait_ge(split, 3)
            v.tensor_tensor(c["r1c"][:, :], c["rest"][:, :], c["r1b"][:, :], ALU.subtract).then_inc(split, 1)
            dve.wait_ge(shaped, 6)
            v.tensor_copy(c["identb"][:, :], c["ident"][:, :]).then_inc(split, 1)

        @block.gpsimd
        def _(pool):
            g = nc.gpsimd
            g.memset(c["w0"][:, :], 0.0).then_inc(emptied, 1)
            g.memset(c["w3"][:, :], 0.0).then_inc(emptied, 1)
            g.memset(c["ones"][:, :], 1.0).then_inc(made, 1)
            g.memset(c["zeros"][:, :], 0.0).then_inc(made, 1)
            g.memset(c["farm"][:, :], 0.0).then_inc(made, 1)
            g.iota(c["spare"][:, :], [[1, 1]], base=N, channel_multiplier=1,
                   allow_small_or_imprecise_dtypes=True).then_inc(shaped, 1)
            g.iota(c["lows"][:, :], [[1, RLOW]], base=0, channel_multiplier=0,
                   allow_small_or_imprecise_dtypes=True).then_inc(shaped, 1)
            g.iota(c["highs"][:, :], [[1, RHIGH]], base=0, channel_multiplier=0,
                   allow_small_or_imprecise_dtypes=True).then_inc(shaped, 1)
            g.iota(c["zline"][:, :], [[1, NZ]], base=0, channel_multiplier=0,
                   allow_small_or_imprecise_dtypes=True).then_inc(shaped, 1)
            g.iota(c["rline"][:, :], [[1, NR]], base=0, channel_multiplier=0,
                   allow_small_or_imprecise_dtypes=True).then_inc(shaped, 1)
            pool.wait_ge(made, 3)
            g.affine_select(out=c["ident"][:, :], in_=c["zeros"][:, 0:P], compare_op=ALU.not_equal, fill=1.0,
                            base=0, pattern=[[-1, P]], channel_multiplier=1).then_inc(shaped, 1)
            g.affine_select(out=c["farm"][:, :].rearrange("p (r j) -> p r j", r=NR),
                            in_=c["farm"][:, :].rearrange("p (r j) -> p r j", r=NR),
                            compare_op=ALU.not_equal, fill=FAR, base=0, pattern=[[-1, NR], [0, D]],
                            channel_multiplier=1).then_inc(shaped, 1)
            g.affine_select(out=c["before"][:, :], in_=c["ones"][:, :], compare_op=ALU.is_gt, fill=0.0,
                            base=0, pattern=[[-1, P]], channel_multiplier=1).then_inc(shaped, 1)
            pool.wait_ge(shaped, 8)

        @block.tensor
        def _(pe):
            pe.wait_ge(landed, 16 * N_LOADS)
            nc.tensor.matmul(pt[0:NE, 0:NZ], c["adT"][:, :], c["embT"][:, :], start=True,
                             stop=True).then_inc(multiplied, 1)
            pe.wait_ge(copied, 1)
            nc.tensor.matmul(pt[0:NZ, 128:128 + NZ], c["ejT"][:, :], c["embT"][:, :], start=True,
                             stop=True).then_inc(multiplied, 1)

        @block.scalar
        def _(act):
            act.wait_ge(multiplied, 1)
            nc.scalar.activation(c["ejT"][:, :], pt[0:NE, 0:NZ], ACT.Copy).then_inc(copied, 1)
            act.wait_ge(multiplied, 2)
            nc.scalar.activation(c["pairs"][:, :], pt[0:NZ, 128:128 + NZ], ACT.Copy).then_inc(copied, 1)
            act.wait_ge(copied, 2)
    return c



def clear_sums(nc, eng, sums, width, cleared):
    n = 0
    for copy in sums:
        rows = copy.rearrange("(k p q) c -> k p (q c)", p=P, q=49)
        for k in range(rows.shape[0]):
            eng.dma_start(rows[k], ZEROS[nc][:, 0:49 * width]).then_inc(cleared, 16)
            n += 16
    return n


ZEROS = {}


def out_degree(nc, c, d, sums0):
    with ExitStack() as ctx:
        s = Scope(nc, ctx, "deg")
        key = [s.sb(f"key{b}", [P, G], I32) for b in range(2)]
        part = s.sb("part", [P, 2, G], I32)
        partf = [s.sb(f"partf{b}", [P, 2, G]) for b in range(2)]
        low = [s.sb(f"low{k}", [P, SUB, RLOW], BF16) for k in range(2)]
        high = [s.sb(f"high{k}", [P, SUB, RHIGH], BF16) for k in range(2)]
        count = s.sb("count", [RHIGH, RLOW])
        ps = s.ps([RHIGH, RLOW])
        loaded = s.sems("loaded", 2)
        stepped, hot, used, counted, copied, stored, cleared = (
            s.sem(x) for x in ("stepped", "hot", "used", "counted", "copied", "stored", "cleared"))
        block = ctx.enter_context(nc.Block())

        @block.sync
        def _(sp):
            def body(u, b, rows):
                g = 2 * u + b
                wait(sp, stepped, 4 * (g - 1))
                sp.dma_start(key[b][0:rows, :], group_rows(d["src"], g, rows)).then_inc(loaded[b], 16)
            over_groups(sp, body)
            sp.wait_ge(copied, 1)
            sp.dma_start(d["outdeg"].rearrange("(h l) -> h l", l=RLOW), count[:, :]).then_inc(stored, 16)
            sp.wait_ge(stored, 16)

        @block.scalar
        def _(act):
            n = clear_sums(nc, act, sums0, 49, cleared)
            act.wait_ge(cleared, n)

        @block.vector
        def _(dve):
            v = nc.vector

            def body(u, b, rows):
                g = 2 * u + b
                st = Steps(dve, stepped, 4, g)
                wait(dve, loaded[b], 16 * (u + 1))
                st.did(v.tensor_scalar(part[0:rows, 0, :], key[b][0:rows, :], RBITS, None,
                                       ALU.logical_shift_right))
                st.did(v.tensor_scalar(part[0:rows, 1, :], key[b][0:rows, :], RLOW - 1, None, ALU.bitwise_and))
                st.wait()
                wait(dve, used, 5 * (g - 1))
                st.did(v.tensor_copy(partf[b][0:rows, 0, :], part[0:rows, 0, :]))
                st.did(v.tensor_copy(partf[b][0:rows, 1, :], part[0:rows, 1, :]))
                st.wait()
                for k in range(UNITS):
                    r = (b + k) % 2
                    wait(dve, used, 5 * g + k - 1)
                    for t in range(SUB):
                        col = SUB * k + t
                        v.tensor_scalar(high[r][0:rows, t, :], c["highs"][0:rows, :],
                                        partf[b][0:rows, 0, col:col + 1], None, ALU.is_equal)
                        last = v.tensor_scalar(low[r][0:rows, t, :], c["lows"][0:rows, :],
                                               partf[b][0:rows, 1, col:col + 1], None, ALU.is_equal)
                    last.then_inc(hot, 1)
                st.end()
            over_groups(dve, body)
            dve.wait_ge(counted, 1)
            v.tensor_copy(count[:, :], ps[:, :]).then_inc(copied, 1)

        @block.tensor
        def _(pe):
            def body(u, b, rows):
                g = 2 * u + b
                for k in range(UNITS):
                    r = (b + k) % 2
                    wait(pe, hot, 5 * g + k + 1)
                    for t in range(SUB):
                        first = isinstance(u, int) and u == 0 and b == 0 and k == 0 and t == 0
                        end = rows == TAIL and k == UNITS - 1 and t == SUB - 1
                        last = nc.tensor.matmul(ps[:, :], high[r][0:rows, t, :], low[r][0:rows, t, :],
                                                start=first, stop=end)
                    last.then_inc(used, 1)
            over_groups(pe, body)
            pe.wait_ge(used, UNITS * NG)
            pe.sem_inc(counted, 1)


def first_table(nc, c, d):
    with ExitStack() as ctx:
        s = Scope(nc, ctx, "t0")
        x = [s.sb(f"x{b}", [P, G * D]) for b in range(2)]
        deg = [s.sb(f"deg{b}", [P, G]) for b in range(2)]
        z = [s.sb(f"z{b}", [P, G], I32) for b in range(2)]
        row = [s.sb(f"row{b}", [P, G, D + 2]) for b in range(2)]
        dm = s.sb("dm", [P, G])
        root = s.sb("root", [P, G])
        ci = s.sb("ci", [P, G])
        loaded, stored = s.sems("loaded", 2), s.sems("stored", 2)
        stepped, rooted, built = s.sem("stepped"), s.sem("rooted"), s.sem("built")
        block = ctx.enter_context(nc.Block())

        @block.sync
        def _(sp):
            def body(u, b, rows):
                g = 2 * u + b
                wait(sp, built, g - 1)
                sp.dma_start(x[b][0:rows, :], group_rows(d["x"], g, rows, D)).then_inc(loaded[b], 16)
                sp.dma_start(deg[b][0:rows, :], group_rows(d["outdeg"], g, rows)).then_inc(loaded[b], 16)
                sp.dma_start(z[b][0:rows, :], group_rows(d["z"], g, rows)).then_inc(loaded[b], 16)
            over_groups(sp, body)

        @block.vector
        def _(dve):
            v = nc.vector

            def body(u, b, rows):
                g = 2 * u + b
                st = Steps(dve, stepped, 4, g)
                R = slice(0, rows)
                wait(dve, loaded[b], 48 * (u + 1))
                st.did(v.tensor_scalar_max(dm[R, :], deg[b][R, :], 1.0))
                wait(dve, stored[b], 16 * u)
                st.did(v.tensor_copy(row[b][R, :, D + 1], z[b][R, :]))
                st.did(v.tensor_copy(row[b][R, :, D], c["ones"][R, 0:G]))
                wait(dve, rooted, g + 1)
                st.did(v.reciprocal(ci[R, :], root[R, :]))
                st.wait()
                v.tensor_tensor(row[b][R, :, 0:D], x[b][R, :].rearrange("p (t c) -> p t c", c=D),
                                spread(ci[R, :], D), ALU.mult).then_inc(built, 1)
                st.end()
            over_groups(dve, body)

        @block.scalar
        def _(act):
            def body(u, b, rows):
                g = 2 * u + b
                R = slice(0, rows)
                wait(act, stepped, 4 * g + 1)
                nc.scalar.activation(root[R, :], dm[R, :], ACT.Sqrt).then_inc(rooted, 1)
                wait(act, built, g + 1)
                act.dma_start(group_rows(d["table0"], g, rows, D + 2),
                              row[b][R, :, :].rearrange("p t c -> p (t c)")).then_inc(stored[b], 16)
            over_groups(act, body)
            act.wait_ge(stored[0], 16 * (PAIRS + 1))
            act.wait_ge(stored[1], 16 * (PAIRS + 1))


class EdgeStage:

    def __init__(self, nc, ctx, c, d, tag, *, table, width, source, target, sums, out_width, clear):
        self.nc, self.c, self.d = nc, c, d
        self.table, self.width, self.sums, self.out_width = d[table], width, [d[x] for x in sums], out_width
        self.source, self.target, self.clear = source, target, clear
        s = self.s = Scope(nc, ctx, tag)
        self.take = [s.sb(f"take{b}", [P, G], I32) for b in range(2)]
        self.key = [s.sb(f"key{b}", [P, G], I32) for b in range(2)]
        self.line = [s.sb(f"line{b}", [P, FULL], I32) for b in range(2)]
        self.keyf = [s.sb(f"keyf{b}", [P, G]) for b in range(2)]
        self.keyd = [s.sb(f"keyd{b}", [P, G]) for b in range(2)]
        self.put = [s.sb(f"put{b}", [P, G], I32) for b in range(2)]
        self.same = [s.sb(f"same{k}", [P, SUB * P]) for k in range(SLOTS)]
        self.earlier = s.sb("earlier", [P, SUB, P])
        self.nearlier = s.sb("nearlier", [P, SUB])
        self.putd = s.sb("putd", [P, SUB])
        self.total = [s.sb(f"total{k}", [P, SUB, out_width]) for k in range(SLOTS)]
        self.psum = s.ps([P, 512])
        self.take_loaded = s.sems("take_loaded", 2)
        self.keys_loaded = s.sems("keys_loaded", 2)
        self.gathered = s.sems("gathered", SLOTS)
        self.added = s.sems("added", 2)
        self.put_ready = s.sem("put_ready")
        self.same_ready = s.sem("same_ready")
        self.summed = s.sem("summed")
        self.total_ready = s.sem("total_ready")
        self.keyed = s.sem("keyed")
        self.passed = s.sem("passed")
        self.cleared = s.sem("cleared")

    def load_indices(self, sp, u, b, rows):
        g = 2 * u + b
        wait(sp, self.gathered[SLOTS - 1], 16 * SUB * (g - 1))
        sp.dma_start(self.take[b][0:rows, :], group_rows(self.d[self.source], g, rows)).then_inc(
            self.take_loaded[b], 16)
        wait(sp, self.put_ready, UNITS * (g - 1))
        sp.dma_start(self.key[b][0:rows, :], group_rows(self.d[self.target], g, rows)).then_inc(
            self.keys_loaded[b], 16)
        sp.dma_start(self.line[b][0:rows, 0:rows * G], group_line(self.d[self.target + "_line"], g, rows)).then_inc(
            self.keys_loaded[b], 16)

    def before_gather(self, pool, u, b, rows, k, freed):
        g = 2 * u + b
        if k == 0:
            hold(pool, self.take_loaded[b], 16 * (u + 1), self.passed)
        hold(pool, freed, UNITS * g + k - (SLOTS - 1), self.passed)

    def gather(self, b, rows, k, t, into):
        col = SUB * k + t
        self.nc.gpsimd.indirect_dma_start(
            out=into[k][0:rows, t, 0:self.width], out_offset=None, in_=self.table,
            in_offset=bass.IndirectOffsetOnAxis(ap=self.take[b][0:rows, col:col + 1], axis=0),
        ).then_inc(self.gathered[k], 16)

    def before_scatter(self, pool, u, b, rows, k):
        g = 2 * u + b
        hold(pool, self.put_ready, UNITS * g + k + 1, self.passed)
        hold(pool, self.total_ready, UNITS * g + k + 1, self.passed)

    def scatter(self, pool, u, b, rows, k, t):
        col = SUB * k + t
        copy = (b + col) % 2
        hold(pool, self.added[copy], 16 * (G * u + (G * b + col) // 2), self.passed)
        self.nc.gpsimd.indirect_dma_start(
            out=self.sums[copy], in_=self.total[k][0:rows, t, :], in_offset=None,
            out_offset=bass.IndirectOffsetOnAxis(ap=self.put[b][0:rows, col:col + 1], axis=0),
            compute_op=ALU.add).then_inc(self.added[copy], 16)

    def pool_program(self, pool, into, freed, lag=LAG):
        def body(u, b, rows):
            first = isinstance(u, int) and u == 0 and b == 0
            for k in range(UNITS):
                if k >= lag:
                    late = (u, b, rows, k - lag)
                elif not first:
                    late = (u if b else u - 1, 1 - b, P, k - lag + UNITS)
                else:
                    late = None
                self.before_gather(pool, u, b, rows, k, freed)
                self.gather(b, rows, k, 0, into)
                if late:
                    self.before_scatter(pool, *late)
                for t in range(SUB):
                    if t:
                        self.gather(b, rows, k, t, into)
                    if late:
                        self.scatter(pool, *late, t)
        over_groups(pool, body)
        for k in range(UNITS - lag, UNITS):
            self.before_scatter(pool, PAIRS, 1, TAIL, k)
            for t in range(SUB):
                self.scatter(pool, PAIRS, 1, TAIL, k, t)
        for copy in range(2):
            pool.wait_ge(self.added[copy], 16 * G * NG // 2)

    KEY_STEPS = 2 + 4 * UNITS

    def key_group(self, dve, st, u, b, rows):
        g = 2 * u + b
        v, R = self.nc.vector, slice(0, rows)
        wait(dve, self.keys_loaded[b], 32 * (u + 1))
        st.did(v.tensor_copy(self.keyf[b][R, :], self.key[b][R, :]))
        st.wait()
        st.did(v.tensor_scalar(self.keyd[b][R, :], self.keyf[b][R, :], self.c["spare"][R, 0:1], None, ALU.subtract))
        st.wait()
        for copy in range(2):
            wait(dve, self.added[copy], 16 * (G * u + (G * (b - 1) + 1 - copy) // 2))

    def same_unit(self, dve, st, u, b, rows, k):
        g = 2 * u + b
        v, R = self.nc.vector, slice(0, rows)
        wait(dve, self.summed, UNITS * g + k - (SLOTS - 1))
        for t in range(SUB):
            col = SUB * k + t
            last = v.tensor_scalar(self.same[k][R, t * rows:(t + 1) * rows],
                                   self.line[b][R, col * rows:(col + 1) * rows],
                                   self.keyf[b][R, col:col + 1], None, ALU.is_equal)
        last.then_inc(self.same_ready, 1)
        wait(dve, self.same_ready, UNITS * g + k + 1)
        cols = slice(SUB * k, SUB * (k + 1))
        st.did(v.tensor_tensor(self.earlier[R, :, R], self.same[k][R, 0:SUB * rows].rearrange("p (t e) -> p t e", t=SUB),
                               along(self.c["before"][R, R], SUB), ALU.mult))
        st.wait()
        st.did(v.tensor_reduce(self.nearlier[R, :], self.earlier[R, :, R], AX, ALU.add))
        st.wait()
        st.did(v.tensor_scalar(self.nearlier[R, :], self.nearlier[R, :], 0.0, None, ALU.is_equal))
        st.wait()
        st.did(v.tensor_tensor(self.putd[R, :], self.nearlier[R, :], self.keyd[b][R, cols], ALU.mult))
        st.wait()
        v.tensor_scalar(self.put[b][R, cols], self.putd[R, :], self.c["spare"][R, 0:1], None,
                        ALU.add).then_inc(self.put_ready, 1)

    def sum_unit(self, pe, u, b, rows, k, messages):
        g = 2 * u + b
        W, R = self.out_width, slice(0, rows)
        wait(pe, self.same_ready, UNITS * g + k + 1)
        wait(pe, self.total_ready, UNITS * g + k)
        for t in range(SUB):
            last = self.nc.tensor.matmul(self.psum[R, t * W:(t + 1) * W], self.same[k][R, t * rows:(t + 1) * rows],
                                         messages[R, t, 0:W], start=True, stop=True)
        last.then_inc(self.summed, 1)

    def copy_unit(self, act, u, b, rows, k):
        g = 2 * u + b
        R = slice(0, rows)
        wait(act, self.summed, UNITS * g + k + 1)
        J = G * b + SUB * k + SUB - G
        for copy in range(2):
            wait(act, self.added[copy], 16 * (G * u + (J + 1 - copy) // 2))
        self.nc.scalar.activation(self.total[k][R, :, :].rearrange("p t c -> p (t c)"),
                                  self.psum[R, 0:SUB * self.out_width], ACT.Copy).then_inc(self.total_ready, 1)

    def clear_next(self, act):
        if self.clear is None:
            return 0
        names, width = self.clear
        return clear_sums(self.nc, act, [self.d[x] for x in names], width, self.cleared)


def plain_edges(nc, c, d, tag, table, width, sums, out_width, clear, types):
    with ExitStack() as ctx:
        e = EdgeStage(nc, ctx, c, d, tag, table=table, width=width, source="src", target="dst", sums=sums,
                      out_width=out_width, clear=clear)
        rows_of = [e.s.sb(f"rows{k}", [P, SUB, width]) for k in range(SLOTS)]
        kind = [e.s.sb(f"kind{b}", [P, G]) for b in range(2)]
        kind_taken = e.s.sem("kind_taken")
        kind_stored = e.s.sems("kind_stored", 2)
        block = ctx.enter_context(nc.Block())

        @block.sync
        def _(sp):
            over_groups(sp, lambda u, b, rows: e.load_indices(sp, u, b, rows))

        @block.gpsimd
        def _(pool):
            e.pool_program(pool, rows_of, e.total_ready)

        @block.vector
        def _(dve):
            def body(u, b, rows):
                st = Steps(dve, e.keyed, e.KEY_STEPS, 2 * u + b)
                e.key_group(dve, st, u, b, rows)
                for k in range(UNITS):
                    e.same_unit(dve, st, u, b, rows, k)
                st.end()
            over_groups(dve, body)

        @block.tensor
        def _(pe):
            def body(u, b, rows):
                for k in range(UNITS):
                    wait(pe, e.gathered[k], 16 * SUB * (2 * u + b + 1))
                    e.sum_unit(pe, u, b, rows, k, rows_of[k])
            over_groups(pe, body)

        @block.scalar
        def _(act):
            n = e.clear_next(act)

            def body(u, b, rows):
                g = 2 * u + b
                if types:
                    wait(act, kind_stored[b], 16 * u)
                for k in range(UNITS):
                    if types:
                        wait(act, e.gathered[k], 16 * SUB * (g + 1))
                        nc.scalar.activation(kind[b][0:rows, SUB * k:SUB * (k + 1)],
                                             rows_of[k][0:rows, :, width - 1], ACT.Copy).then_inc(kind_taken, 1)
                    e.copy_unit(act, u, b, rows, k)
                if types:
                    wait(act, kind_taken, UNITS * (g + 1))
                    act.dma_start(group_rows(d["srctype"], g, rows), kind[b][0:rows, :]).then_inc(kind_stored[b], 16)
            over_groups(act, body)
            if types:
                for b in range(2):
                    act.wait_ge(kind_stored[b], 16 * (PAIRS + 1))
            wait(act, e.cleared, n)


def filter_edges(nc, c, d):
    W1 = D + 2
    A, B = 3, SUB - 3
    with ExitStack() as ctx:
        e = EdgeStage(nc, ctx, c, d, "flt", table="table1", width=W1, source="dst", target="src",
                      sums=("sum1a", "sum1b"), out_width=D + 1, clear=(("sum2a", "sum2b"), D))
        s = e.s
        rows_of = [s.sb(f"rows{k}", [P, SUB, W1]) for k in range(SLOTS)]
        attr = [s.sb(f"attr{b}", [NA, FULL]) for b in range(2)]
        dist = [s.sb(f"dist{b}", [P, G]) for b in range(2)]
        kind = [s.sb(f"kind{b}", [P, G]) for b in range(2)]
        near = s.sb("near", [P, G])
        sine = s.sb("sine", [P, G])
        inside = s.sb("inside", [P, G])
        cut = [s.sb(f"cut{b}", [P, G]) for b in range(2)]
        hot_d = s.sb("hot_d", [P, SUB, NZ])
        hot_s = s.sb("hot_s", [P, SUB, NZ])
        hot_dT = s.sb("hot_dT", [NZ, SUB * P])
        hidden = s.sb("hidden", [D + 1, SUB * P])
        picked = s.sb("picked", [P, SUB, NZ])
        logit = s.sb("logit", [P, SUB])
        weight = s.sb("weight", [P, SUB])
        hw = s.sb("hw", [P, SUB, D])
        gated = s.sb("gated", [P, SUB, D])
        message = [s.sb(f"message{k}", [P, SUB, D + 1]) for k in range(2)]
        p_hidden = s.ps([P, 2, 512])
        p_hot = s.ps([P, 2, 512])
        p_pair = s.ps([P, 2, 512])
        p_gate = s.ps([P, 512])
        linear_loaded = s.sems("linear_loaded", 2)
        pe_passed = s.sem("pe_passed")
        near_ready, sine_ready, hot_ready, hidden_mult, hidden_ready = (
            s.sem(x) for x in ("near_ready", "sine_ready", "hot_ready", "hidden_mult", "hidden_ready"))
        turned, turned_copied, pair_ready, gate_ready, message_ready = (
            s.sem(x) for x in ("turned", "turned_copied", "pair_ready", "gate_ready", "message_ready"))
        messaged, prepared, ones_placed = s.sem("messaged"), s.sem("prepared"), s.sem("ones_placed")
        block = ctx.enter_context(nc.Block())

        @block.sync
        def _(sp):
            sp.dma_start(hidden[D:D + 1, :].rearrange("p (t e) -> p t e", t=SUB),
                         along(c["ones"][0:1, :], SUB)).then_inc(ones_placed, 16)

            def body(u, b, rows):
                g = 2 * u + b
                e.load_indices(sp, u, b, rows)
                wait(sp, message_ready, UNITS * (g - 1))
                wait(sp, gate_ready, UNITS * (g - 1))
                if rows == P:
                    sp.dma_start(attr[b][:, :], d["attr"][bass.ds(g * NA, NA), :]).then_inc(linear_loaded[b], 16)
                else:
                    sp.dma_start(attr[b][:, 0:rows * G], d["attr_tail"]).then_inc(linear_loaded[b], 16)
                sp.dma_start(dist[b][0:rows, :], group_rows(d["dist"], g, rows)).then_inc(linear_loaded[b], 16)
                sp.dma_start(kind[b][0:rows, :], group_rows(d["srctype"], g, rows)).then_inc(linear_loaded[b], 16)
            over_groups(sp, body)

        @block.gpsimd
        def _(pool):
            e.pool_program(pool, rows_of, message_ready)

        @block.vector
        def _(dve):
            v = nc.vector

            steps = [None]

            def begin(u, b, rows):
                g = 2 * u + b
                R = slice(0, rows)
                st = steps[0] = Steps(dve, e.keyed, e.KEY_STEPS + 4, g)
                e.key_group(dve, st, u, b, rows)
                wait(dve, linear_loaded[b], 48 * (u + 1))
                v.tensor_scalar(near[R, :], dist[b][R, :], CUTOFF, PI / (2 * CUTOFF), ALU.min,
                                ALU.mult).then_inc(near_ready, 1)
                st.did(v.tensor_scalar(inside[R, :], dist[b][R, :], CUTOFF, None, ALU.is_lt))
                wait(dve, sine_ready, g + 1)
                st.did(v.tensor_tensor(cut[b][R, :], sine[R, :], sine[R, :], ALU.mult))
                st.wait()
                st.did(v.tensor_scalar(cut[b][R, :], cut[b][R, :], -1.0, 1.0, ALU.mult, ALU.add))
                st.wait()
                st.did(v.tensor_tensor(cut[b][R, :], cut[b][R, :], inside[R, :], ALU.mult))

            def hot_rows(u, b, rows, k):
                q = UNITS * (2 * u + b) + k
                R = slice(0, rows)
                wait(dve, e.gathered[k], 16 * SUB * (2 * u + b + 1))
                wait(dve, turned, q)
                v.tensor_tensor(hot_d[R, :, :], spread(rows_of[k][R, :, W1 - 1], NZ), along(c["zline"][R, :], SUB),
                                ALU.is_equal).then_inc(hot_ready, 1)

            def messages(u, b, rows, k):
                q = UNITS * (2 * u + b) + k
                R = slice(0, rows)
                st = Steps(dve, messaged, 5, q)
                wait(dve, pair_ready, q + 1)
                wait(dve, prepared, 3 * (q + 1))
                st.did(v.tensor_tensor(picked[R, 0:A, :], p_pair[R, 0, 0:A * NZ].rearrange("p (t z) -> p t z", t=A),
                                       hot_s[R, 0:A, :], ALU.mult))
                st.did(v.tensor_tensor(picked[R, A:SUB, :], p_pair[R, 1, 0:B * NZ].rearrange("p (t z) -> p t z", t=B),
                                       hot_s[R, A:SUB, :], ALU.mult))
                st.wait()
                st.did(v.tensor_reduce(logit[R, :], picked[R, :, :], AX, ALU.add))
                st.wait()
                wait(dve, gate_ready, q + 1)
                st.did(v.tensor_tensor(gated[R, :, :], p_gate[R, 0:SUB * D].rearrange("p (t c) -> p t c", t=SUB),
                                       spread(logit[R, :], D), ALU.add))
                m = message[(b + k) % 2]
                wait(dve, e.summed, q - 1)
                st.did(v.tensor_copy(m[R, :, D], rows_of[k][R, :, D]))
                st.wait()
                st.end()
                v.tensor_tensor(m[R, :, 0:D], gated[R, :, :], hw[R, :, :], ALU.mult).then_inc(message_ready, 1)

            def prepare(u, b, rows, k):
                q = UNITS * (2 * u + b) + k
                R = slice(0, rows)
                cols = slice(SUB * k, SUB * (k + 1))
                wait(dve, e.keyed, (2 * u + b) * steps[0].per + steps[0].n)
                wait(dve, message_ready, q)
                v.tensor_tensor(hot_s[R, :, :], spread(kind[b][R, cols], NZ), along(c["zline"][R, :], SUB),
                                ALU.is_equal).then_inc(prepared, 1)
                v.tensor_tensor(weight[R, :], cut[b][R, cols], rows_of[k][R, :, D], ALU.mult).then_inc(prepared, 1)
                wait(dve, prepared, 3 * q + 2)
                v.tensor_tensor(hw[R, :, :], rows_of[k][R, :, 0:D], spread(weight[R, :], D),
                                ALU.mult).then_inc(prepared, 1)

            def body(u, b, rows):
                begin(u, b, rows)
                for k in range(UNITS):
                    hot_rows(u, b, rows, k)
                    before = unit_before(u, b, rows, k)
                    if before:
                        messages(*before)
                    prepare(u, b, rows, k)
                    e.same_unit(dve, steps[0], u, b, rows, k)
                steps[0].end()
            over_groups(dve, body)
            messages(PAIRS, 1, TAIL, UNITS - 1)

        @block.tensor
        def _(pe):
            pe.wait_ge(ones_placed, 16)

            def turn(u, b, rows, k):
                q = UNITS * (2 * u + b) + k
                R = slice(0, rows)
                wait(pe, hot_ready, q + 1)
                wait(pe, turned_copied, q)
                for t in range(SUB):
                    bank, o = (0, t) if t < A else (1, t - A)
                    last = nc.tensor.transpose(p_hot[0:NZ, bank, o * rows:(o + 1) * rows], hot_d[R, t, :],
                                               c["ident"][R, R])
                last.then_inc(turned, 1)

            def products(u, b, rows, k):
                q = UNITS * (2 * u + b) + k
                R = slice(0, rows)
                hold(pe, linear_loaded[b], 48 * (u + 1), pe_passed)
                hold(pe, hidden_ready, q, pe_passed)
                for bank, t0, n in ((0, 0, A), (1, A, B)):
                    at = (SUB * k + t0) * rows
                    last = nc.tensor.matmul(p_hidden[0:D, bank, 0:n * rows], c["f1"][:, :],
                                            attr[b][:, at:at + n * rows], start=True, stop=True)
                last.then_inc(hidden_mult, 1)
                wait(pe, turned_copied, q + 1)
                wait(pe, message_ready, q)
                for t in range(SUB):
                    bank, o = (0, t) if t < A else (1, t - A)
                    last = nc.tensor.matmul(p_pair[R, bank, o * NZ:(o + 1) * NZ],
                                            hot_dT[:, t * rows:(t + 1) * rows], c["pairs"][:, :],
                                            start=True, stop=True)
                last.then_inc(pair_ready, 1)
                wait(pe, hidden_ready, q + 1)
                for t in range(SUB):
                    last = nc.tensor.matmul(p_gate[R, t * D:(t + 1) * D], hidden[:, t * rows:(t + 1) * rows],
                                            c["f2"][:, :], start=True, stop=True)
                last.then_inc(gate_ready, 1)

            def body(u, b, rows):
                for k in range(UNITS):
                    turn(u, b, rows, k)
                    before = unit_before(u, b, rows, k)
                    if before:
                        pu, pb, prows, pk = before
                        wait(pe, message_ready, UNITS * (2 * pu + pb) + pk + 1)
                        e.sum_unit(pe, *before, message[(pb + pk) % 2])
                    products(u, b, rows, k)
            over_groups(pe, body)
            wait(pe, message_ready, UNITS * NG)
            e.sum_unit(pe, PAIRS, 1, TAIL, UNITS - 1, message[UNITS % 2])

        @block.scalar
        def _(act):
            n = e.clear_next(act)

            def begin(u, b, rows):
                wait(act, near_ready, 2 * u + b + 1)
                nc.scalar.activation(sine[0:rows, :], near[0:rows, :], ACT.Sin).then_inc(sine_ready, 1)

            def copies(u, b, rows, k):
                q = UNITS * (2 * u + b) + k
                wait(act, turned, q + 1)
                wait(act, pair_ready, q)
                nc.scalar.activation(hot_dT[:, 0:A * rows], p_hot[0:NZ, 0, 0:A * rows], ACT.Copy)
                nc.scalar.activation(hot_dT[:, A * rows:SUB * rows], p_hot[0:NZ, 1, 0:B * rows],
                                     ACT.Copy).then_inc(turned_copied, 1)
                wait(act, hidden_mult, q + 1)
                wait(act, gate_ready, q)
                nc.scalar.activation(hidden[0:D, 0:A * rows], p_hidden[0:D, 0, 0:A * rows], ACT.Silu,
                                     bias=c["f1b"][:, 0:1])
                nc.scalar.activation(hidden[0:D, A * rows:SUB * rows], p_hidden[0:D, 1, 0:B * rows], ACT.Silu,
                                     bias=c["f1b"][:, 0:1]).then_inc(hidden_ready, 1)

            over_units(act, copies, lambda u, b, rows, k: e.copy_unit(act, u, b, rows, k), begin)
            wait(act, e.cleared, n)


def relation_edges(nc, c, d):
    A, B = 3, SUB - 3
    with ExitStack() as ctx:
        e = EdgeStage(nc, ctx, c, d, "rel", table="table2", width=D, source="src", target="dst",
                      sums=("sum2a", "sum2b"), out_width=D, clear=(("sum3a", "sum3b"), D))
        s = e.s
        rows_of = [s.sb(f"rows{k}", [P, SUB, D]) for k in range(SLOTS)]
        parts = [[s.sb(f"parts{i}{k}", [P, SUB, KS + 1], BF16) for k in range(2)] for i in range(2)]
        rest = s.sb("rest", [P, SUB, D])
        norm = [s.sb(f"norm{b}", [P, G]) for b in range(2)]
        rel = [s.sb(f"rel{b}", [P, G], I32) for b in range(2)]
        relf = s.sb("relf", [P, G])
        xT = [s.sb(f"xT{i}", [KS, SUB * P], BF16) for i in range(2)]
        h1 = [s.sb(f"h1_{ch}", [P, SUB * P]) for ch in range(CHUNKS)]
        message = [s.sb(f"message{k}", [P, SUB, D]) for k in range(2)]
        p_x = [s.ps([P, 512]).bitcast(BF16) for i in range(2)]
        p_h1 = [s.ps([P, 2, 512]) for q in range(2)]
        p_h2 = s.ps([P, 512])
        linear_loaded = s.sems("linear_loaded", 2)
        pe_passed = s.sem("pe_passed")
        ones_ready, parted, turned, turned_copied, h2_ready, message_ready = (
            s.sem(x) for x in ("ones_ready", "parted", "turned", "turned_copied", "h2_ready", "message_ready"))
        rows_read = s.sem("rows_read")
        h1_mult = s.sem("h1_mult")
        h1_ready_a, h1_ready_b = s.sem("h1_ready_a"), s.sem("h1_ready_b")
        block = ctx.enter_context(nc.Block())

        @block.sync
        def _(sp):
            def body(u, b, rows):
                g = 2 * u + b
                e.load_indices(sp, u, b, rows)
                wait(sp, message_ready, UNITS * (g - 1))
                sp.dma_start(norm[b][0:rows, :], group_rows(d["norm"], g, rows)).then_inc(linear_loaded[b], 16)
                sp.dma_start(rel[b][0:rows, :], group_rows(d["rel"], g, rows)).then_inc(linear_loaded[b], 16)
            over_groups(sp, body)

        @block.gpsimd
        def _(pool):
            e.pool_program(pool, rows_of, rows_read, lag=LAG + 1)

        @block.vector
        def _(dve):
            v = nc.vector
            for i in range(2):
                for k in range(2):
                    v.tensor_copy(parts[i][k][:, :, KX - 1], c["ones"][:, 0:SUB]).then_inc(ones_ready, 1)
            dve.wait_ge(ones_ready, 4)

            def relus(u, b, rows, k):
                q = UNITS * (2 * u + b) + k
                wait(dve, h2_ready, q)
                for ch in range(CHUNKS):
                    wait(dve, h1_mult, CHUNKS * q + ch + 1)
                    v.tensor_scalar_max(h1[ch][:, A * rows:SUB * rows], p_h1[(b + k + ch) % 2][:, 1, 0:B * rows],
                                        0.0).then_inc(h1_ready_b, 1)

            def split_rows(u, b, rows, k):
                g = 2 * u + b
                q = UNITS * g + k
                R = slice(0, rows)
                first, second = parts[0][(b + k) % 2], parts[1][(b + k) % 2]
                wait(dve, turned, q - 1)
                for part in (first, second):
                    v.tensor_tensor(part[R, :, D:D + NR], spread(relf[R, SUB * k:SUB * (k + 1)], NR),
                                    along(c["rline"][R, :], SUB), ALU.not_equal).then_inc(parted, 1)
                wait(dve, e.gathered[k], 16 * SUB * (g + 1))
                x = rows_of[k][R, :, :]
                v.tensor_copy(first[R, :, 0:D], x).then_inc(parted, 1)
                wait(dve, parted, 6 * q + 3)
                v.tensor_tensor(rest[R, :, :], x, first[R, :, 0:D], ALU.subtract).then_inc(rows_read, 1)
                wait(dve, rows_read, q + 1)
                v.tensor_copy(second[R, :, 0:D], first[R, :, 0:D]).then_inc(parted, 1)
                v.tensor_copy(first[R, :, KX:KS], rest[R, :, :]).then_inc(parted, 1)
                wait(dve, parted, 6 * q + 5)
                v.tensor_tensor(second[R, :, KX:KS], rest[R, :, :], first[R, :, KX:KS],
                                ALU.subtract).then_inc(parted, 1)

            def message_of(u, b, rows, k):
                q = UNITS * (2 * u + b) + k
                R = slice(0, rows)
                wait(dve, h2_ready, q + 1)
                wait(dve, e.summed, q - 1)
                v.tensor_tensor(message[(b + k) % 2][R, :, :],
                                p_h2[R, 0:SUB * D].rearrange("p (t c) -> p t c", t=SUB),
                                spread(norm[b][R, SUB * k:SUB * (k + 1)], D), ALU.mult).then_inc(message_ready, 1)

            def body(u, b, rows):
                g = 2 * u + b
                R = slice(0, rows)
                st = Steps(dve, e.keyed, e.KEY_STEPS + 1, g)
                e.key_group(dve, st, u, b, rows)
                wait(dve, linear_loaded[b], 32 * (u + 1))
                st.did(v.tensor_copy(relf[R, :], rel[b][R, :]))
                st.wait()
                for k in range(UNITS):
                    split_rows(u, b, rows, k)
                    before = unit_before(u, b, rows, k)
                    if before:
                        before2 = unit_before(*before)
                        if before2:
                            message_of(*before2)
                        relus(*before)
                    e.same_unit(dve, st, u, b, rows, k)
                st.end()
            over_groups(dve, body)
            message_of(PAIRS, 1, TAIL, UNITS - 2)
            relus(PAIRS, 1, TAIL, UNITS - 1)
            message_of(PAIRS, 1, TAIL, UNITS - 1)

        @block.tensor
        def _(pe):
            pe.wait_ge(ones_ready, 4)

            def turn(u, b, rows, k):
                g = 2 * u + b
                q = UNITS * g + k
                R = slice(0, rows)
                hold(pe, parted, 6 * (q + 1), pe_passed)
                hold(pe, turned_copied, 2 * q, pe_passed)
                for i in range(2):
                    for t in range(SUB):
                        last = nc.tensor.transpose(p_x[i][0:KS, t * rows:(t + 1) * rows],
                                                   parts[i][(b + k) % 2][R, t, 0:KS], c["identb"][R, R])
                last.then_inc(turned, 1)

            def first_products(u, b, rows, k):
                q = UNITS * (2 * u + b) + k
                wait(pe, turned_copied, 2 * (q + 1))
                for ch in range(CHUNKS):
                    wait(pe, h1_ready_a, CHUNKS * q + ch - 1)
                    wait(pe, h1_ready_b, CHUNKS * q + ch - 1)
                    for i, (weight, x) in enumerate((("r1a", xT[0]), ("r1b", xT[0]), ("r1c", xT[1]))):
                        for bank, t0, n in ((0, 0, A), (1, A, B)):
                            last = nc.tensor.matmul(p_h1[(b + k + ch) % 2][:, bank, 0:n * rows],
                                                    c[weight][:, ch * P:(ch + 1) * P],
                                                    x[:, t0 * rows:(t0 + n) * rows], start=(i == 0), stop=(i == 2))
                    last.then_inc(h1_mult, 1)

            def second_products(u, b, rows, k):
                q = UNITS * (2 * u + b) + k
                R = slice(0, rows)
                wait(pe, message_ready, q)
                wait(pe, h1_ready_a, CHUNKS * (q + 1))
                wait(pe, h1_ready_b, CHUNKS * (q + 1))
                for t in range(SUB):
                    for ch in range(CHUNKS):
                        last = nc.tensor.matmul(p_h2[R, t * D:(t + 1) * D], h1[ch][:, t * rows:(t + 1) * rows],
                                                c["r2"][:, ch, :], start=(ch == 0), stop=(ch == CHUNKS - 1))
                last.then_inc(h2_ready, 1)

            def sums(u, b, rows, k):
                wait(pe, message_ready, UNITS * (2 * u + b) + k + 1)
                e.sum_unit(pe, u, b, rows, k, message[(b + k) % 2])

            def body(u, b, rows):
                for k in range(UNITS):
                    turn(u, b, rows, k)
                    before = unit_before(u, b, rows, k)
                    if before:
                        second_products(*before)
                    first_products(u, b, rows, k)
                    if before:
                        sums(*before)
            over_groups(pe, body)
            second_products(PAIRS, 1, TAIL, UNITS - 1)
            sums(PAIRS, 1, TAIL, UNITS - 1)

        @block.scalar
        def _(act):
            n = e.clear_next(act)

            def copies(u, b, rows, k):
                q = UNITS * (2 * u + b) + k
                wait(act, turned, q + 1)
                wait(act, h1_mult, CHUNKS * q)
                for i in range(2):
                    nc.scalar.activation(xT[i][:, 0:SUB * rows], p_x[i][0:KS, 0:SUB * rows],
                                         ACT.Copy).then_inc(turned_copied, 1)
                wait(act, h2_ready, q)
                for ch in range(CHUNKS):
                    wait(act, h1_mult, CHUNKS * q + ch + 1)
                    nc.scalar.activation(h1[ch][:, 0:A * rows], p_h1[(b + k + ch) % 2][:, 0, 0:A * rows],
                                         ACT.Relu).then_inc(h1_ready_a, 1)

            over_units(act, copies, lambda u, b, rows, k: e.copy_unit(act, u, b, rows, k))
            wait(act, e.cleared, n)


class Norm:

    def __init__(self, s, nc, tag):
        self.nc = nc
        self.total, self.mean, self.spread, self.var, self.root, self.inv = (
            s.sb(f"{tag}_{n}", [P, G]) for n in ("total", "mean", "spread", "var", "root", "inv"))
        self.centred = [s.sb(f"{tag}_centred{b}", [P, G, D]) for b in range(2)]
        self.square = [s.sb(f"{tag}_square{b}", [P, G, D]) for b in range(2)]
        self.averaged, self.centred_ready, self.squared, self.spreaded, self.var_ready, self.rooted, self.inverted = (
            s.sem(f"{tag}_{n}") for n in ("averaged", "centred_ready", "squared", "spreaded", "var_ready", "rooted",
                                          "inverted"))

    def centre(self, dve, u, b, rows, x):
        v, R = self.nc.vector, slice(0, rows)
        st = Steps(dve, self.averaged, 2, 2 * u + b)
        st.did(v.tensor_reduce(self.total[R, :], x, AX, ALU.add))
        st.wait()
        st.did(v.tensor_scalar(self.mean[R, :], self.total[R, :], 1.0 / D, None, ALU.mult))
        st.wait()
        v.tensor_tensor(self.centred[b][R, :, :], x, spread(self.mean[R, :], D), ALU.subtract).then_inc(
            self.centred_ready, 1)

    def variance(self, dve, u, b, rows):
        v, R, g = self.nc.vector, slice(0, rows), 2 * u + b
        wait(dve, self.squared, g + 1)
        v.tensor_reduce(self.spread[R, :], self.square[b][R, :, :], AX, ALU.add).then_inc(self.spreaded, 1)
        wait(dve, self.spreaded, g + 1)
        v.tensor_scalar(self.var[R, :], self.spread[R, :], 1.0 / D, EPS, ALU.mult, ALU.add).then_inc(
            self.var_ready, 1)

    def scale(self, dve, u, b, rows, out):
        v, R, g = self.nc.vector, slice(0, rows), 2 * u + b
        wait(dve, self.rooted, g + 1)
        v.reciprocal(self.inv[R, :], self.root[R, :]).then_inc(self.inverted, 1)
        wait(dve, self.inverted, g + 1)
        return v.tensor_tensor(out, self.centred[b][R, :, :], spread(self.inv[R, :], D), ALU.mult)

    def squares(self, act, u, b, rows):
        R = slice(0, rows)
        wait(act, self.centred_ready, 2 * u + b + 1)
        self.nc.scalar.activation(self.square[b][R, :, :], self.centred[b][R, :, :], ACT.Square).then_inc(
            self.squared, 1)

    def deviation(self, act, u, b, rows):
        R = slice(0, rows)
        wait(act, self.var_ready, 2 * u + b + 1)
        self.nc.scalar.activation(self.root[R, :], self.var[R, :], ACT.Sqrt).then_inc(self.rooted, 1)


class Product:

    W = D + 1
    PER = 8
    CHUNKS = -(-G // PER)
    BANK = 10

    def __init__(self, s, nc, c, weight):
        self.nc, self.c, self.weight = nc, c, weight
        self.x = [s.sb(f"h{b}", [P, G, self.W]) for b in range(2)]
        self.xT = [s.sb(f"xT{i}", [2 * self.W, self.PER // 2 * P]) for i in range(2)]
        self.p_x = s.ps([P, 2, 512])
        self.p_y = [s.ps([P, 3, 512]) for b in range(2)]
        self.ones_ready, self.x_ready, self.turned, self.turned_copied, self.multiplied, self.taken, self.pe_passed = (
            s.sem(n) for n in ("ones_ready", "x_ready", "turned", "turned_copied", "multiplied", "taken",
                               "pe_passed"))

    def pairs(self, j):
        return [(t, min(2, G - t)) for t in range(self.PER * j, min(self.PER * (j + 1), G), 2)]

    def place_ones(self):
        for b in range(2):
            self.nc.vector.tensor_copy(self.x[b][:, :, D], self.c["ones"][:, 0:G]).then_inc(self.ones_ready, 1)

    def results(self, dve, u, b, rows):
        R = slice(0, rows)
        wait(dve, self.multiplied, self.CHUNKS * (2 * u + b + 1))
        two = 2 * self.BANK
        return ((slice(0, two), self.p_y[b][R, 0:2, 0:self.BANK * D]),
                (slice(two, G), self.p_y[b][R, 2:3, 0:(G - two) * D]))

    @staticmethod
    def by_bank(x):
        return x.rearrange("p (k t) c -> p k (t c)", k=2 if x.shape[1] > Product.BANK else 1)

    def tensor_program(self, pe):
        def turn(u, b, rows, j):
            g, R = 2 * u + b, slice(0, rows)
            if j == 0:
                hold(pe, self.x_ready, g + 1, self.pe_passed)
            hold(pe, self.turned_copied, self.CHUNKS * g + j - 1, self.pe_passed)
            for i, (t, n) in enumerate(self.pairs(j)):
                last = self.nc.tensor.transpose(self.p_x[0:n * self.W, j % 2, i * rows:(i + 1) * rows],
                                                self.x[b][R, t:t + n, :].rearrange("p t c -> p (t c)"),
                                                self.c["ident"][R, R])
            last.then_inc(self.turned, 1)

        def multiply(u, b, rows, j):
            g, R = 2 * u + b, slice(0, rows)
            hold(pe, self.turned_copied, self.CHUNKS * g + j + 1, self.pe_passed)
            if j == 0:
                hold(pe, self.taken, 2 * (g - 1), self.pe_passed)
            for i, (t, n) in enumerate(self.pairs(j)):
                at = t % self.BANK * D
                last = self.nc.tensor.matmul(self.p_y[b][R, t // self.BANK, at:at + n * D],
                                             self.xT[j % 2][0:n * self.W, i * rows:(i + 1) * rows],
                                             self.c[self.weight][0:n * self.W, 0:n * D], start=True, stop=True)
            last.then_inc(self.multiplied, 1)

        def body(u, b, rows):
            for j in range(self.CHUNKS):
                turn(u, b, rows, j)
                if j:
                    multiply(u, b, rows, j - 1)
                elif group_before(u, b, rows, 1):
                    multiply(*group_before(u, b, rows, 1), self.CHUNKS - 1)

        pe.wait_ge(self.ones_ready, 2)
        over_groups(pe, body)
        multiply(PAIRS, 1, TAIL, self.CHUNKS - 1)

    def copies(self, act, u, b, rows):
        for j in range(self.CHUNKS):
            q = self.CHUNKS * (2 * u + b) + j
            pairs = self.pairs(j)
            height, columns = pairs[0][1] * self.W, len(pairs) * rows
            wait(act, self.turned, q + 1)
            wait(act, self.multiplied, q - 1)
            self.nc.scalar.activation(self.xT[j % 2][0:height, 0:columns], self.p_x[0:height, j % 2, 0:columns],
                                      ACT.Copy).then_inc(self.turned_copied, 1)


def nodes0(nc, c, d):
    W = D + 1
    with ExitStack() as ctx:
        s = Scope(nc, ctx, "n0")
        sa = [s.sb(f"sa{b}", [P, G * W]) for b in range(2)]
        sb_ = [s.sb(f"sb{b}", [P, G * W]) for b in range(2)]
        x = [s.sb(f"x{b}", [P, G, D]) for b in range(2)]
        kept = [s.sb(f"kept{b}", [P, G, D]) for b in range(2)]
        z = [s.sb(f"z{b}", [P, G], I32) for b in range(2)]
        mult = [s.sb(f"mult{b}", [P, G]) for b in range(2)]
        total = [s.sb(f"total{b}", [P, G, W]) for b in range(2)]
        deg = [s.sb(f"deg{b}", [P, G]) for b in range(2)]
        dm, root, cj, alone = (s.sb(n, [P, G]) for n in ("dm", "root", "cj", "alone"))
        own = s.sb("own", [P, G, D])
        y = s.sb("y", [P, G, D])
        row = [s.sb(f"row{b}", [P, G, D + 2]) for b in range(2)]
        norm, prod = Norm(s, nc, "norm"), Product(s, nc, c, "w0")
        h = prod.x
        loaded, tail_loaded, stored, deg_stored = (s.sems(n, 2) for n in ("loaded", "tail_loaded", "stored",
                                                                          "deg_stored"))
        summed, kept_ready, owned, alone_ready, dm_ready, rooted, stepped, tailed, built, pool_passed, sp_passed = (
            s.sem(n) for n in ("summed", "kept_ready", "owned", "alone_ready", "dm_ready", "rooted", "stepped",
                               "tailed", "built", "pool_passed", "sp_passed"))
        block = ctx.enter_context(nc.Block())

        @block.sync
        def _(sp):
            def tail(u, b, rows):
                hold(sp, built, 2 * u + b - 1, sp_passed)
                sp.dma_start(z[b][0:rows, :], group_rows(d["z"], 2 * u + b, rows)).then_inc(tail_loaded[b], 16)
                sp.dma_start(mult[b][0:rows, :], group_rows(d["mult"], 2 * u + b, rows)).then_inc(
                    tail_loaded[b], 16)

            def body(u, b, rows):
                g = 2 * u + b
                R = slice(0, rows)
                hold(sp, owned, g - 1, sp_passed)
                for dst, src, w in ((sa[b][R, :], d["sum0a"], W), (sb_[b][R, :], d["sum0b"], W),
                                    (x[b][R, :, :].rearrange("p t c -> p (t c)"), d["x"], D)):
                    sp.dma_start(dst, group_rows(src, g, rows, w)).then_inc(loaded[b], 16)
                if group_before(u, b, rows, 1):
                    tail(*group_before(u, b, rows, 1))
            over_groups(sp, body)
            tail(PAIRS, 1, TAIL)

        @block.gpsimd
        def _(pool):
            def body(u, b, rows):
                g = 2 * u + b
                R = slice(0, rows)
                hold(pool, loaded[b], 48 * (u + 1), pool_passed)
                hold(pool, prod.x_ready, g - 1, pool_passed)
                nc.gpsimd.tensor_tensor(total[b][R, :, :].rearrange("p t c -> p (t c)"), sa[b][R, :], sb_[b][R, :],
                                        ALU.add).then_inc(summed, 1)
                hold(pool, prod.taken, 2 * (g - 1), pool_passed)
                nc.gpsimd.tensor_copy(kept[b][R, :, :], x[b][R, :, :]).then_inc(kept_ready, 1)
                hold(pool, alone_ready, g + 1, pool_passed)
                hold(pool, prod.x_ready, g, pool_passed)
                nc.gpsimd.tensor_tensor(own[R, :, :], x[b][R, :, :], spread(alone[R, :], D),
                                        ALU.mult).then_inc(owned, 1)
            over_groups(pool, body)

        @block.vector
        def _(dve):
            v = nc.vector
            prod.place_ones()

            def degrees(u, b, rows):
                R = slice(0, rows)
                wait(dve, summed, 2 * u + b + 1)
                v.tensor_scalar(alone[R, :], total[b][R, :, D], 0.0, None, ALU.is_equal).then_inc(alone_ready, 1)
                wait(dve, deg_stored[b], 16 * u)
                v.tensor_copy(deg[b][R, :], total[b][R, :, D]).then_inc(dm_ready, 1)
                v.tensor_scalar_max(dm[R, :], total[b][R, :, D], 1.0).then_inc(dm_ready, 1)

            def operands(u, b, rows):
                g = 2 * u + b
                R = slice(0, rows)
                st = Steps(dve, stepped, 2, g)
                wait(dve, rooted, g + 1)
                st.did(v.reciprocal(cj[R, :], root[R, :]))
                st.wait()
                wait(dve, prod.turned, prod.CHUNKS * (g - 1))
                st.did(v.tensor_tensor(h[b][R, :, 0:D], total[b][R, :, 0:D], spread(cj[R, :], D), ALU.mult))
                st.wait()
                wait(dve, owned, g + 1)
                v.tensor_tensor(h[b][R, :, 0:D], h[b][R, :, 0:D], own[R, :, :], ALU.add).then_inc(prod.x_ready, 1)

            def residual(u, b, rows):
                g = 2 * u + b
                R = slice(0, rows)
                wait(dve, kept_ready, g + 1)
                for tiles, product in prod.results(dve, u, b, rows):
                    v.scalar_tensor_tensor(prod.by_bank(y[R, tiles, :]), product, 0.0,
                                           prod.by_bank(kept[b][R, tiles, :]), ALU.max,
                                           ALU.add).then_inc(prod.taken, 1)
                wait(dve, prod.taken, 2 * (g + 1))
                norm.centre(dve, u, b, rows, y[R, :, :])

            def table_rows(u, b, rows):
                g = 2 * u + b
                R = slice(0, rows)
                wait(dve, tail_loaded[b], 32 * (u + 1))
                wait(dve, stored[b], 16 * u)
                v.tensor_copy(row[b][R, :, D + 1], z[b][R, :]).then_inc(tailed, 1)
                v.tensor_copy(row[b][R, :, D], mult[b][R, :]).then_inc(tailed, 1)
                norm.scale(dve, u, b, rows, row[b][R, :, 0:D]).then_inc(built, 1)

            over_lagged(dve, [(0, degrees), (2, lambda *at: norm.variance(dve, *at)), (0, operands), (1, residual),
                              (2, table_rows)])

        @block.tensor
        def _(pe):
            prod.tensor_program(pe)

        @block.scalar
        def _(act):
            def first(u, b, rows):
                g = 2 * u + b
                R = slice(0, rows)
                wait(act, dm_ready, 2 * (g + 1))
                nc.scalar.activation(root[R, :], dm[R, :], ACT.Sqrt).then_inc(rooted, 1)
                act.dma_start(group_rows(d["indeg"], g, rows), deg[b][R, :]).then_inc(deg_stored[b], 16)

            def store(u, b, rows):
                wait(act, built, 2 * u + b + 1)
                act.dma_start(group_rows(d["table1"], 2 * u + b, rows, D + 2),
                              row[b][0:rows, :, :].rearrange("p t c -> p (t c)")).then_inc(stored[b], 16)

            over_lagged(act, [(0, first), (2, lambda *at: norm.deviation(act, *at)),
                              (0, lambda *at: prod.copies(act, *at)), (1, lambda *at: norm.squares(act, *at)),
                              (2, store)])
            for b in range(2):
                act.wait_ge(stored[b], 16 * (PAIRS + 1))
                act.wait_ge(deg_stored[b], 16 * (PAIRS + 1))


def nodes1(nc, c, d):
    W = D + 1
    with ExitStack() as ctx:
        s = Scope(nc, ctx, "n1")
        sa = [s.sb(f"sa{b}", [P, G * W]) for b in range(2)]
        sb_ = [s.sb(f"sb{b}", [P, G * W]) for b in range(2)]
        x = [s.sb(f"x{b}", [P, G, D + 2]) for b in range(2)]
        total = [s.sb(f"total{b}", [P, G, W]) for b in range(2)]
        shifted = [s.sb(f"shifted{b}", [P, G, D]) for b in range(2)]
        share = s.sb("share", [P, G])
        y = s.sb("y", [P, G, D])
        y1 = s.sb("y1", [P, G, D])
        y2 = s.sb("y2", [P, G, D])
        out = [s.sb(f"out{b}", [P, G, D]) for b in range(2)]
        norm, norm2 = Norm(s, nc, "norm"), Norm(s, nc, "norm2")
        loaded, stored = s.sems("loaded", 2), s.sems("stored", 2)
        summed, shifted_ready, joined, stepped, scaled, built, pool_passed = (
            s.sem(n) for n in ("summed", "shifted_ready", "joined", "stepped", "scaled", "built", "pool_passed"))
        block = ctx.enter_context(nc.Block())

        @block.sync
        def _(sp):
            def body(u, b, rows):
                g = 2 * u + b
                R = slice(0, rows)
                wait(sp, shifted_ready, g - 1)
                wait(sp, joined, g - 1)
                for dst, src, w in ((sa[b][R, :], d["sum1a"], W), (sb_[b][R, :], d["sum1b"], W),
                                    (x[b][R, :, :].rearrange("p t c -> p (t c)"), d["table1"], D + 2)):
                    sp.dma_start(dst, group_rows(src, g, rows, w)).then_inc(loaded[b], 16)
            over_groups(sp, body)

        @block.gpsimd
        def _(pool):
            def body(u, b, rows):
                g = 2 * u + b
                R = slice(0, rows)
                hold(pool, loaded[b], 48 * (u + 1), pool_passed)
                hold(pool, joined, g - 1, pool_passed)
                nc.gpsimd.tensor_tensor(total[b][R, :, :].rearrange("p t c -> p (t c)"), sa[b][R, :], sb_[b][R, :],
                                        ALU.add).then_inc(summed, 1)
                hold(pool, scaled, 3 * (g - 1), pool_passed)
                nc.gpsimd.tensor_tensor(shifted[b][R, :, :], x[b][R, :, 0:D], along(c["beta1"][R, :], G),
                                        ALU.add).then_inc(shifted_ready, 1)
            over_groups(pool, body)

        @block.vector
        def _(dve):
            v = nc.vector

            def join(u, b, rows):
                g = 2 * u + b
                R = slice(0, rows)
                st = Steps(dve, stepped, 3, g)
                wait(dve, summed, g + 1)
                st.did(v.tensor_scalar_max(share[R, :], total[b][R, :, D], 1e-8))
                st.wait()
                st.did(v.reciprocal(share[R, :], share[R, :]))
                st.wait()
                st.did(v.tensor_tensor(y[R, :, :], total[b][R, :, 0:D], spread(share[R, :], D), ALU.mult))
                st.wait()
                wait(dve, loaded[b], 48 * (u + 1))
                v.tensor_tensor(y[R, :, :], y[R, :, :], x[b][R, :, 0:D], ALU.add).then_inc(joined, 1)
                wait(dve, joined, g + 1)
                norm.centre(dve, u, b, rows, y[R, :, :])

            def residual(u, b, rows):
                g = 2 * u + b
                R = slice(0, rows)
                st = Steps(dve, scaled, 3, g)
                st.did(norm.scale(dve, u, b, rows, y1[R, :, :]))
                st.wait()
                st.did(v.tensor_tensor(y2[R, :, :], y1[R, :, :], along(c["gamma1"][R, :], G), ALU.mult))
                st.wait()
                wait(dve, shifted_ready, g + 1)
                st.did(v.tensor_tensor(y2[R, :, :], y2[R, :, :], shifted[b][R, :, :], ALU.add))
                st.wait()
                norm2.centre(dve, u, b, rows, y2[R, :, :])

            def result(u, b, rows):
                wait(dve, stored[b], 16 * u)
                norm2.scale(dve, u, b, rows, out[b][0:rows, :, :]).then_inc(built, 1)

            over_lagged(dve, [(1, lambda *at: norm.variance(dve, *at)), (2, lambda *at: norm2.variance(dve, *at)),
                              (0, join), (1, residual), (2, result)])

        @block.scalar
        def _(act):
            def store(u, b, rows):
                wait(act, built, 2 * u + b + 1)
                act.dma_start(group_rows(d["table2"], 2 * u + b, rows, D),
                              out[b][0:rows, :, :].rearrange("p t c -> p (t c)")).then_inc(stored[b], 16)

            over_lagged(act, [(1, lambda *at: norm.deviation(act, *at)), (2, lambda *at: norm2.deviation(act, *at)),
                              (0, lambda *at: norm.squares(act, *at)), (1, lambda *at: norm2.squares(act, *at)),
                              (2, store)])
            for b in range(2):
                act.wait_ge(stored[b], 16 * (PAIRS + 1))


def nodes2(nc, c, d):
    with ExitStack() as ctx:
        s = Scope(nc, ctx, "n2")
        sa = [s.sb(f"sa{b}", [P, G, D]) for b in range(2)]
        sb_ = [s.sb(f"sb{b}", [P, G, D]) for b in range(2)]
        x = [s.sb(f"x{b}", [P, G, D]) for b in range(2)]
        deg = [s.sb(f"deg{b}", [P, G]) for b in range(2)]
        total = [s.sb(f"total{b}", [P, G, D]) for b in range(2)]
        y = s.sb("y", [P, G, D])
        dm, root = (s.sb(n, [P, G]) for n in ("dm", "root"))
        dinv = [s.sb(f"dinv{b}", [P, G]) for b in range(2)]
        out = [s.sb(f"out{b}", [P, G, D]) for b in range(2)]
        row = [s.sb(f"row{b}", [P, G, D]) for b in range(2)]
        norm = Norm(s, nc, "norm")
        loaded, stored = s.sems("loaded", 2), s.sems("stored", 2)
        summed, dm_ready, rooted, joined, inverted, normed, built, pool_passed = (
            s.sem(n) for n in ("summed", "dm_ready", "rooted", "joined", "inverted", "normed", "built",
                               "pool_passed"))
        block = ctx.enter_context(nc.Block())

        @block.sync
        def _(sp):
            def body(u, b, rows):
                g = 2 * u + b
                R = slice(0, rows)
                wait(sp, joined, g - 1)
                for dst, src in ((sa[b], d["sum2a"]), (sb_[b], d["sum2b"]), (x[b], d["table2"])):
                    sp.dma_start(dst[R, :, :].rearrange("p t c -> p (t c)"), group_rows(src, g, rows, D)).then_inc(
                        loaded[b], 16)
                sp.dma_start(deg[b][R, :], group_rows(d["indeg"], g, rows)).then_inc(loaded[b], 16)
            over_groups(sp, body)

        @block.gpsimd
        def _(pool):
            def body(u, b, rows):
                g = 2 * u + b
                R = slice(0, rows)
                hold(pool, loaded[b], 64 * (u + 1), pool_passed)
                hold(pool, joined, g - 1, pool_passed)
                nc.gpsimd.tensor_tensor(total[b][R, :, :], sa[b][R, :, :], sb_[b][R, :, :],
                                        ALU.add).then_inc(summed, 1)
                hold(pool, summed, 2 * g + 1, pool_passed)
                nc.gpsimd.tensor_tensor(total[b][R, :, :], total[b][R, :, :], along(c["rb2"][R, :], G),
                                        ALU.add).then_inc(summed, 1)
            over_groups(pool, body)

        @block.vector
        def _(dve):
            v = nc.vector

            def join(u, b, rows):
                g = 2 * u + b
                R = slice(0, rows)
                wait(dve, loaded[b], 64 * (u + 1))
                v.tensor_scalar_add(dm[R, :], deg[b][R, :], 1.0).then_inc(dm_ready, 1)
                wait(dve, summed, 2 * (g + 1))
                v.scalar_tensor_tensor(y[R, :, :], total[b][R, :, :], 0.0, x[b][R, :, :], ALU.max,
                                       ALU.add).then_inc(joined, 1)
                wait(dve, joined, g + 1)
                norm.centre(dve, u, b, rows, y[R, :, :])
                wait(dve, rooted, g + 1)
                v.reciprocal(dinv[b][R, :], root[R, :]).then_inc(inverted, 1)

            def result(u, b, rows):
                g = 2 * u + b
                R = slice(0, rows)
                wait(dve, stored[b], 32 * u)
                norm.scale(dve, u, b, rows, out[b][R, :, :]).then_inc(normed, 1)
                wait(dve, normed, g + 1)
                wait(dve, inverted, g + 1)
                v.tensor_tensor(row[b][R, :, :], out[b][R, :, :], spread(dinv[b][R, :], D), ALU.mult).then_inc(built, 1)

            over_lagged(dve, [(1, lambda *at: norm.variance(dve, *at)), (0, join), (1, result)])

        @block.scalar
        def _(act):
            def first(u, b, rows):
                R = slice(0, rows)
                wait(act, dm_ready, 2 * u + b + 1)
                nc.scalar.activation(root[R, :], dm[R, :], ACT.Sqrt).then_inc(rooted, 1)
                norm.squares(act, u, b, rows)

            def store(u, b, rows):
                g = 2 * u + b
                wait(act, built, g + 1)
                for dst, src in ((d["x3"], out[b]), (d["table3"], row[b])):
                    act.dma_start(group_rows(dst, g, rows, D),
                                  src[0:rows, :, :].rearrange("p t c -> p (t c)")).then_inc(stored[b], 16)

            over_lagged(act, [(1, lambda *at: norm.deviation(act, *at)), (0, first), (1, store)])
            for b in range(2):
                act.wait_ge(stored[b], 32 * (PAIRS + 1))


def nodes3(nc, c, d, ally):
    with ExitStack() as ctx:
        s = Scope(nc, ctx, "n3")
        sa = [s.sb(f"sa{b}", [P, G, D]) for b in range(2)]
        sb_ = [s.sb(f"sb{b}", [P, G, D]) for b in range(2)]
        x = [s.sb(f"x{b}", [P, G, D]) for b in range(2)]
        total = [s.sb(f"total{b}", [P, G, D]) for b in range(2)]
        deg = [s.sb(f"deg{b}", [P, G]) for b in range(2)]
        dm, root, dinv = (s.sb(n, [P, G]) for n in ("dm", "root", "dinv"))
        prod = Product(s, nc, c, "w3")
        h = prod.x
        loaded = s.sems("loaded", 2)
        summed, dm_ready, rooted, inverted, pool_passed, sp_passed = (
            s.sem(n) for n in ("summed", "dm_ready", "rooted", "inverted", "pool_passed", "sp_passed"))
        block = ctx.enter_context(nc.Block())

        @block.sync
        def _(sp):
            def body(u, b, rows):
                g = 2 * u + b
                R = slice(0, rows)
                hold(sp, dm_ready, g - 1, sp_passed)
                hold(sp, summed, 2 * (g - 1), sp_passed)
                for dst, src in ((sa[b], d["sum3a"]), (sb_[b], d["sum3b"]), (x[b], d["table3"])):
                    sp.dma_start(dst[R, :, :].rearrange("p t c -> p (t c)"), group_rows(src, g, rows, D)).then_inc(
                        loaded[b], 16)
                sp.dma_start(deg[b][R, :], group_rows(d["indeg"], g, rows)).then_inc(loaded[b], 16)
            over_groups(sp, body)

        @block.gpsimd
        def _(pool):
            def body(u, b, rows):
                g = 2 * u + b
                R = slice(0, rows)
                hold(pool, loaded[b], 64 * (u + 1), pool_passed)
                hold(pool, prod.x_ready, g - 1, pool_passed)
                nc.gpsimd.tensor_tensor(total[b][R, :, :], sa[b][R, :, :], sb_[b][R, :, :],
                                        ALU.add).then_inc(summed, 1)
                hold(pool, summed, 2 * g + 1, pool_passed)
                nc.gpsimd.tensor_tensor(total[b][R, :, :], total[b][R, :, :], x[b][R, :, :],
                                        ALU.add).then_inc(summed, 1)
            over_groups(pool, body)

        @block.vector
        def _(dve):
            v = nc.vector
            prod.place_ones()

            def operands(u, b, rows):
                g = 2 * u + b
                R = slice(0, rows)
                wait(dve, loaded[b], 64 * (u + 1))
                v.tensor_scalar_add(dm[R, :], deg[b][R, :], 1.0).then_inc(dm_ready, 1)
                wait(dve, rooted, g + 1)
                v.reciprocal(dinv[R, :], root[R, :]).then_inc(inverted, 1)
                wait(dve, inverted, g + 1)
                wait(dve, summed, 2 * (g + 1))
                wait(dve, prod.turned, prod.CHUNKS * (g - 1))
                v.tensor_tensor(h[b][R, :, 0:D], total[b][R, :, :], spread(dinv[R, :], D),
                                ALU.mult).then_inc(prod.x_ready, 1)

            def keep(u, b, rows):
                R = slice(0, rows)
                y = ally[R, bass.ds((2 * u + b) * (G * D), G * D)].rearrange("p (t c) -> p t c", c=D)
                for tiles, product in prod.results(dve, u, b, rows):
                    v.tensor_copy(prod.by_bank(y[:, tiles, :]), product).then_inc(prod.taken, 1)

            over_lagged(dve, [(0, operands), (1, keep)])

        @block.tensor
        def _(pe):
            prod.tensor_program(pe)

        @block.scalar
        def _(act):
            def body(u, b, rows):
                R = slice(0, rows)
                wait(act, dm_ready, 2 * u + b + 1)
                nc.scalar.activation(root[R, :], dm[R, :], ACT.Sqrt).then_inc(rooted, 1)
                prod.copies(act, u, b, rows)
            over_groups(act, body)


def batch_statistics(nc, c, ally):
    CH = 15
    with ExitStack() as ctx:
        s = Scope(nc, ctx, "bn")
        part = s.sb("part", [P, 2, D])
        part2 = s.sb("part2", [P, CH + 1, D])
        square = [s.sb(f"square{k}", [P, G, D]) for k in range(2)]
        var, root, inv = (s.sb(n, [P, D]) for n in ("var", "root", "inv"))
        ps = s.ps([P, 512])
        stepped, parted, meaned, squared, reduced, vared, rooted = (
            s.sem(n) for n in ("stepped", "parted", "meaned", "squared", "reduced", "vared", "rooted"))
        centred = s.sem("centred")
        block = ctx.enter_context(nc.Block())
        chunks = [(P, k * G * D) for k in range(NG - 1)] + [(TAIL, (NG - 1) * G * D)]

        def chunk(k):
            rows, at = chunks[k]
            return ally[0:rows, at:at + G * D]

        def reduce_chunk(dve, k):
            rows = chunks[k][0]
            dve.wait_ge(squared, k + 1)
            nc.vector.tensor_reduce(part2[0:rows, k, :], square[k % 2][0:rows, :, :].rearrange("p t c -> p c t"), AX,
                                    ALU.add).then_inc(reduced, 1)

        @block.vector
        def _(dve):
            v = nc.vector
            main = (NG - 1) * G * D
            v.tensor_reduce(part[:, 0, :], ally[:, 0:main].rearrange("p (t c) -> p c t", c=D), AX,
                            ALU.add).then_inc(parted, 1)
            v.tensor_reduce(part[0:TAIL, 1, :], ally[0:TAIL, main:main + G * D].rearrange("p (t c) -> p c t", c=D),
                            AX, ALU.add).then_inc(parted, 1)
            dve.wait_ge(meaned, 1)
            v.tensor_scalar(c["mean"][:, :], ps[:, 0:D], 1.0 / N, None, ALU.mult).then_inc(stepped, 1)
            dve.wait_ge(stepped, 1)
            for k in range(NG):
                rows = chunks[k][0]
                y = chunk(k).rearrange("p (t c) -> p t c", c=D)
                v.tensor_tensor(y, y, along(c["mean"][0:rows, :], G), ALU.subtract).then_inc(centred, 1)
                if k:
                    reduce_chunk(dve, k - 1)
            reduce_chunk(dve, NG - 1)
            dve.wait_ge(vared, 1)
            v.tensor_scalar(var[:, :], ps[:, 64:64 + D], 1.0 / N, EPS, ALU.mult, ALU.add).then_inc(stepped, 1)
            dve.wait_ge(rooted, 1)
            v.reciprocal(inv[:, :], root[:, :]).then_inc(stepped, 1)
            dve.wait_ge(stepped, 3)
            v.tensor_tensor(c["scale3"][:, :], inv[:, :], c["gamma3"][:, :], ALU.mult).then_inc(stepped, 1)
            dve.wait_ge(stepped, 4)

        @block.scalar
        def _(act):
            for k in range(NG):
                rows = chunks[k][0]
                act.wait_ge(centred, k + 1)
                wait(act, reduced, k - 1)
                nc.scalar.activation(square[k % 2][0:rows, :, :].rearrange("p t c -> p (t c)"), chunk(k),
                                     ACT.Square).then_inc(squared, 1)
            act.wait_ge(stepped, 2)
            nc.scalar.activation(root[:, :], var[:, :], ACT.Sqrt).then_inc(rooted, 1)

        @block.tensor
        def _(pe):
            pe.wait_ge(parted, 2)
            nc.tensor.matmul(ps[:, 0:D], c["ones"][:, :], part[:, 0, :], start=True, stop=False)
            nc.tensor.matmul(ps[:, 0:D], c["ones"][0:TAIL, :], part[0:TAIL, 1, :], start=False,
                             stop=True).then_inc(meaned, 1)
            pe.wait_ge(reduced, NG)
            for k in range(NG):
                rows = chunks[k][0]
                last = nc.tensor.matmul(ps[:, 64:64 + D], c["ones"][0:rows, :], part2[0:rows, k, :],
                                        start=(k == 0), stop=(k == NG - 1))
            last.then_inc(vared, 1)


def finish(nc, c, d, ally):
    with ExitStack() as ctx:
        s = Scope(nc, ctx, "fin")
        x = [s.sb(f"x{b}", [P, G, D]) for b in range(2)]
        scaled = [s.sb(f"scaled{b}", [P, G, D]) for b in range(2)]
        y = s.sb("y", [P, G, D])
        out = [s.sb(f"out{b}", [P, G, D]) for b in range(2)]
        norm = Norm(s, nc, "norm")
        loaded, stored = s.sems("loaded", 2), s.sems("stored", 2)
        shifted, joined, built, pool_passed = (s.sem(n) for n in ("shifted", "joined", "built", "pool_passed"))
        block = ctx.enter_context(nc.Block())

        @block.sync
        def _(sp):
            def body(u, b, rows):
                g = 2 * u + b
                wait(sp, joined, g - 1)
                sp.dma_start(x[b][0:rows, :, :].rearrange("p t c -> p (t c)"),
                             group_rows(d["x3"], g, rows, D)).then_inc(loaded[b], 16)
            over_groups(sp, body)

        @block.gpsimd
        def _(pool):
            def body(u, b, rows):
                g = 2 * u + b
                R = slice(0, rows)
                hold(pool, joined, g - 1, pool_passed)
                nc.gpsimd.tensor_tensor(scaled[b][R, :, :], ally[R, bass.ds(g * (G * D), G * D)].rearrange(
                    "p (t c) -> p t c", c=D), along(c["scale3"][R, :], G), ALU.mult).then_inc(shifted, 1)
                hold(pool, shifted, 2 * g + 1, pool_passed)
                nc.gpsimd.tensor_tensor(scaled[b][R, :, :], scaled[b][R, :, :], along(c["beta3"][R, :], G),
                                        ALU.add).then_inc(shifted, 1)
            over_groups(pool, body)

        @block.vector
        def _(dve):
            def join(u, b, rows):
                g = 2 * u + b
                R = slice(0, rows)
                wait(dve, loaded[b], 16 * (u + 1))
                wait(dve, shifted, 2 * (g + 1))
                nc.vector.scalar_tensor_tensor(y[R, :, :], scaled[b][R, :, :], 0.0, x[b][R, :, :], ALU.max,
                                               ALU.add).then_inc(joined, 1)
                wait(dve, joined, g + 1)
                norm.centre(dve, u, b, rows, y[R, :, :])

            def result(u, b, rows):
                wait(dve, stored[b], 16 * u)
                norm.scale(dve, u, b, rows, out[b][0:rows, :, :]).then_inc(built, 1)

            over_lagged(dve, [(1, lambda *at: norm.variance(dve, *at)), (0, join), (1, result)])

        @block.scalar
        def _(act):
            def store(u, b, rows):
                g = 2 * u + b
                wait(act, built, g + 1)
                act.dma_start(group_rows(d["out"], g, rows, D),
                              out[b][0:rows, :, :].rearrange("p t c -> p (t c)")).then_inc(stored[b], 16)

            over_lagged(act, [(1, lambda *at: norm.deviation(act, *at)), (0, lambda *at: norm.squares(act, *at)),
                              (1, store)])
            for b in range(2):
                act.wait_ge(stored[b], 16 * (PAIRS + 1))


def gnn_kernel(nc, d, upto=99):
    with ExitStack() as ctx:
        keep = Scope(nc, ctx, "keep")
        PSUM_OF[nc] = ctx.enter_context(nc.psum_tensor("psum", [P, 8, 512], F32))
        c = load_constants(nc, keep, d)
        ZEROS[nc] = c["zeros"]
        stages = [
            lambda: out_degree(nc, c, d, [d["sum0a"], d["sum0b"]]),
            lambda: first_table(nc, c, d),
            lambda: plain_edges(nc, c, d, "gcn", "table0", D + 2, ("sum0a", "sum0b"), D + 1,
                                (("sum1a", "sum1b"), D + 1), True),
            lambda: nodes0(nc, c, d),
            lambda: filter_edges(nc, c, d),
            lambda: nodes1(nc, c, d),
            lambda: relation_edges(nc, c, d),
            lambda: nodes2(nc, c, d),
            lambda: plain_edges(nc, c, d, "last", "table3", D, ("sum3a", "sum3b"), D, None, False),
        ]
        for f in stages[:upto]:
            f()
        if upto >= 99:
            ally = keep.sb("ally", [P, NG * G * D])
            nodes3(nc, c, d, ally)
            batch_statistics(nc, c, ally)
            finish(nc, c, d, ally)


SCRATCH_ROWS = P * 49 * 8


def declare(nc, arrays):
    dt = {"float32": F32, "int32": I32}
    d = {}
    for name, a in arrays.items():
        d[name] = nc.dram_tensor(f"in_{name}", a.shape, dt[a.dtype.name], kind="ExternalInput").ap()
    scratch = dict(outdeg=(RHIGH * RLOW,), indeg=(N,), srctype=(N,), table0=(N, D + 2), table1=(N, D + 2),
                   table2=(N, D), table3=(N, D), x3=(N, D))
    for i, w in enumerate((D + 1, D + 1, D, D)):
        scratch[f"sum{i}a"] = scratch[f"sum{i}b"] = (SCRATCH_ROWS, w)
    for name, shape in scratch.items():
        d[name] = nc.dram_tensor(f"tmp_{name}", shape, F32, kind="Internal").ap()
    d["out"] = nc.dram_tensor("out_0", (N, D), F32, kind="ExternalOutput").ap()
    return d


def lay_out(inputs):
    import numpy as np

    def tile_major(a):
        main = a[:TAIL0].reshape(NG - 1, P, G).transpose(0, 2, 1).reshape(-1)
        tail = a[TAIL0:].reshape(TAIL, G).T.reshape(-1)
        return np.concatenate([main, tail])

    i = {k: np.asarray(v) for k, v in inputs.items()}
    attr = i["edge_attr_40"]
    a = dict(
        x=i["x"], src=i["src"], dst=i["dst"], src_line=tile_major(i["src"]), dst_line=tile_major(i["dst"]),
        attr=attr[:TAIL0].reshape(NG - 1, P, G, NA).transpose(0, 3, 2, 1).reshape((NG - 1) * NA, FULL),
        attr_tail=attr[TAIL0:].reshape(TAIL, G, NA).transpose(2, 1, 0).reshape(NA, TAIL * G),
        rel=i["edge_type_8"], dist=i["edge_weight"], norm=i["edge_weight1"].reshape(-1), z=i["node_type_119"],
        mult=i["node_vec"], w0=i["L0_gnn_W"].T, w0b=i["L0_gnn_b"], f1=i["L1_gnn_W1"].T, f1b=i["L1_gnn_b1"],
        f2=i["L1_gnn_W2"].T, f2b=i["L1_gnn_b2"], embT=i["L1_gnn_emb"].T, adT=i["L1_gnn_adaptW"].T,
        gamma1=i["L1_gnn_gamma"], beta1=i["L1_gnn_beta"], r1=i["L2_gnn_weight1"], r2=i["L2_gnn_weight2"],
        rb1=i["L2_gnn_bias1"], rb2=i["L2_gnn_bias2"], w3=i["L3_gnn_W"], w3b=i["L3_gnn_b"],
        gamma3=i["L3_gnn_gamma"], beta3=i["L3_gnn_beta"])
    return {k: np.ascontiguousarray(v) for k, v in a.items()}


def kernel(**inputs):
    import concourse.bacc as bacc
    from concourse.bass_utils import run_bass_kernel_spmd

    arrays = lay_out(inputs)
    nc = bacc.Bacc("TRN2", target_bir_lowering=False, num_devices=1)
    d = declare(nc, arrays)
    gnn_kernel(nc, d)
    r = run_bass_kernel_spmd(nc, [{f"in_{k}": v for k, v in arrays.items()}], core_ids=[0])
    return r.results[0]["out_0"]
```
